# Optimizing a Trainium2 kernel written in Bass

```python
import numpy as np
import jax
import jax.numpy as jnp

def _softmax(x, axis=-1):
    return jax.nn.softmax(x, axis=axis)

def _gelu(x):
    return jax.nn.gelu(x, approximate=True)

def _silu(x):
    return jax.nn.silu(x)

def _sigmoid(x):
    return jax.nn.sigmoid(x)

def _layernorm(x, axis=-1, eps=1e-05):
    m = jnp.mean(x, axis=axis, keepdims=True)
    v = jnp.var(x, axis=axis, keepdims=True)
    return (x - m) / jnp.sqrt(v + eps)

def _scatter_add(tgt, idx, src, axis=0):
    return tgt.at[idx].add(src)

def _segment_sum(src, seg, n):
    return jax.ops.segment_sum(src, seg, n)
kernel_name = 'mk_sandwich_d4_jaxref_r8_5403c7'

def setup_inputs(seed: int=0):
    np.random.seed(seed)
    _w = jnp.asarray

    def _L0_attn_setup():
        import jax, jax.numpy as jnp
        import numpy as np
        N_HEAD = 16
        D_MODEL = 128
        HEAD_DIM = D_MODEL // N_HEAD
        LAMBDA_INIT = 0.8 - 0.6 * float(np.exp(-0.3 * 1))

        def _rms_norm(x):
            eps = jnp.finfo(x.dtype).eps
            return x * jax.lax.rsqrt(jnp.mean(jnp.square(x), axis=-1, keepdims=True) + eps)

        def _rotary_cos_sin(T, dim, base=10000.0):
            inv_freq = 1.0 / base ** (jnp.arange(0, dim, 2, dtype=jnp.float32) / dim)
            freqs = jnp.outer(jnp.arange(T, dtype=jnp.float32), inv_freq)
            return (jnp.cos(freqs), jnp.sin(freqs))

        def _apply_rotary(x, cos, sin):
            d = x.shape[-1] // 2
            c = cos[None, :, None, None, :]
            s = sin[None, :, None, None, :]
            x1, x2 = (x[..., :d], x[..., d:])
            return jnp.concatenate([x1 * c + x2 * s, -x1 * s + x2 * c], axis=-1)

        def _causal_attn(q, k, v, scale):
            T = q.shape[1]
            scores = jnp.einsum('bthd,bshd->bhts', q, k) * scale
            mask = jnp.tril(jnp.ones((T, T), dtype=bool))
            scores = jnp.where(mask, scores, -jnp.inf)
            w = jax.nn.softmax(scores, axis=-1)
            return jnp.einsum('bhts,bshd->bthd', w, v)
        key = jax.random.key(seed)
        ks = jax.random.split(key, 10)
        B, T, D = (1, 256, D_MODEL)
        std = 0.02
        return {'x': jax.random.normal(ks[0], (B, T, D), jnp.float32), 'Wq': jax.random.normal(ks[1], (D, D), jnp.float32) * std, 'Wk': jax.random.normal(ks[2], (D, D), jnp.float32) * std, 'Wv': jax.random.normal(ks[3], (D, D), jnp.float32) * std, 'Wproj': jax.random.normal(ks[4], (D, D), jnp.float32) * std, 'lambda_q1': jax.random.normal(ks[5], (HEAD_DIM // 2,), jnp.float32) * 0.1, 'lambda_k1': jax.random.normal(ks[6], (HEAD_DIM // 2,), jnp.float32) * 0.1, 'lambda_q2': jax.random.normal(ks[7], (HEAD_DIM // 2,), jnp.float32) * 0.1, 'lambda_k2': jax.random.normal(ks[8], (HEAD_DIM // 2,), jnp.float32) * 0.1}
    _L0_attn_in = _L0_attn_setup()

    def _L0_ffn_setup():
        import jax, jax.numpy as jnp
        import numpy as np
        DIM = 128
        HIDDEN = 384
        SCALE = 1.0 / 127.0

        def _dequant(w_int, dtype):
            return w_int.astype(dtype) * jnp.asarray(SCALE, dtype)
        key = jax.random.key(seed)
        k_x, k_g, k_u, k_d = jax.random.split(key, 4)
        x = jax.random.normal(k_x, (4, 256, DIM), dtype=jnp.float32)
        w_gate = jax.random.randint(k_g, (HIDDEN, DIM), -127, 128, dtype=jnp.int32)
        w_up = jax.random.randint(k_u, (HIDDEN, DIM), -127, 128, dtype=jnp.int32)
        w_down = jax.random.randint(k_d, (DIM, HIDDEN), -127, 128, dtype=jnp.int32)
        return {'x': x, 'w_gate': w_gate, 'w_up': w_up, 'w_down': w_down}
    _L0_ffn_in = _L0_ffn_setup()

    def _L1_attn_setup():
        import jax, jax.numpy as jnp
        import numpy as np
        ATT_WIDTH = 64

        def _band_mask(T, width, dtype):
            lower = width // 2
            upper = (width - 1) // 2
            i = jnp.arange(T)[:, None]
            j = jnp.arange(T)[None, :]
            keep = (i - j <= lower) & (j - i <= upper)
            return keep.astype(dtype)
        key = jax.random.key(seed)
        k1, k2, k3, k4 = jax.random.split(key, 4)
        B, T, H, D = (8, 256, 128, 128)
        scale = 1.0 / np.sqrt(H)
        return {'inputs': jax.random.normal(k1, (B, T, H), dtype=jnp.float32), 'WQ': jax.random.normal(k2, (H, D), dtype=jnp.float32) * scale, 'WK': jax.random.normal(k3, (H, D), dtype=jnp.float32) * scale, 'WV': jax.random.normal(k4, (H, D), dtype=jnp.float32) * scale}
    _L1_attn_in = _L1_attn_setup()

    def _L1_ffn_setup():
        import jax, jax.numpy as jnp
        import numpy as np
        E = 8
        K = 2
        D = 128
        B, N = (4, 512)
        DC = 64
        key = jax.random.key(seed)
        ks = jax.random.split(key, 6)
        x = jax.random.normal(ks[0], (B, N, D), jnp.float32)
        cond = jax.random.normal(ks[1], (B, N, DC), jnp.float32)
        mask = jnp.ones((B, N), jnp.float32)
        W_shared = jax.random.normal(ks[2], (D, D), jnp.float32) * 0.02
        W_expert = jax.random.normal(ks[3], (D, D), jnp.float32) * 0.02
        W_gate = jax.random.normal(ks[4], (D, E - 1), jnp.float32) * 0.02
        bias = jnp.zeros((D,), jnp.float32)
        return dict(x=x, cond=cond, mask=mask, W_shared=W_shared, W_expert=W_expert, W_gate=W_gate, bias=bias)
    _L1_ffn_in = _L1_ffn_setup()

    def _L2_attn_setup():
        import jax, jax.numpy as jnp
        import numpy as np
        B, T, DIM = (2, 128, 128)
        H, D = (16, 64)
        key = jax.random.key(seed)
        k1, k2, k3, k4 = jax.random.split(key, 4)
        s = DIM ** (-0.5)
        return {'x': jax.random.normal(k1, (B, T, DIM), jnp.float32), 'w_qkv': jax.random.normal(k2, (DIM, 3 * H * D), jnp.float32) * s, 'w_gate': jax.random.normal(k3, (DIM, H * D), jnp.float32) * s, 'w_out': jax.random.normal(k4, (H * D, DIM), jnp.float32) * s}
    _L2_attn_in = _L2_attn_setup()

    def _L2_ffn_setup():
        import jax, jax.numpy as jnp
        import numpy as np
        TOP_K = 2
        key = jax.random.key(seed)
        k1, k2, k3, k4, k5 = jax.random.split(key, 5)
        B, S, D, F, E = (2, 128, 128, 256, 8)
        return {'x': jax.random.normal(k1, (B, S, D), dtype=jnp.float32), 'router_kernel_DE': jax.random.normal(k2, (D, E), dtype=jnp.float32) * 0.02, 'kernel_gating_EDF': jax.random.normal(k3, (E, D, F), dtype=jnp.float32) * 0.02, 'kernel_up_EDF': jax.random.normal(k4, (E, D, F), dtype=jnp.float32) * 0.02, 'kernel_down_EFD': jax.random.normal(k5, (E, F, D), dtype=jnp.float32) * 0.02}
    _L2_ffn_in = _L2_ffn_setup()

    def _L3_attn_setup():
        import jax, jax.numpy as jnp
        import numpy as np
        import math
        D_MODEL = 128
        NUM_HEADS = 16
        HEAD_DIM = D_MODEL // NUM_HEADS
        key = jax.random.key(seed)
        k_x, k_qkv, k_o = jax.random.split(key, 3)
        B, S = (2, 256)
        x = jax.random.normal(k_x, (B, S, D_MODEL), dtype=jnp.float32)
        sigma_qkv = math.sqrt(2.0 / (D_MODEL + 3 * D_MODEL))
        w_qkv = jax.random.truncated_normal(k_qkv, -3.0, 3.0, (3 * D_MODEL, D_MODEL), dtype=jnp.float32) * sigma_qkv
        sigma_o = math.sqrt(2.0 / (D_MODEL + D_MODEL))
        w_out = jax.random.truncated_normal(k_o, -3.0, 3.0, (D_MODEL, D_MODEL), dtype=jnp.float32) * sigma_o
        return {'x': x, 'w_qkv': w_qkv, 'w_out': w_out}
    _L3_attn_in = _L3_attn_setup()

    def _L3_ffn_setup():
        import jax, jax.numpy as jnp
        import numpy as np
        DIM = 128
        DEPTH = 6
        HEADS = 16
        DIM_HEAD = 64
        WINDOW = 32
        INNER = HEADS * DIM_HEAD
        DIM_INNER = int(DIM * 4 * 2 / 3)
        QK_SCALE = 8.0

        def shift_tokens(t):
            a, s = jnp.split(t, 2, -1)
            s = jnp.pad(s, ((0, 0), (1, 0), (0, 0)))[:, :-1]
            return jnp.concatenate([a, s], -1)

        def l2norm(t):
            return t / jnp.maximum(jnp.linalg.norm(t, axis=-1, keepdims=True), 1e-12)

        def rotate_half(x):
            x1, x2 = jnp.split(x, 2, -1)
            return jnp.concatenate([-x2, x1], -1)

        def rotary_tables(n):
            half = jnp.arange(0, DIM_HEAD, 2, dtype=jnp.float32)
            inv_freq = 1.0 / 10000.0 ** (half / DIM_HEAD)
            t = jnp.arange(n, dtype=jnp.float32)
            freqs = t[:, None] * inv_freq[None, :]
            freqs = jnp.concatenate([freqs, freqs], -1)
            base_scale = (half + 0.4 * DIM_HEAD) / (1.4 * DIM_HEAD)
            power = (t - n // 2) / (WINDOW // 2)
            scale = base_scale[None, :] ** power[:, None]
            scale = jnp.concatenate([scale, scale], -1)
            return (freqs, scale)

        def local_attention(q, k, v):
            b, h, n, d = q.shape
            w = WINDOW
            nw = n // w
            bq = q.reshape(b, h, nw, w, d)
            bk = k.reshape(b, h, nw, w, d)
            bv = v.reshape(b, h, nw, w, d)

            def look(t):
                p = jnp.pad(t, ((0, 0), (0, 0), (1, 0), (0, 0), (0, 0)))
                return jnp.concatenate([p[:, :, :nw], p[:, :, 1:]], axis=3)
            bk2, bv2 = (look(bk), look(bv))
            seq = jnp.arange(n).reshape(nw, w)
            seq_p = jnp.pad(seq, ((1, 0), (0, 0)), constant_values=-1)
            jt = jnp.concatenate([seq_p[:nw], seq_p[1:]], axis=1)
            it = seq[:, :, None]
            jb = jt[:, None, :]
            mask = (it < jb) | (it > jb + w) | (jb == -1)
            sim = jnp.einsum('bhwie,bhwje->bhwij', bq, bk2) * QK_SCALE
            sim = jnp.where(mask, -jnp.finfo(sim.dtype).max, sim)
            attn = jax.nn.softmax(sim, -1)
            out = jnp.einsum('bhwij,bhwje->bhwie', attn, bv2)
            return out.reshape(b, h, n, d)

        def attn_layer(x, Wqkv, qs, ksc, Wo):
            b, n, _ = x.shape
            qkv = x @ Wqkv
            q, k, v = jnp.split(qkv, 3, -1)
            sh = lambda t: t.reshape(b, n, HEADS, DIM_HEAD).transpose(0, 2, 1, 3)
            q, k, v = (sh(q), sh(k), sh(v))
            q = l2norm(q) * qs
            k = l2norm(k) * ksc
            freqs, scale = rotary_tables(n)
            cos, sin = (jnp.cos(freqs), jnp.sin(freqs))
            q = q * cos * scale + rotate_half(q) * sin * scale
            inv = 1.0 / scale
            k = k * cos * inv + rotate_half(k) * sin * inv
            out = local_attention(q, k, v)
            out = out.transpose(0, 2, 1, 3).reshape(b, n, INNER)
            return out @ Wo

        def ffn_layer(x, g, bln, W1, b1, W2, b2):
            mu = x.mean(-1, keepdims=True)
            var = ((x - mu) ** 2).mean(-1, keepdims=True)
            xn = (x - mu) / jnp.sqrt(var + 1e-05) * g + bln
            hg = xn @ W1 + b1
            a, gate = jnp.split(hg, 2, -1)
            return a * jax.nn.gelu(gate, approximate=False) @ W2 + b2
        key = jax.random.key(seed)
        ks = jax.random.split(key, 8)
        B, N = (2, 256)
        init = lambda k, shape: jax.random.normal(k, shape, jnp.float32) * 0.02
        return {'x': jax.random.normal(ks[0], (B, N, DIM), jnp.float32), 'Wqkv': init(ks[1], (DEPTH, DIM, 3 * INNER)), 'q_scale': jnp.ones((DEPTH, DIM_HEAD), jnp.float32), 'k_scale': jnp.ones((DEPTH, DIM_HEAD), jnp.float32), 'Wo': init(ks[2], (DEPTH, INNER, DIM)), 'ln_g': jnp.ones((DEPTH, DIM), jnp.float32), 'ln_b': jnp.zeros((DEPTH, DIM), jnp.float32), 'W1': init(ks[3], (DEPTH, DIM, 2 * DIM_INNER)), 'b1': jnp.zeros((DEPTH, 2 * DIM_INNER), jnp.float32), 'W2': init(ks[4], (DEPTH, DIM_INNER, DIM)), 'b2': jnp.zeros((DEPTH, DIM), jnp.float32)}
    _L3_ffn_in = _L3_ffn_setup()
    _d = {'L0_attn_x': _L0_attn_in['x'], 'L0_attn_Wq': _L0_attn_in['Wq'], 'L0_attn_Wk': _L0_attn_in['Wk'], 'L0_attn_Wv': _L0_attn_in['Wv'], 'L0_attn_Wproj': _L0_attn_in['Wproj'], 'L0_attn_lambda_q1': _L0_attn_in['lambda_q1'], 'L0_attn_lambda_k1': _L0_attn_in['lambda_k1'], 'L0_attn_lambda_q2': _L0_attn_in['lambda_q2'], 'L0_attn_lambda_k2': _L0_attn_in['lambda_k2'], 'L0_ffn_w_gate': _L0_ffn_in['w_gate'], 'L0_ffn_w_up': _L0_ffn_in['w_up'], 'L0_ffn_w_down': _L0_ffn_in['w_down'], 'L1_attn_WQ': _L1_attn_in['WQ'], 'L1_attn_WK': _L1_attn_in['WK'], 'L1_attn_WV': _L1_attn_in['WV'], 'L1_ffn_cond': _L1_ffn_in['cond'], 'L1_ffn_mask': _L1_ffn_in['mask'], 'L1_ffn_W_shared': _L1_ffn_in['W_shared'], 'L1_ffn_W_expert': _L1_ffn_in['W_expert'], 'L1_ffn_W_gate': _L1_ffn_in['W_gate'], 'L1_ffn_bias': _L1_ffn_in['bias'], 'L2_attn_w_qkv': _L2_attn_in['w_qkv'], 'L2_attn_w_gate': _L2_attn_in['w_gate'], 'L2_attn_w_out': _L2_attn_in['w_out'], 'L2_ffn_router_kernel_DE': _L2_ffn_in['router_kernel_DE'], 'L2_ffn_kernel_gating_EDF': _L2_ffn_in['kernel_gating_EDF'], 'L2_ffn_kernel_up_EDF': _L2_ffn_in['kernel_up_EDF'], 'L2_ffn_kernel_down_EFD': _L2_ffn_in['kernel_down_EFD'], 'L3_attn_w_qkv': _L3_attn_in['w_qkv'], 'L3_attn_w_out': _L3_attn_in['w_out'], 'L3_ffn_Wqkv': _L3_ffn_in['Wqkv'], 'L3_ffn_q_scale': _L3_ffn_in['q_scale'], 'L3_ffn_k_scale': _L3_ffn_in['k_scale'], 'L3_ffn_Wo': _L3_ffn_in['Wo'], 'L3_ffn_ln_g': _L3_ffn_in['ln_g'], 'L3_ffn_ln_b': _L3_ffn_in['ln_b'], 'L3_ffn_W1': _L3_ffn_in['W1'], 'L3_ffn_b1': _L3_ffn_in['b1'], 'L3_ffn_W2': _L3_ffn_in['W2'], 'L3_ffn_b2': _L3_ffn_in['b2']}
    _x0 = _d['L0_attn_x']
    _d['L0_attn_x'] = jax.random.normal(jax.random.fold_in(jax.random.key(seed), 1), (4, 512, 128), dtype=_x0.dtype)
    del _x0
    return _d

def reference(L0_attn_x, L0_attn_Wq, L0_attn_Wk, L0_attn_Wv, L0_attn_Wproj, L0_attn_lambda_q1, L0_attn_lambda_k1, L0_attn_lambda_q2, L0_attn_lambda_k2, L0_ffn_w_gate, L0_ffn_w_up, L0_ffn_w_down, L1_attn_WQ, L1_attn_WK, L1_attn_WV, L1_ffn_cond, L1_ffn_mask, L1_ffn_W_shared, L1_ffn_W_expert, L1_ffn_W_gate, L1_ffn_bias, L2_attn_w_qkv, L2_attn_w_gate, L2_attn_w_out, L2_ffn_router_kernel_DE, L2_ffn_kernel_gating_EDF, L2_ffn_kernel_up_EDF, L2_ffn_kernel_down_EFD, L3_attn_w_qkv, L3_attn_w_out, L3_ffn_Wqkv, L3_ffn_q_scale, L3_ffn_k_scale, L3_ffn_Wo, L3_ffn_ln_g, L3_ffn_ln_b, L3_ffn_W1, L3_ffn_b1, L3_ffn_W2, L3_ffn_b2):

    def _L0_attn_ref(x, Wq, Wk, Wv, Wproj, lambda_q1, lambda_k1, lambda_q2, lambda_k2):
        import jax, jax.numpy as jnp
        import numpy as np
        N_HEAD = 16
        D_MODEL = 128
        HEAD_DIM = D_MODEL // N_HEAD
        LAMBDA_INIT = 0.8 - 0.6 * float(np.exp(-0.3 * 1))

        def _rms_norm(x):
            eps = jnp.finfo(x.dtype).eps
            return x * jax.lax.rsqrt(jnp.mean(jnp.square(x), axis=-1, keepdims=True) + eps)

        def _rotary_cos_sin(T, dim, base=10000.0):
            inv_freq = 1.0 / base ** (jnp.arange(0, dim, 2, dtype=jnp.float32) / dim)
            freqs = jnp.outer(jnp.arange(T, dtype=jnp.float32), inv_freq)
            return (jnp.cos(freqs), jnp.sin(freqs))

        def _apply_rotary(x, cos, sin):
            d = x.shape[-1] // 2
            c = cos[None, :, None, None, :]
            s = sin[None, :, None, None, :]
            x1, x2 = (x[..., :d], x[..., d:])
            return jnp.concatenate([x1 * c + x2 * s, -x1 * s + x2 * c], axis=-1)

        def _causal_attn(q, k, v, scale):
            T = q.shape[1]
            scores = jnp.einsum('bthd,bshd->bhts', q, k) * scale
            mask = jnp.tril(jnp.ones((T, T), dtype=bool))
            scores = jnp.where(mask, scores, -jnp.inf)
            w = jax.nn.softmax(scores, axis=-1)
            return jnp.einsum('bhts,bshd->bthd', w, v)
        B, T, D = x.shape
        nh, hd = (N_HEAD, HEAD_DIM)
        q = (x @ Wq.T).reshape(B, T, 2, nh // 2, hd)
        k = (x @ Wk.T).reshape(B, T, 2, nh // 2, hd)
        v = (x @ Wv.T).reshape(B, T, nh // 2, 2 * hd)
        q, k = (_rms_norm(q), _rms_norm(k))
        cos, sin = _rotary_cos_sin(T, hd)
        q, k = (_apply_rotary(q, cos, sin), _apply_rotary(k, cos, sin))
        q1, q2 = (q[:, :, 0], q[:, :, 1])
        k1, k2 = (k[:, :, 0], k[:, :, 1])
        scale = 1.0 / jnp.sqrt(jnp.asarray(hd, x.dtype))
        y1 = _causal_attn(q1, k1, v, scale)
        y2 = _causal_attn(q2, k2, v, scale)
        lambda_1 = jnp.exp(jnp.sum(lambda_q1 * lambda_k1))
        lambda_2 = jnp.exp(jnp.sum(lambda_q2 * lambda_k2))
        lambda_full = lambda_1 - lambda_2 + LAMBDA_INIT
        y = (y1 - lambda_full * y2).reshape(B, T, D)
        return y @ Wproj.T

    def _L0_ffn_ref(x, w_gate, w_up, w_down):
        import jax, jax.numpy as jnp
        import numpy as np
        DIM = 128
        HIDDEN = 384
        SCALE = 1.0 / 127.0

        def _dequant(w_int, dtype):
            return w_int.astype(dtype) * jnp.asarray(SCALE, dtype)
        wg = _dequant(w_gate, x.dtype)
        wu = _dequant(w_up, x.dtype)
        wd = _dequant(w_down, x.dtype)
        gate = jnp.einsum('bsd,hd->bsh', x, wg)
        up = jnp.einsum('bsd,hd->bsh', x, wu)
        h = jax.nn.silu(gate) * up
        return jnp.einsum('bsh,dh->bsd', h, wd)

    def _L1_attn_ref(inputs, WQ, WK, WV):
        import jax, jax.numpy as jnp
        import numpy as np
        ATT_WIDTH = 64

        def _band_mask(T, width, dtype):
            lower = width // 2
            upper = (width - 1) // 2
            i = jnp.arange(T)[:, None]
            j = jnp.arange(T)[None, :]
            keep = (i - j <= lower) & (j - i <= upper)
            return keep.astype(dtype)
        B, T, H = inputs.shape
        D = WQ.shape[1]
        scale = jnp.asarray(D, inputs.dtype) ** 0.5
        q = jnp.einsum('bth,hd->btd', inputs, WQ)
        k = jnp.einsum('bth,hd->btd', inputs, WK)
        v = jnp.einsum('bth,hd->btd', inputs, WV)
        score = jnp.einsum('bqd,bkd->bqk', q, k) / scale
        local = _band_mask(T, ATT_WIDTH, score.dtype)
        score = score * local[None, :, :]
        attn = jax.nn.softmax(score, axis=-1)
        return jnp.einsum('bqk,bkd->bqd', attn, v)

    def _L1_ffn_ref(x, cond, mask, W_shared, W_expert, W_gate, bias):
        import jax, jax.numpy as jnp
        import numpy as np
        E = 8
        K = 2
        D = 128
        B, N = (4, 512)
        DC = 64
        b, n, d = x.shape
        T = b * n
        xf = x.reshape(T, d)
        scores = jax.nn.softmax(xf @ W_gate, axis=-1)
        expert_weights, _ = jax.lax.top_k(scores, K)
        expert_weights = expert_weights / expert_weights.sum(-1, keepdims=True)
        expert_indices = (jnp.arange(T * K) % E).reshape(T, K)
        te = expert_indices.reshape(-1)
        w = expert_weights.reshape(-1)
        capacity = K * T // E
        order = jnp.argsort(te, stable=True)
        sorted_e = te[order]
        hist = jnp.bincount(te, length=E)
        starts = jnp.concatenate([jnp.zeros((1,), hist.dtype), jnp.cumsum(hist)[:-1]])
        pos = jnp.arange(T * K) - starts[sorted_e]
        valid = pos < capacity
        dest = jnp.where(valid, sorted_e * capacity + pos, E * capacity)
        tok = order // K
        gathered = jnp.zeros((E * capacity + 1, d), x.dtype).at[dest].set(xf[tok])
        gathered = gathered[:-1]
        y = gathered @ W_expert.T
        contrib = w[order][:, None] * y[jnp.minimum(dest, E * capacity - 1)]
        moe_out = jnp.zeros((T, d), x.dtype).at[tok].add(jnp.where(valid[:, None], contrib, 0.0))
        shared = xf @ W_shared.T
        out = (shared + moe_out + bias).reshape(b, n, d)
        return out

    def _L2_attn_ref(x, w_qkv, w_gate, w_out):
        import jax, jax.numpy as jnp
        import numpy as np
        B, T, DIM = (2, 128, 128)
        H, D = (16, 64)
        b, t, c = x.shape
        qkv = (x @ w_qkv).reshape(b, t, 3, H, D)
        q, k, v = (qkv[:, :, 0], qkv[:, :, 1], qkv[:, :, 2])
        gate = jax.nn.sigmoid((x @ w_gate).reshape(b, t, H, D))
        q = jax.nn.elu(q) + 1.0
        k = jax.nn.elu(k) + 1.0
        k_cum = jnp.cumsum(k, axis=1)
        kv = jnp.cumsum(k[..., None, :] * v[..., :, None], axis=1)
        numerator = jnp.einsum('bthj,bthij->bthi', q, kv)
        denominator = jnp.einsum('bthj,bthj->bth', q, k_cum)
        out = numerator / (denominator[..., None] + 1e-06)
        out = out * gate
        return out.reshape(b, t, H * D) @ w_out

    def _L2_ffn_ref(x, router_kernel_DE, kernel_gating_EDF, kernel_up_EDF, kernel_down_EFD):
        import jax, jax.numpy as jnp
        import numpy as np
        TOP_K = 2
        E = router_kernel_DE.shape[-1]
        x = x.astype(jnp.float32)
        logits_BSE = jnp.einsum('BSD,DE->BSE', x, router_kernel_DE)
        probs_BSE = jax.nn.softmax(logits_BSE.astype(jnp.float32), axis=-1)
        weights_BSK, indices_BSK = jax.lax.top_k(probs_BSE, TOP_K)
        norm_weights_BSK = jax.nn.softmax(weights_BSK, axis=-1)
        one_hot_BSKE = jax.nn.one_hot(indices_BSK, num_classes=E, dtype=x.dtype)
        full_weights_BSE = jnp.sum(one_hot_BSKE * norm_weights_BSK[..., None], axis=2)
        gating_BSEF = jnp.einsum('BSD,EDF->BSEF', x, kernel_gating_EDF)
        act_BSEF = jax.nn.silu(gating_BSEF)
        up_BSEF = jnp.einsum('BSD,EDF->BSEF', x, kernel_up_EDF)
        fuse_BSEF = act_BSEF * up_BSEF
        down_BSED = jnp.einsum('BSEF,EFD->BSED', fuse_BSEF, kernel_down_EFD)
        out_BSD = jnp.einsum('BSED,BSE->BSD', down_BSED, full_weights_BSE)
        return out_BSD.astype(jnp.float32)

    def _L3_attn_ref(x, w_qkv, w_out):
        import jax, jax.numpy as jnp
        import numpy as np
        import math
        D_MODEL = 128
        NUM_HEADS = 16
        HEAD_DIM = D_MODEL // NUM_HEADS
        B, S, _ = x.shape
        qkv = jnp.einsum('bsi,oi->bso', x, w_qkv)
        q, k, v = jnp.split(qkv, 3, axis=-1)

        def to_heads(t):
            return t.reshape(B, S, NUM_HEADS, HEAD_DIM).transpose(0, 2, 1, 3)
        q, k, v = (to_heads(q), to_heads(k), to_heads(v))
        scale = 1.0 / math.sqrt(HEAD_DIM)
        logits = jnp.einsum('bhsd,bhtd->bhst', q, k) * scale
        mask = jnp.tril(jnp.ones((S, S), dtype=bool))
        neg_inf = jnp.finfo(jnp.float32).min
        logits = jnp.where(mask, logits, neg_inf)
        probs = jax.nn.softmax(logits, axis=-1)
        probs = probs * mask.astype(probs.dtype)
        out = jnp.einsum('bhst,bhtd->bhsd', probs, v)
        out = out.transpose(0, 2, 1, 3).reshape(B, S, D_MODEL)
        return jnp.einsum('bsi,oi->bso', out, w_out)

    def _L3_ffn_ref(x, Wqkv, q_scale, k_scale, Wo, ln_g, ln_b, W1, b1, W2, b2):
        import jax, jax.numpy as jnp
        import numpy as np
        DIM = 128
        DEPTH = 6
        HEADS = 16
        DIM_HEAD = 64
        WINDOW = 32
        INNER = HEADS * DIM_HEAD
        DIM_INNER = int(DIM * 4 * 2 / 3)
        QK_SCALE = 8.0

        def shift_tokens(t):
            a, s = jnp.split(t, 2, -1)
            s = jnp.pad(s, ((0, 0), (1, 0), (0, 0)))[:, :-1]
            return jnp.concatenate([a, s], -1)

        def l2norm(t):
            return t / jnp.maximum(jnp.linalg.norm(t, axis=-1, keepdims=True), 1e-12)

        def rotate_half(x):
            x1, x2 = jnp.split(x, 2, -1)
            return jnp.concatenate([-x2, x1], -1)

        def rotary_tables(n):
            half = jnp.arange(0, DIM_HEAD, 2, dtype=jnp.float32)
            inv_freq = 1.0 / 10000.0 ** (half / DIM_HEAD)
            t = jnp.arange(n, dtype=jnp.float32)
            freqs = t[:, None] * inv_freq[None, :]
            freqs = jnp.concatenate([freqs, freqs], -1)
            base_scale = (half + 0.4 * DIM_HEAD) / (1.4 * DIM_HEAD)
            power = (t - n // 2) / (WINDOW // 2)
            scale = base_scale[None, :] ** power[:, None]
            scale = jnp.concatenate([scale, scale], -1)
            return (freqs, scale)

        def local_attention(q, k, v):
            b, h, n, d = q.shape
            w = WINDOW
            nw = n // w
            bq = q.reshape(b, h, nw, w, d)
            bk = k.reshape(b, h, nw, w, d)
            bv = v.reshape(b, h, nw, w, d)

            def look(t):
                p = jnp.pad(t, ((0, 0), (0, 0), (1, 0), (0, 0), (0, 0)))
                return jnp.concatenate([p[:, :, :nw], p[:, :, 1:]], axis=3)
            bk2, bv2 = (look(bk), look(bv))
            seq = jnp.arange(n).reshape(nw, w)
            seq_p = jnp.pad(seq, ((1, 0), (0, 0)), constant_values=-1)
            jt = jnp.concatenate([seq_p[:nw], seq_p[1:]], axis=1)
            it = seq[:, :, None]
            jb = jt[:, None, :]
            mask = (it < jb) | (it > jb + w) | (jb == -1)
            sim = jnp.einsum('bhwie,bhwje->bhwij', bq, bk2) * QK_SCALE
            sim = jnp.where(mask, -jnp.finfo(sim.dtype).max, sim)
            attn = jax.nn.softmax(sim, -1)
            out = jnp.einsum('bhwij,bhwje->bhwie', attn, bv2)
            return out.reshape(b, h, n, d)

        def attn_layer(x, Wqkv, qs, ksc, Wo):
            b, n, _ = x.shape
            qkv = x @ Wqkv
            q, k, v = jnp.split(qkv, 3, -1)
            sh = lambda t: t.reshape(b, n, HEADS, DIM_HEAD).transpose(0, 2, 1, 3)
            q, k, v = (sh(q), sh(k), sh(v))
            q = l2norm(q) * qs
            k = l2norm(k) * ksc
            freqs, scale = rotary_tables(n)
            cos, sin = (jnp.cos(freqs), jnp.sin(freqs))
            q = q * cos * scale + rotate_half(q) * sin * scale
            inv = 1.0 / scale
            k = k * cos * inv + rotate_half(k) * sin * inv
            out = local_attention(q, k, v)
            out = out.transpose(0, 2, 1, 3).reshape(b, n, INNER)
            return out @ Wo

        def ffn_layer(x, g, bln, W1, b1, W2, b2):
            mu = x.mean(-1, keepdims=True)
            var = ((x - mu) ** 2).mean(-1, keepdims=True)
            xn = (x - mu) / jnp.sqrt(var + 1e-05) * g + bln
            hg = xn @ W1 + b1
            a, gate = jnp.split(hg, 2, -1)
            return a * jax.nn.gelu(gate, approximate=False) @ W2 + b2
        for i in range(DEPTH):
            x = attn_layer(shift_tokens(x), Wqkv[i], q_scale[i], k_scale[i], Wo[i]) + x
            x = ffn_layer(shift_tokens(x), ln_g[i], ln_b[i], W1[i], b1[i], W2[i], b2[i]) + x
        return x
    x = L0_attn_x
    x = x + _layernorm(_L0_attn_ref(_layernorm(x, axis=-1), L0_attn_Wq, L0_attn_Wk, L0_attn_Wv, L0_attn_Wproj, L0_attn_lambda_q1, L0_attn_lambda_k1, L0_attn_lambda_q2, L0_attn_lambda_k2), axis=-1)
    x = x + _layernorm(_L0_ffn_ref(_layernorm(x, axis=-1), L0_ffn_w_gate, L0_ffn_w_up, L0_ffn_w_down), axis=-1)
    x = x + _layernorm(_L1_attn_ref(_layernorm(x, axis=-1), L1_attn_WQ, L1_attn_WK, L1_attn_WV), axis=-1)
    x = x + _layernorm(_L1_ffn_ref(_layernorm(x, axis=-1), L1_ffn_cond, L1_ffn_mask, L1_ffn_W_shared, L1_ffn_W_expert, L1_ffn_W_gate, L1_ffn_bias), axis=-1)
    x = x + _layernorm(_L2_attn_ref(_layernorm(x, axis=-1), L2_attn_w_qkv, L2_attn_w_gate, L2_attn_w_out), axis=-1)
    x = x + _layernorm(_L2_ffn_ref(_layernorm(x, axis=-1), L2_ffn_router_kernel_DE, L2_ffn_kernel_gating_EDF, L2_ffn_kernel_up_EDF, L2_ffn_kernel_down_EFD), axis=-1)
    x = x + _layernorm(_L3_attn_ref(_layernorm(x, axis=-1), L3_attn_w_qkv, L3_attn_w_out), axis=-1)
    x = x + _layernorm(_L3_ffn_ref(_layernorm(x, axis=-1), L3_ffn_Wqkv, L3_ffn_q_scale, L3_ffn_k_scale, L3_ffn_Wo, L3_ffn_ln_g, L3_ffn_ln_b, L3_ffn_W1, L3_ffn_b1, L3_ffn_W2, L3_ffn_b2), axis=-1)
    return x

_drawn_inputs = setup_inputs


def setup_inputs(seed=0):
    import zlib

    import numpy as np

    out = dict(_drawn_inputs(seed))
    spreads = {'L1_ffn_bias': (0.0, 0.1),
     'L3_ffn_q_scale': (1.0, 0.6),
     'L3_ffn_k_scale': (1.0, 0.6),
     'L3_ffn_ln_g': (1.0, 0.6),
     'L3_ffn_ln_b': (0.0, 0.8),
     'L3_ffn_b1': (0.0, 0.8),
     'L3_ffn_b2': (0.0, 0.8)}
    factors = {'L1_ffn_W_gate': 64.0, 'L3_ffn_W1': 7.258, 'L3_ffn_W2': 6.99}
    for name, (base, spread) in spreads.items():
        noise = np.random.default_rng([zlib.crc32(name.encode()), seed]).standard_normal(out[name].shape)
        drawn = base * np.exp(spread * noise) if base else spread * noise
        out[name] = jnp.asarray(drawn.astype(out[name].dtype))
    for name, factor in factors.items():
        out[name] = (out[name] * factor).astype(out[name].dtype)
    return out
```

```python
from collections import namedtuple
from contextlib import ExitStack

import numpy as np

import concourse.bass as bass
from concourse import mybir

F32 = mybir.dt.float32
I32 = mybir.dt.int32
U32 = mybir.dt.uint32
ALU = mybir.AluOpType
ACT = mybir.ActivationFunctionType
AX_X = mybir.AxisListType.X

P = 128
D = 128
SEQS = 4
TOK = 512
TILES = TOK // P
ALL_TILES = SEQS * TILES
BANK = 512
LN_EPS = 1e-5


class Shared:
    pass


def normalise_rows(core, dve, src, dst, sems, turn):
    st, sm = core.bn, core.small
    with dve.Fori(0, SEQS) as g:
        for u in range(4):
            dve.bn_stats(st[:, g * 4 + u, :], src[:, g, u, :])
    dve.drain()
    dve.tensor_tensor(sm[:, 0], st[:, :, 1], st[:, :, 4], ALU.add)
    dve.tensor_tensor(sm[:, 1], st[:, :, 1], st[:, :, 4], ALU.subtract)
    dve.tensor_tensor(sm[:, 2], st[:, :, 2], st[:, :, 5], ALU.add)
    dve.drain()
    dve.tensor_scalar(sm[:, 3], sm[:, 0], 0.5, None, ALU.mult)
    dve.tensor_tensor(sm[:, 4], sm[:, 1], sm[:, 1], ALU.mult)
    dve.tensor_scalar(sm[:, 5], sm[:, 2], 1.0 / D, LN_EPS, ALU.mult, ALU.add)
    dve.drain()
    dve.scalar_tensor_tensor(out=sm[:, 6], in0=sm[:, 4], scalar=0.25, in1=sm[:, 5],
                             op0=ALU.mult, op1=ALU.add).then_inc(sems.var_ready, 1)
    dve.wait_ge(sems.rstd_ready, turn + 1)
    for g in range(SEQS):
        for t in range(TILES):
            n = TILES * g + t
            last = dve.tensor_scalar(dst[:, g, t, :], src[:, g, t, :], sm[:, 3, n:n + 1], sm[:, 7, n:n + 1],
                                     ALU.subtract, ALU.mult)
        if turn == sems.last_turn:
            last.then_inc(sems.xn_ready, 1)


def residual_and_norm(core, first=False, final=None):
    nc = core.nc
    turns = (0 if first else 1) + (1 if final is None else 0)
    with ExitStack() as ctx:
        sems = core.norm
        t0, c0 = sems.turns, sems.calls
        sems.turns += turns
        sems.calls += 1 if final is None else 0
        sems.last_turn = t0 + turns - 1 if final is None else -1
        x_ready, turned, stored = sems.x_ready, sems.turned, sems.stored
        x0 = sems.adds * SEQS
        sems.adds += 0 if first else 1
        block = ctx.enter_context(nc.Block())

        @block.sync
        def _(sync):
            if final is not None:
                for b in range(SEQS):
                    sync.wait_ge(x_ready, x0 + b + 1)
                    sync.dma_start(final[b].rearrange("(t p) d -> p t d", p=P),
                                   core.x[:, b]).then_inc(stored, 16)
                sync.wait_ge(stored, 16 * SEQS)

        @block.vector
        def _(dve):
            turn = t0
            if first:
                dve.wait_ge(core.x_loaded, 16)
                dve.wait_ge(core.tables_loaded, 16 * core.n_tables)
            else:
                normalise_rows(core, dve, core.y, core.y, sems, turn)
                turn += 1
                dve.drain()
                for b in range(SEQS):
                    dve.tensor_tensor(core.x[:, b], core.x[:, b], core.y[:, b], ALU.add).then_inc(x_ready, 1)
                dve.drain()
            if final is None:
                normalise_rows(core, dve, core.x, core.y, sems, turn)

        @block.tensor
        def _(pe):
            if final is None:
                if first:
                    pe.wait_ge(core.tables_loaded, 16 * core.n_tables)
                for b in range(SEQS):
                    pe.wait_ge(sems.xn_ready, c0 * SEQS + b + 1)
                    for t in range(TILES):
                        last = pe.transpose(core.ps[:, b, t * P:(t + 1) * P], core.y[:, b, t, :], core.ident[:])
                    last.then_inc(turned, 1)

        @block.scalar
        def _(act):
            for turn in range(t0, t0 + turns):
                act.wait_ge(sems.var_ready, turn + 1)
                inverse_sqrt(act, core.small[:, 7], core.small[:, 6], core.small[:, 7]).then_inc(sems.rstd_ready, 1)
            if final is None:
                for b in range(SEQS):
                    act.wait_ge(turned, c0 * SEQS + b + 1)
                    act.copy(core.xnT[:, b, :], core.ps[:, b, :])


def inverse_sqrt(act, dst, src, logs, scale=1.0):
    act.activation(logs, src, ACT.Ln, scale=scale)
    act.drain()
    return act.activation(dst, logs, ACT.Exp, scale=-0.5)


def pair_of_blocks(buf, c, off, step):
    v = buf[:, c, off:off + P].unsqueeze(1)
    return bass.AP(v.tensor, v.offset, [list(v.ap[0]), [step, 2], [1, P]])


def diff_attention(core, w):
    nc = core.nc
    HEADS, HD = 16, 8
    PAIRS, VD = HEADS // 2, 2 * HD
    VW = VD + 1
    SPAN = TILES * (TILES + 1) // 2 * P
    OFF = [0, 512, 1024, 896]
    LAMBDA_INIT = 0.8 - 0.6 * float(np.exp(-0.3 * 1))
    RMS_EPS = float(np.finfo(np.float32).eps)
    with ExitStack() as ctx:
        def sb(n, shape, dt=F32):
            return ctx.enter_context(nc.sbuf_tensor(f"da_{n}", shape, dt))

        def sem(n):
            return core.sem(f"da_{n}")

        wT = sb("wT", [P, 4, P])
        qk = sb("qk", [P, TILES, 2 * P])
        rot = sb("rot", [P, TILES, 2 * P])
        swp = sb("swp", [P, TILES, 2 * P])
        ss = sb("ss", [P, TILES, 2 * HEADS])
        rr = sb("rr", [P, TILES, 2 * HEADS])
        vals = sb("vals", [P, TILES, PAIRS, VW])
        qT = sb("qT", [P, TOK])
        kT = sb("kT", [P, TOK])
        qz = sb("qz", [P, 2, TOK])
        probs = sb("probs", [P, 2, SPAN])
        rden = sb("rden", [P, 2, TILES])
        part = sb("part", [P, 2, TILES, VD])
        att = sb("att", [P, TILES, PAIRS, VD])
        attT = sb("attT", [P, TOK])
        lam = sb("lam", [P, 8])
        lamv = sb("lamv", [P, 2, HD // 2])
        xs = sb("xs", [P, TOK])
        xs_ready = sem("xs_ready")
        w_turned = sem("w_turned")
        wT_ready = sem("wT_ready")
        lam_sums = sem("lam_sums")
        lam_exps = sem("lam_exps")
        ones_set = sem("ones_set")
        qkv_ready = sem("qkv_ready")
        sq_ready = sem("sq_ready")
        v_ready = sem("v_ready")
        ms_ready = sem("ms_ready")
        rms_ready = sem("rms_ready")
        rot_ready = sem("rot_ready")
        qkT_turned = sem("qkT_turned")
        qT_ready = sem("qT_ready")
        kT_ready = sem("kT_ready")
        qz_ready = sem("qz_ready")
        scores_ready = sem("scores_ready")
        exp_ready = sem("exp_ready")
        masked = sem("masked")
        out_ready = sem("out_ready")
        out_used = sem("out_used")
        att_ready = sem("att_ready")
        attT_turned = sem("attT_turned")
        attT_ready = sem("attT_ready")
        proj_ready = sem("proj_ready")
        proj_used = sem("proj_used")
        ps = core.ps
        scores = [ps[:, 0:3, :].rearrange("p a b -> p (a b)"), ps[:, 3:6, :].rearrange("p a b -> p (a b)")]
        outs = [ps[:, 6, 0:TILES * VW].rearrange("p (t c) -> p t c", c=VW),
                ps[:, 7, 0:TILES * VW].rearrange("p (t c) -> p t c", c=VW)]
        block = ctx.enter_context(nc.Block())

        @block.tensor
        def _(pe):
            pe.wait_ge(w.loaded, 16 * w.n)
            for n, m in enumerate((w.Wq, w.Wk, w.Wv, w.Wproj)):
                last = pe.transpose(ps[:, 0, n * P:(n + 1) * P], m[:], core.ident[:])
            last.then_inc(w_turned, 1)
            pe.wait_ge(wT_ready, 1)
            with pe.Fori(0, SEQS) as b:
                pe.wait_ge(proj_used, b + 1)
                pe.wait_ge(xs_ready, b + 1)
                for t in range(TILES):
                    last = pe.matmul(ps[:, t, 0:3 * P], xs[:, t * P:(t + 1) * P],
                                     wT[:, 0:3, :], start=True, stop=True)
                last.then_inc(qkv_ready, 1)
                pe.wait_ge(rot_ready, b + 1)
                for c in range(2):
                    for t in range(TILES):
                        last = pe.transpose(ps[:, 4 + c, t * P:(t + 1) * P], rot[:, t, c * P:(c + 1) * P],
                                            core.ident[:])
                last.then_inc(qkT_turned, 1)
                pe.wait_ge(kT_ready, b + 1)
                pe.wait_ge(v_ready, b + 1)

                def score(n, c):
                    pe.wait_ge(qz_ready, n)
                    for j in range(TILES):
                        last = pe.matmul(scores[c][:, OFF[j]:OFF[j] + TOK - j * P], kT[:, j * P:(j + 1) * P],
                                         qz[:, c, j * P:TOK], start=True, stop=True)
                    last.then_inc(scores_ready, 1)

                def values(n, c, pair):
                    pe.wait_ge(masked, n)
                    pe.wait_ge(out_used, n)
                    for i in range(TILES):
                        for j in range(i + 1):
                            last = pe.matmul(outs[c][:, i, :], probs[:, c, OFF[j] + (i - j) * P:OFF[j] + (i - j + 1) * P],
                                             vals[:, j, pair, :], start=(j == 0), stop=(j == i))
                    last.then_inc(out_ready, 1)

                score(b * HEADS + 1, 0)
                with pe.Fori(0, PAIRS - 1) as k:
                    score(b * HEADS + k * 2 + 2, 1)
                    values(b * HEADS + k * 2 + 1, 0, k)
                    score(b * HEADS + k * 2 + 3, 0)
                    values(b * HEADS + k * 2 + 2, 1, k)
                score(b * HEADS + HEADS, 1)
                values(b * HEADS + HEADS - 1, 0, PAIRS - 1)
                values(b * HEADS + HEADS, 1, PAIRS - 1)
                pe.wait_ge(att_ready, b + 1)
                for t in range(TILES):
                    last = pe.transpose(ps[:, 0, t * P:(t + 1) * P], att[:, t].rearrange("p h d -> p (h d)"), core.ident[:])
                last.then_inc(attT_turned, 1)
                pe.wait_ge(attT_ready, b + 1)
                for t in range(TILES):
                    last = pe.matmul(ps[:, 1, t * P:(t + 1) * P], attT[:, t * P:(t + 1) * P], wT[:, 3, :],
                                     start=True, stop=True)
                last.then_inc(proj_ready, 1)

        @block.scalar
        def _(act):
            act.wait_ge(w_turned, 1)
            act.copy(wT[:], ps[:, 0, :].rearrange("p (n c) -> p n c", n=4)).then_inc(wT_ready, 1)
            act.wait_ge(lam_sums, 1)
            act.activation(lam[:, 2:4], lam[:, 0:2], ACT.Exp).then_inc(lam_exps, 1)
            act.wait_ge(ones_set, 1)
            act.sem_inc(out_ready, 2)
            with act.Fori(0, SEQS) as b:
                act.wait_ge(qkv_ready, b + 2)
                act.activation(swp[:], ps[:, 0:TILES, 0:2 * P], ACT.Square).then_inc(sq_ready, 1)
                for t in range(TILES):
                    last = act.copy(vals[:, t, :, 0:VD], ps[:, t, 2 * P:3 * P].rearrange("p (h d) -> p h d", d=VD))
                last.then_inc(v_ready, 1)
                act.wait_ge(ms_ready, b + 1)
                inverse_sqrt(act, rr[:], ss[:], rr[:]).then_inc(rms_ready, 1)
                act.wait_ge(qkT_turned, b + 1)
                act.copy(qT[:], ps[:, 4, :]).then_inc(qT_ready, 1)
                act.copy(kT[:], ps[:, 5, :]).then_inc(kT_ready, 1)
                with act.Fori(0, PAIRS) as k:
                    for c in range(2):
                        act.wait_ge(scores_ready, b * HEADS + k * 2 + c + 1)
                        act.wait_ge(out_ready, b * HEADS + k * 2 + c + 1)
                        act.activation(probs[:, c, :], scores[c][:, 0:SPAN], ACT.Exp,
                                       scale=float(HD) ** -0.5).then_inc(exp_ready, 1)
                act.wait_ge(attT_turned, b + 1)
                act.copy(attT[:], ps[:, 0, :]).then_inc(attT_ready, 1)
                act.wait_ge(proj_ready, b + 1)
                act.copy(core.y[:, b],
                         ps[:, 1, :].rearrange("p (t d) -> p t d", t=TILES)).then_inc(proj_used, 1)

        @block.gpsimd
        def _(pool):
            pool.sem_inc(qkv_ready, 1)
            with pool.Fori(0, SEQS) as b:
                pool.wait_ge(qkv_ready, b + 1)
                pool.tensor_copy(xs[:], core.xnT[:, b, :]).then_inc(xs_ready, 1)

        @block.vector
        def _(dve):
            dve.wait_ge(w.loaded, 16 * w.n)
            dve.tensor_tensor(lamv[:, 0], w.lam[:, 0], w.lam[:, 1], ALU.mult)
            dve.tensor_tensor(lamv[:, 1], w.lam[:, 2], w.lam[:, 3], ALU.mult)
            dve.drain()
            dve.tensor_reduce(lam[:, 0:2], lamv[:], AX_X, ALU.add).then_inc(lam_sums, 1)
            dve.memset(vals[:], 1.0).then_inc(ones_set, 1)
            dve.sem_inc(proj_used, 1)
            dve.wait_ge(lam_exps, 1)
            dve.tensor_tensor(lam[:, 4:5], lam[:, 3:4], lam[:, 2:3], ALU.subtract)
            dve.drain()
            dve.tensor_scalar(lam[:, 5:6], lam[:, 4:5], -LAMBDA_INIT, None, ALU.add)
            dve.sem_inc(out_used, 2)
            heads = "p t (h d) -> p t h d"
            with dve.Fori(0, SEQS) as b:
                dve.wait_ge(sq_ready, b + 1)
                dve.tensor_reduce(ss[:], swp[:].rearrange(heads, d=HD), AX_X, ALU.add)
                dve.drain()
                dve.tensor_scalar(ss[:], ss[:], 1.0 / HD, RMS_EPS, ALU.mult, ALU.add).then_inc(ms_ready, 1)
                dve.wait_ge(rms_ready, b + 1)
                dve.wait_ge(v_ready, b + 1)
                for t in range(TILES):
                    dve.tensor_tensor(qk[:, t].rearrange("p (h d) -> p h d", d=HD),
                                      ps[:, t, 0:2 * P].rearrange("p (h d) -> p h d", d=HD),
                                      rr[:, t].unsqueeze(2).broadcast_to([P, 2 * HEADS, HD]), ALU.mult)
                dve.drain()
                for t in range(TILES):
                    src = qk[:, t].rearrange("p (h d) -> p h d", d=HD)
                    dst = swp[:, t].rearrange("p (h d) -> p h d", d=HD)
                    for half in range(2):
                        a, z = slice(4 * half, 4 * half + 4), slice(4 - 4 * half, 8 - 4 * half)
                        dve.tensor_tensor(dst[:, :, a], src[:, :, z],
                                          core.t.rope8[:, 1, t, a].unsqueeze(1).broadcast_to([P, 2 * HEADS, 4]), ALU.mult)
                    dve.tensor_tensor(rot[:, t].rearrange("p (h d) -> p h d", d=HD), src,
                                      core.t.rope8[:, 0, t, :].unsqueeze(1).broadcast_to([P, 2 * HEADS, HD]), ALU.mult)
                dve.drain()
                dve.tensor_tensor(rot[:], rot[:], swp[:], ALU.add).then_inc(rot_ready, 1)

                def head_q(n, h, c, ring_free):
                    if ring_free is not None:
                        dve.wait_ge(scores_ready, ring_free)
                    dve.tensor_scalar(qz[:, c, :], qT[:], core.t.head8[:, h, :], None, ALU.mult).then_inc(qz_ready, 1)

                def causal(n, c):
                    dve.wait_ge(exp_ready, n)
                    for off, step in ((0, 512), (896, 128)):
                        blocks = pair_of_blocks(probs, c, off, step)
                        last = dve.tensor_tensor(blocks, blocks,
                                                 core.t.upper[:].unsqueeze(1).broadcast_to([P, 2, P]), ALU.mult)
                    last.then_inc(masked, 1)

                def weigh(n, c, k):
                    dve.wait_ge(out_ready, n + 2)
                    dve.reciprocal(rden[:, c, :], outs[c][:, :, VD])
                    dve.drain()
                    dve.tensor_tensor(part[:, c], outs[c][:, :, 0:VD],
                                      rden[:, c, :].unsqueeze(2).broadcast_to([P, TILES, VD]), ALU.mult).then_inc(out_used, 1)
                    if c == 0:
                        return
                    dve.drain()
                    return dve.scalar_tensor_tensor(out=att[:, :, k, :], in0=part[:, 1], scalar=lam[:, 5:6],
                                                    in1=part[:, 0], op0=ALU.mult, op1=ALU.add)

                def step(k, c, more=True, before=True):
                    n = b * HEADS + k * 2 + c + 1
                    causal(n, c)
                    if more:
                        head_q(n, k + 1 + PAIRS * c, c, n)
                    if before:
                        weigh(n - 1, 1 - c, k if c else k - 1)

                dve.wait_ge(qT_ready, b + 1)
                head_q(0, 0, 0, None)
                head_q(0, PAIRS, 1, None)
                step(0, 0, before=False)
                step(0, 1)
                with dve.Fori(1, PAIRS - 1) as k:
                    step(k, 0)
                    step(k, 1)
                step(PAIRS - 1, 0, more=False)
                step(PAIRS - 1, 1, more=False)
                weigh(b * HEADS + HEADS, 1, PAIRS - 1).then_inc(att_ready, 1)


def gated_ffn(core, w):
    nc = core.nc
    CHUNKS = 384 // P
    with ExitStack() as ctx:
        def sb(n, shape, dt=F32):
            return ctx.enter_context(nc.sbuf_tensor(f"gf_{n}", shape, dt))

        def sem(n):
            return core.sem(f"gf_{n}")

        wf = sb("wf", [P, 3, CHUNKS, P])
        wT = sb("wT", [P, 3, CHUNKS, P])
        act_g = sb("act_g", [P, 2, TOK])
        hid = sb("hid", [P, 2, CHUNKS, TOK])
        w_float = sem("w_float")
        w_turned = sem("w_turned")
        wT_ready = sem("wT_ready")
        gu_ready = sem("gu_ready")
        silu_ready = sem("silu_ready")
        hid_ready = sem("hid_ready")
        down_ready = sem("down_ready")
        y_ready = sem("y_ready")
        ps = core.ps
        block = ctx.enter_context(nc.Block())

        @block.vector
        def _(dve):
            dve.wait_ge(w.loaded, 16 * w.n)
            for n, m in enumerate((w.gate, w.up, w.down)):
                last = dve.tensor_scalar(wf[:, n], m[:], float(np.float32(1.0 / 127.0)), None, ALU.mult)
            last.then_inc(w_float, 1)
            dve.sem_inc(y_ready, 1)
            with dve.Fori(0, SEQS // 2) as b2:
                for s in range(2):
                    for c in range(CHUNKS):
                        n = (b2 * 2 + s) * CHUNKS + c
                        dve.wait_ge(silu_ready, n + 1)
                        dve.tensor_tensor(hid[:, s, c], act_g[:, (s * CHUNKS + c) % 2], ps[:, 4 + (s * CHUNKS + c) % 2, :],
                                          ALU.mult).then_inc(hid_ready, 1)
                    dve.wait_ge(down_ready, b2 * 2 + s + 1)
                    dve.tensor_copy(core.y[:, b2 * 2 + s], ps[:, 6 + s, :].rearrange("p (t d) -> p t d", d=D)).then_inc(y_ready, 1)

        @block.tensor
        def _(pe):
            pe.wait_ge(w_float, 1)
            for n in range(3):
                for c in range(CHUNKS):
                    last = pe.transpose(ps[:, n, c * P:(c + 1) * P], wf[:, n, c, :], core.ident[:])
            last.then_inc(w_turned, 1)
            pe.wait_ge(wT_ready, 1)

            def down(n, s):
                pe.wait_ge(y_ready, n + 1)
                pe.wait_ge(hid_ready, (n + 1) * CHUNKS + 2)
                for t in range(TILES):
                    for c in range(CHUNKS):
                        last = pe.matmul(ps[:, 6 + s, t * P:(t + 1) * P], hid[:, s, c, t * P:(t + 1) * P], wT[:, 2, c, :],
                                         start=(c == 0), stop=(c == CHUNKS - 1))
                last.then_inc(down_ready, 1)

            with pe.Fori(0, SEQS // 2) as b2:
                for s in range(2):
                    for c in range(CHUNKS):
                        n = (b2 * 2 + s) * CHUNKS + c
                        pe.wait_ge(hid_ready, n + 1)
                        for g in range(2):
                            last = pe.matmul(ps[:, 2 + 2 * g + (s * CHUNKS + c) % 2, :], wT[:, g, c, :],
                                             core.xnT[:, b2 * 2 + s, :], start=True, stop=True)
                        last.then_inc(gu_ready, 1)
                    down(b2 * 2 + s, s)

        @block.scalar
        def _(act):
            act.wait_ge(w_turned, 1)
            act.copy(wT[:], ps[:, 0:3, 0:3 * P].rearrange("p n (c k) -> p n c k", c=CHUNKS)).then_inc(wT_ready, 1)
            act.sem_inc(hid_ready, 2)
            with act.Fori(0, SEQS // 2) as b2:
                for s in range(2):
                    for c in range(CHUNKS):
                        n = (b2 * 2 + s) * CHUNKS + c
                        act.wait_ge(gu_ready, n + 1)
                        act.wait_ge(hid_ready, n + 1)
                        act.activation(act_g[:, (s * CHUNKS + c) % 2], ps[:, 2 + (s * CHUNKS + c) % 2, :],
                                       ACT.Silu).then_inc(silu_ready, 1)


def band_attention(core, w):
    nc = core.nc
    STEPS = SEQS * TILES
    with ExitStack() as ctx:
        def sb(n, shape, dt=F32):
            return ctx.enter_context(nc.sbuf_tensor(f"ba_{n}", shape, dt))

        def sem(n):
            return core.sem(f"ba_{n}")

        xs = sb("xs", [P, TOK])
        qT = sb("qT", [P, TOK])
        kT = sb("kT", [P, TOK])
        vals = sb("vals", [P, TILES, D])
        sc = sb("sc", [P, 2, TOK])
        pr = sb("pr", [P, 2, TOK])
        prT = sb("prT", [P, 2, TILES, P])
        top = sb("top", [P, 2, 4])
        xs_ready = sem("xs_ready")
        qk_ready = sem("qk_ready")
        v_ready = sem("v_ready")
        qT_ready = sem("qT_ready")
        kT_ready = sem("kT_ready")
        vals_ready = sem("vals_ready")
        scores_ready = sem("scores_ready")
        banded = sem("banded")
        exp_ready = sem("exp_ready")
        turned = sem("turned")
        prT_ready = sem("prT_ready")
        out_ready = sem("out_ready")
        y_ready = sem("y_ready")
        ps = core.ps
        block = ctx.enter_context(nc.Block())

        @block.gpsimd
        def _(pool):
            pool.sem_inc(v_ready, 1)
            with pool.Fori(0, SEQS) as b:
                pool.wait_ge(v_ready, b + 1)
                pool.tensor_copy(xs[:], core.xnT[:, b, :]).then_inc(xs_ready, 1)

        @block.tensor
        def _(pe):
            pe.wait_ge(w.loaded, 16 * w.n)
            with pe.Fori(0, SEQS) as b:
                pe.wait_ge(y_ready, b * TILES + 2)
                for n, m in enumerate((w.WQ, w.WK)):
                    last = pe.matmul(ps[:, n, :], m[:], core.xnT[:, b, :], start=True, stop=True)
                last.then_inc(qk_ready, 1)
                pe.wait_ge(xs_ready, b + 1)
                for t in range(TILES):
                    last = pe.matmul(ps[:, 2, t * P:(t + 1) * P], xs[:, t * P:(t + 1) * P], w.WV[:], start=True, stop=True)
                last.then_inc(v_ready, 1)
                pe.wait_ge(qT_ready, b + 1)
                pe.wait_ge(kT_ready, b + 1)

                def score(t):
                    last = pe.matmul(ps[:, t % 2, :], qT[:, t * P:(t + 1) * P], kT[:], start=True, stop=True)
                    last.then_inc(scores_ready, 1)

                score(0)
                for t in range(TILES):
                    n = b * TILES + t
                    if t + 1 < TILES:
                        pe.wait_ge(banded, n + 1)
                        score(t + 1)
                    pe.wait_ge(exp_ready, n + 1)
                    for k in range(TILES):
                        last = pe.transpose(ps[:, 3 + t % 2, k * P:(k + 1) * P], pr[:, t % 2, k * P:(k + 1) * P], core.ident[:])
                    last.then_inc(turned, 1)
                    if t == 0:
                        pe.wait_ge(vals_ready, b + 1)
                    pe.wait_ge(prT_ready, n + 1)
                    pe.wait_ge(y_ready, n + 1)
                    for k in range(TILES):
                        last = pe.matmul(ps[:, 5 + t % 2, 0:D], prT[:, t % 2, k], vals[:, k], start=(k == 0),
                                         stop=(k == TILES - 1))
                    last.then_inc(out_ready, 1)

        @block.scalar
        def _(act):
            with act.Fori(0, SEQS) as b:
                act.wait_ge(qk_ready, b + 1)
                act.copy(qT[:], ps[:, 0, :]).then_inc(qT_ready, 1)
                act.wait_ge(v_ready, b + 2)
                act.copy(vals[:], ps[:, 2, :].rearrange("p (t d) -> p t d", d=D)).then_inc(vals_ready, 1)
                for t in range(TILES):
                    n = b * TILES + t
                    c = t % 2
                    act.wait_ge(banded, n + 1)
                    act.activation(pr[:, c], sc[:, c], ACT.Exp, bias=top[:, c, 1:2],
                                   accum_out=top[:, c, 2:3]).then_inc(exp_ready, 1)
                    act.wait_ge(turned, n + 1)
                    act.copy(prT[:, c], ps[:, 3 + c, :].rearrange("p (k q) -> p k q", q=P)).then_inc(prT_ready, 1)

        @block.vector
        def _(dve):
            dve.sem_inc(y_ready, 2)
            with dve.Fori(0, SEQS) as b:
                dve.wait_ge(qk_ready, b + 1)
                dve.tensor_copy(kT[:], ps[:, 1, :]).then_inc(kT_ready, 1)

                def weigh(n, t):
                    c = t % 2
                    dve.wait_ge(exp_ready, n)
                    dve.reciprocal(top[:, c, 3:4], top[:, c, 2:3])
                    dve.drain()
                    dve.wait_ge(out_ready, n)
                    dve.tensor_scalar(core.y[:, b, t, :], ps[:, 5 + c, 0:D], top[:, c, 3:4], None, ALU.mult).then_inc(y_ready, 1)

                for t in range(TILES):
                    n = b * TILES + t
                    c = t % 2
                    dve.wait_ge(scores_ready, n + 1)
                    dve.tensor_tensor(sc[:, c], ps[:, c, :], core.t.band[:, t, :], ALU.mult)
                    dve.drain()
                    dve.tensor_reduce(top[:, c, 1:2], sc[:, c], AX_X, ALU.max, negate=True).then_inc(banded, 1)
                    if t:
                        weigh(n, t - 1)
                weigh(b * TILES + TILES, TILES - 1)


def shared_expert_ffn(core, w):
    nc = core.nc
    E1 = 7
    with ExitStack() as ctx:
        def sb(n, shape, dt=F32):
            return ctx.enter_context(nc.sbuf_tensor(f"se_{n}", shape, dt))

        def sem(n):
            return core.sem(f"se_{n}")

        xs = sb("xs", [P, 2, TOK])
        wT = sb("wT", [P, 2 * P + E1])
        pr = sb("pr", [P, TILES, 8])
        m = sb("m", [P, 8, TILES])
        top = sb("top", [P, TILES, 8])
        base = sb("base", [P, 2, TILES, D])
        one = sb("one", [P, TILES, D])
        w_turned = sem("w_turned")
        wT_ready = sem("wT_ready")
        xs_ready = sem("xs_ready")
        mm_ready = sem("mm_ready")
        shifted = sem("shifted")
        exp_ready = sem("exp_ready")
        y_ready = sem("y_ready")
        ps = core.ps
        block = ctx.enter_context(nc.Block())

        @block.gpsimd
        def _(pool):
            pool.wait_ge(w.loaded, 16 * w.n)
            pool.tensor_copy(wT[:, 2 * P:], w.W_gate[:]).then_inc(wT_ready, 1)
            pool.sem_inc(mm_ready, 2)
            with pool.Fori(0, SEQS // 2) as b2:
                for s in range(2):
                    pool.wait_ge(mm_ready, b2 * 2 + s + 1)
                    pool.tensor_copy(xs[:, s], core.xnT[:, b2 * 2 + s, :]).then_inc(xs_ready, 1)

        @block.tensor
        def _(pe):
            pe.wait_ge(w.loaded, 16 * w.n)
            for n, mat in enumerate((w.W_shared, w.W_expert)):
                last = pe.transpose(ps[:, 0, n * P:(n + 1) * P], mat[:], core.ident[:])
            last.then_inc(w_turned, 1)
            pe.wait_ge(wT_ready, 2)
            with pe.Fori(0, SEQS // 2) as b2:
                for s in range(2):
                    pe.wait_ge(xs_ready, b2 * 2 + s + 1)
                    pe.wait_ge(y_ready, b2 * 2 + s + 1)
                    for t in range(TILES):
                        last = pe.matmul(ps[:, 4 * s + t, 0:2 * P + E1], xs[:, s, t * P:(t + 1) * P], wT[:],
                                         start=True, stop=True)
                    last.then_inc(mm_ready, 1)

        @block.scalar
        def _(act):
            act.wait_ge(w_turned, 1)
            act.copy(wT[:, 0:2 * P], ps[:, 0, 0:2 * P]).then_inc(wT_ready, 1)
            with act.Fori(0, SEQS) as b:
                act.wait_ge(shifted, b + 1)
                act.activation(pr[:, :, 0:E1], pr[:, :, 0:E1], ACT.Exp).then_inc(exp_ready, 1)

        @block.vector
        def _(dve):
            dve.wait_ge(w.loaded, 16 * w.n)
            dve.memset(pr[:], -1.0)
            dve.sem_inc(y_ready, 2)
            dve.drain()
            with dve.Fori(0, SEQS // 2) as b2:
                for s in range(2):
                    n = b2 * 2 + s
                    logits = ps[:, 4 * s:4 * s + 4, 2 * P:2 * P + E1]
                    dve.wait_ge(mm_ready, n + 3)
                    dve.tensor_reduce(m[:, 0], logits, AX_X, ALU.max)
                    dve.drain()
                    dve.tensor_tensor(pr[:, :, 0:E1], logits, m[:, 0].unsqueeze(2).broadcast_to([P, TILES, E1]),
                                      ALU.subtract).then_inc(shifted, 1)
                    for t in range(TILES):
                        dve.tensor_tensor(base[:, s, t], ps[:, 4 * s + t, 0:P], w.bias[:], ALU.add)
                    dve.wait_ge(exp_ready, n + 1)
                    dve.tensor_reduce(m[:, 1], pr[:, :, 0:E1], AX_X, ALU.add)
                    dve.drain()
                    dve.reciprocal(m[:, 2], m[:, 1])
                    dve.drain()
                    dve.tensor_tensor(pr[:, :, 0:E1], pr[:, :, 0:E1], m[:, 2].unsqueeze(2).broadcast_to([P, TILES, E1]), ALU.mult)
                    dve.drain()
                    for t in range(TILES):
                        dve.max(top[:, t], pr[:, t])
                    dve.drain()
                    dve.tensor_tensor(m[:, 3], top[:, :, 0], top[:, :, 1], ALU.add)
                    dve.drain()
                    dve.reciprocal(m[:, 4], m[:, 3])
                    dve.drain()
                    for c in range(2):
                        dve.tensor_tensor(m[:, 5 + c], top[:, :, c], m[:, 4], ALU.mult)
                    dve.drain()
                    for t in range(TILES):
                        dve.scalar_tensor_tensor(out=one[:, t], in0=ps[:, 4 * s + t, P:2 * P], scalar=m[:, 5, t:t + 1],
                                                 in1=base[:, s, t], op0=ALU.mult, op1=ALU.add)
                    dve.drain()
                    for t in range(TILES):
                        last = dve.scalar_tensor_tensor(out=core.y[:, n, t, :], in0=ps[:, 4 * s + t, P:2 * P],
                                                        scalar=m[:, 6, t:t + 1], in1=one[:, t], op0=ALU.mult, op1=ALU.add)
                    last.then_inc(y_ready, 1)


def linear_attention(core, w):
    nc = core.nc
    HEADS, HD = 16, 64
    PAIRS = HEADS // 2
    INNER = HEADS * HD
    VW = HD + 1
    ROUNDS = [(0, 3), (3, 3), (6, 2)]
    with ExitStack() as ctx:
        def sb(n, shape, dt=F32):
            return ctx.enter_context(nc.sbuf_tensor(f"la_{n}", shape, dt))

        def sem(n):
            return core.sem(f"la_{n}")

        xs = sb("xs", [P, TOK])
        relu = sb("relu", [P, 2, BANK])
        expo = sb("expo", [P, 2, BANK])
        qk = sb("qk", [P, 2, 2, INNER])
        vals = sb("vals", [P, 2, HEADS, VW])
        gate = sb("gate", [P, 2, INNER])
        qT = sb("qT", [P, PAIRS, P])
        kTz = sb("kTz", [P, PAIRS, 2, P])
        inner = sb("inner", [P, PAIRS, 2, P])
        state = sb("state", [P, PAIRS, 2 * VW])
        rden = sb("rden", [P, HEADS])
        att = sb("att", [P, INNER])
        attT = sb("attT", [P, PAIRS, P])
        ready = sem("ready")
        xs_ready = sem("xs_ready")
        proj_ready = sem("proj_ready")
        exp_ready = sem("exp_ready")
        phi_ready = sem("phi_ready")
        vg_ready = sem("vg_ready")
        k_turned = sem("k_turned")
        q_turned = sem("q_turned")
        kz_low = sem("kz_low")
        kz_high = sem("kz_high")
        qT_ready = sem("qT_ready")
        inner_ready = sem("inner_ready")
        masked = sem("masked")
        out_ready = sem("out_ready")
        att_ready = sem("att_ready")
        outer_ready = sem("outer_ready")
        state_ready = sem("state_ready")
        att_turned = sem("att_turned")
        attT_ready = sem("attT_ready")
        y_psum = sem("y_psum")
        y_ready = sem("y_ready")
        ps = core.ps
        block = ctx.enter_context(nc.Block())
        rhs = [w.w_qkv[:, j * BANK:(j + 1) * BANK] for j in range(6)] + [w.w_gate[:, j * BANK:(j + 1) * BANK] for j in range(2)]

        @block.gpsimd
        def _(pool):
            pool.memset(kTz[:], 0.0)
            pool.memset(vals[:], 1.0)
            pool.memset(state[:], 0.0).then_inc(ready, 1)
            pool.sem_inc(y_psum, 2)
            with pool.Fori(0, SEQS) as b:
                pool.wait_ge(y_psum, b * TILES + 1)
                pool.tensor_copy(xs[:], core.xnT[:, b, :]).then_inc(xs_ready, 1)

        @block.tensor
        def _(pe):
            pe.wait_ge(w.loaded, 16 * w.n)
            pe.wait_ge(ready, 1)
            with pe.Fori(0, SEQS) as b:
                def project(t, js):
                    n = b * TILES + t
                    for j in js:
                        if j < 2:
                            pe.wait_ge(vg_ready, n * 4 + 3 + j)
                        elif j < 6:
                            pe.wait_ge(phi_ready, n * 4 + j - 1)
                        else:
                            pe.wait_ge(vg_ready, n * 4 + j - 1)
                        last = pe.matmul(ps[:, j % 2, :], xs[:, t * P:(t + 1) * P], rhs[j], start=True, stop=True)
                        last.then_inc(proj_ready, 1)

                def outer(t, r):
                    p0, np_ = ROUNDS[r]
                    pe.wait_ge(state_ready, (b * TILES + t) * 3 + r + 1)
                    for p in range(p0, p0 + np_):
                        last = pe.matmul(ps[:, 7, (p - p0) * 2 * VW:(p - p0 + 1) * 2 * VW],
                                         qk[:, t % 2, 1, p * P:(p + 1) * P],
                                         vals[:, t % 2, 2 * p:2 * p + 2, :].rearrange("p h c -> p (h c)"), start=True, stop=True)
                    last.then_inc(outer_ready, 1)

                pe.wait_ge(xs_ready, b + 1)
                project(0, range(8))
                for t in range(TILES):
                    n = b * TILES + t
                    s = t % 2
                    pe.wait_ge(phi_ready, n * 4 + 4)
                    pe.wait_ge(y_ready, n + 1)
                    pe.wait_ge(attT_ready, n + 1)
                    for p in range(PAIRS):
                        last = pe.transpose(ps[:, 2 + p // 4, (p % 4) * P:(p % 4 + 1) * P], qk[:, s, 1, p * P:(p + 1) * P], core.ident[:])
                    last.then_inc(k_turned, 1)
                    for p in range(PAIRS):
                        last = pe.transpose(ps[:, 4 + p // 4, (p % 4) * P:(p % 4 + 1) * P], qk[:, s, 0, p * P:(p + 1) * P], core.ident[:])
                    last.then_inc(q_turned, 1)
                    pe.wait_ge(kz_low, n + 1)
                    pe.wait_ge(kz_high, n + 1)
                    pe.wait_ge(qT_ready, n + 1)
                    for g in range(4):
                        if g >= 2:
                            pe.wait_ge(masked, n * 4 + g - 1)
                        for u in range(4):
                            p, h = 2 * g + u // 2, u % 2
                            last = pe.matmul(ps[:, 2 + g % 2, u * P:(u + 1) * P], kTz[:, p, h, :], qT[:, p, :], start=True, stop=True)
                        last.then_inc(inner_ready, 1)
                    pe.wait_ge(state_ready, n * 3 + 1)
                    pe.wait_ge(vg_ready, n * 4 + 6)
                    for r, (p0, np_) in enumerate(ROUNDS):
                        pe.wait_ge(masked, n * 4 + (p0 + np_ + 1) // 2)
                        for p in range(p0, p0 + np_):
                            o = (p - p0) * 2 * VW
                            pe.matmul(ps[:, 4 + r, o:o + 2 * VW], qT[:, p, :], state[:, p, :], start=True, stop=True)
                            for h in range(2):
                                last = pe.matmul(ps[:, 4 + r, o + h * VW:o + (h + 1) * VW], inner[:, p, h, :],
                                                 vals[:, s, 2 * p + h, :], start=False, stop=True, skip_group_check=True)
                        last.then_inc(out_ready, 1)
                    outer(t, 0)
                    if t + 1 < TILES:
                        project(t + 1, range(0, 4))
                    outer(t, 1)
                    if t + 1 < TILES:
                        project(t + 1, range(4, 8))
                    outer(t, 2)
                    pe.wait_ge(att_ready, n + 1)
                    for p in range(PAIRS):
                        last = pe.transpose(ps[:, 2 + p // 4, (p % 4) * P:(p % 4 + 1) * P], att[:, p * P:(p + 1) * P], core.ident[:])
                    last.then_inc(att_turned, 1)
                    pe.wait_ge(attT_ready, n + 2)
                    for p in range(PAIRS):
                        last = pe.matmul(ps[:, 6, 0:D], attT[:, p, :], w.w_out[:, p, :], start=(p == 0), stop=(p == PAIRS - 1))
                    last.then_inc(y_psum, 1)

        @block.scalar
        def _(act):
            act.wait_ge(ready, 1)
            act.sem_inc(vg_ready, 4)
            act.sem_inc(attT_ready, 1)
            with act.Fori(0, SEQS) as b:
                def features(t):
                    n = b * TILES + t
                    for j in range(8):
                        act.wait_ge(proj_ready, n * 8 + j + 1)
                        src = ps[:, j % 2, :]
                        if j < 4:
                            act.wait_ge(phi_ready, n * 4 + j - 1) if j >= 2 else None
                            act.activation(relu[:, j % 2], src, ACT.Relu, scale=-1.0)
                            act.drain()
                            act.activation(expo[:, j % 2], relu[:, j % 2], ACT.Exp, scale=-1.0).then_inc(exp_ready, 1)
                        elif j < 6:
                            act.copy(vals[:, t % 2, 8 * (j - 4):8 * (j - 3), 0:HD], src.rearrange("p (h d) -> p h d", d=HD)).then_inc(vg_ready, 1)
                        else:
                            act.activation(gate[:, t % 2, (j - 6) * BANK:(j - 5) * BANK], src, ACT.Tanh, scale=0.5).then_inc(vg_ready, 1)

                features(0)
                for t in range(TILES):
                    n = b * TILES + t
                    act.wait_ge(k_turned, n + 1)
                    act.copy(kTz[0:64, :, 0, :], ps[0:64, 2:4, :].rearrange("p a (b c) -> p (a b) c", c=P)).then_inc(kz_low, 1)
                    act.wait_ge(q_turned, n + 1)
                    act.copy(qT[:], ps[:, 4:6, :].rearrange("p a (b c) -> p (a b) c", c=P)).then_inc(qT_ready, 1)
                    if t + 1 < TILES:
                        features(t + 1)
                    act.wait_ge(att_turned, n + 1)
                    act.copy(attT[:], ps[:, 2:4, :].rearrange("p a (b c) -> p (a b) c", c=P)).then_inc(attT_ready, 1)

        @block.vector
        def _(dve):
            dve.wait_ge(ready, 1)
            dve.sem_inc(y_ready, 1)
            dve.sem_inc(state_ready, 1)
            with dve.Fori(0, SEQS) as b:
                def phi(t, j):
                    dve.wait_ge(exp_ready, (b * TILES + t) * 4 + j + 1)
                    dve.scalar_tensor_tensor(out=qk[:, t % 2, j // 2, (j % 2) * BANK:(j % 2 + 1) * BANK], in0=ps[:, j % 2, :],
                                             scalar=0.0, in1=expo[:, j % 2], op0=ALU.max, op1=ALU.add).then_inc(phi_ready, 1)

                def add_state(t, r):
                    p0, np_ = ROUNDS[r]
                    dve.wait_ge(outer_ready, (b * TILES + t) * 3 + r + 1)
                    src = ps[:, 7, 0:np_ * 2 * VW].rearrange("p (a c) -> p a c", c=2 * VW)
                    for h in range(2):
                        rows, cols = slice(64 * h, 64 * h + 64), slice(VW * h, VW * h + VW)
                        dst = state[rows, p0:p0 + np_, cols]
                        if t == TILES - 1:
                            last = dve.memset(dst, 0.0)
                        else:
                            last = dve.tensor_tensor(dst, dst, src[rows, :, cols], ALU.add)
                    last.then_inc(state_ready, 1)

                for j in range(4):
                    phi(0, j)
                for t in range(TILES):
                    n = b * TILES + t
                    dve.wait_ge(k_turned, n + 1)
                    dve.tensor_copy(kTz[64:128, :, 1, :], ps[64:128, 2:4, :].rearrange("p a (b c) -> p (a b) c", c=P)).then_inc(kz_high, 1)
                    for g in range(4):
                        dve.wait_ge(inner_ready, n * 4 + g + 1)
                        dve.tensor_tensor(inner[:, 2 * g:2 * g + 2].rearrange("p a h c -> p (a h) c"),
                                          ps[:, 2 + g % 2, :].rearrange("p (a c) -> p a c", c=P),
                                          core.t.upper[:].unsqueeze(1).broadcast_to([P, 4, P]), ALU.mult).then_inc(masked, 1)
                    dve.wait_ge(vg_ready, n * 4 + 8)
                    for r, (p0, np_) in enumerate(ROUNDS):
                        h0, nh = 2 * p0, 2 * np_
                        o = ps[:, 4 + r, 0:nh * VW].rearrange("p (h c) -> p h c", c=VW)
                        a = att[:, h0 * HD:(h0 + nh) * HD].rearrange("p (h c) -> p h c", c=HD)
                        dve.wait_ge(out_ready, n * 3 + r + 1)
                        dve.tensor_scalar(rden[:, h0:h0 + nh], o[:, :, HD], 2.0, 2e-6, ALU.mult, ALU.add)
                        dve.scalar_tensor_tensor(out=a, in0=gate[:, t % 2, h0 * HD:(h0 + nh) * HD].rearrange("p (h c) -> p h c", c=HD),
                                                 scalar=1.0, in1=o[:, :, 0:HD], op0=ALU.add, op1=ALU.mult)
                        dve.drain()
                        dve.reciprocal(rden[:, h0:h0 + nh], rden[:, h0:h0 + nh])
                        dve.drain()
                        last = dve.tensor_tensor(a, a, rden[:, h0:h0 + nh].unsqueeze(2).broadcast_to([P, nh, HD]), ALU.mult)
                    last.then_inc(att_ready, 1)
                    add_state(t, 0)
                    if t + 1 < TILES:
                        phi(t + 1, 0)
                        phi(t + 1, 1)
                    add_state(t, 1)
                    if t + 1 < TILES:
                        phi(t + 1, 2)
                        phi(t + 1, 3)
                    add_state(t, 2)
                    dve.wait_ge(y_psum, n + 3)
                    dve.tensor_copy(core.y[:, b, t, :], ps[:, 6, 0:D]).then_inc(y_ready, 1)


def expert_ffn(core, w):
    nc = core.nc
    E, CH = 8, 2
    STEPS = E * CH
    with ExitStack() as ctx:
        def sb(n, shape, dt=F32):
            return ctx.enter_context(nc.sbuf_tensor(f"ef_{n}", shape, dt))

        def sem(n):
            return core.sem(f"ef_{n}")

        xs = sb("xs", [P, TOK])
        pr = sb("pr", [P, TILES, E])
        top = sb("top", [P, TILES, 8])
        idx = sb("idx", [P, TILES, 8], U32)
        idf = sb("idf", [P, TILES, 8])
        m = sb("m", [P, 8, TILES])
        hot = sb("hot", [P, 2, TILES, E])
        full = sb("full", [P, TILES, E])
        act_g = sb("act_g", [P, 2, TOK])
        hid = sb("hid", [P, 2, CH, TOK])
        acc = sb("acc", [P, TILES, D])
        xs_ready = sem("xs_ready")
        routed = sem("routed")
        shifted = sem("shifted")
        exp_ready = sem("exp_ready")
        picked = sem("picked")
        exp2_ready = sem("exp2_ready")
        gu_ready = sem("gu_ready")
        silu_ready = sem("silu_ready")
        hid_ready = sem("hid_ready")
        down_ready = sem("down_ready")
        down_used = sem("down_used")
        ps = core.ps
        block = ctx.enter_context(nc.Block())

        @block.gpsimd
        def _(pool):
            pool.sem_inc(routed, 1)
            with pool.Fori(0, SEQS) as b:
                pool.wait_ge(routed, b + 1)
                pool.tensor_copy(xs[:], core.xnT[:, b, :]).then_inc(xs_ready, 1)

        @block.tensor
        def _(pe):
            pe.wait_ge(w.loaded, 16 * w.n)
            with pe.Fori(0, SEQS) as b:
                pe.wait_ge(xs_ready, b + 1)
                pe.wait_ge(down_used, b * E + 2)
                for t in range(TILES):
                    last = pe.matmul(ps[:, 6, t * E:(t + 1) * E], xs[:, t * P:(t + 1) * P], w.router[:], start=True, stop=True)
                last.then_inc(routed, 1)

                def down(e):
                    n = b * E + e
                    pe.wait_ge(down_used, n + 1)
                    pe.wait_ge(hid_ready, n * CH + CH + 2)
                    for t in range(TILES):
                        for c in range(CH):
                            last = pe.matmul(ps[:, 4 + e % 2, t * P:(t + 1) * P], hid[:, e % 2, c, t * P:(t + 1) * P],
                                             w.down[:, e, c, :], start=(c == 0), stop=(c == CH - 1))
                    last.then_inc(down_ready, 1)

                for e in range(E):
                    for c in range(CH):
                        pe.wait_ge(hid_ready, (b * E + e) * CH + c + 1)
                        for g, m_ in enumerate((w.gating, w.up)):
                            last = pe.matmul(ps[:, 2 * g + c, :], m_[:, e, c * P:(c + 1) * P], core.xnT[:, b, :], start=True, stop=True)
                        last.then_inc(gu_ready, 1)
                    if e:
                        down(e - 1)
                down(E - 1)

        @block.scalar
        def _(act):
            act.sem_inc(hid_ready, 2)
            with act.Fori(0, SEQS) as b:
                act.wait_ge(shifted, b + 1)
                act.activation(pr[:], pr[:], ACT.Exp).then_inc(exp_ready, 1)
                act.wait_ge(picked, b + 1)
                act.activation(m[:, 4], m[:, 3], ACT.Exp).then_inc(exp2_ready, 1)
                for e in range(E):
                    for c in range(CH):
                        n = (b * E + e) * CH + c
                        act.wait_ge(gu_ready, n + 1)
                        act.wait_ge(hid_ready, n + 1)
                        act.activation(act_g[:, c], ps[:, c, :], ACT.Silu).then_inc(silu_ready, 1)

        @block.vector
        def _(dve):
            dve.sem_inc(down_used, 2)
            with dve.Fori(0, SEQS) as b:
                dve.wait_ge(routed, b + 2)
                logits = ps[:, 6, 0:TILES * E].rearrange("p (t e) -> p t e", e=E)
                dve.tensor_reduce(m[:, 0], logits, AX_X, ALU.max)
                dve.drain()
                dve.tensor_tensor(pr[:], logits, m[:, 0].unsqueeze(2).broadcast_to([P, TILES, E]), ALU.subtract).then_inc(shifted, 1)
                dve.wait_ge(exp_ready, b + 1)
                dve.tensor_reduce(m[:, 1], pr[:], AX_X, ALU.add)
                dve.drain()
                dve.reciprocal(m[:, 2], m[:, 1])
                dve.drain()
                dve.tensor_tensor(pr[:], pr[:], m[:, 2].unsqueeze(2).broadcast_to([P, TILES, E]), ALU.mult)
                dve.drain()
                for t in range(TILES):
                    dve.max(top[:, t], pr[:, t])
                dve.drain()
                for t in range(TILES):
                    dve.max_index(idx[:, t], top[:, t], pr[:, t])
                dve.tensor_tensor(m[:, 3], top[:, :, 1], top[:, :, 0], ALU.subtract).then_inc(picked, 1)
                dve.drain()
                dve.tensor_copy(idf[:], idx[:])
                dve.drain()
                for k in range(2):
                    dve.tensor_tensor(hot[:, k], core.t.count8[:], idf[:, :, k:k + 1].broadcast_to([P, TILES, E]), ALU.is_equal)
                dve.wait_ge(exp2_ready, b + 1)
                dve.tensor_scalar(m[:, 5], m[:, 4], 1.0, None, ALU.add)
                dve.drain()
                dve.reciprocal(m[:, 6], m[:, 5])
                dve.drain()
                dve.tensor_tensor(m[:, 7], m[:, 6], m[:, 4], ALU.mult)
                dve.drain()
                for k in range(2):
                    dve.tensor_tensor(hot[:, k], hot[:, k], m[:, 6 + k].unsqueeze(2).broadcast_to([P, TILES, E]), ALU.mult)
                dve.drain()
                dve.tensor_tensor(full[:], hot[:, 0], hot[:, 1], ALU.add)
                dve.drain()

                def weigh(e):
                    n = b * E + e
                    dve.wait_ge(down_ready, n + 1)
                    for t in range(TILES):
                        src, dst, wt = ps[:, 4 + e % 2, t * P:(t + 1) * P], acc[:, t], full[:, t, e:e + 1]
                        if e == 0:
                            last = dve.tensor_scalar(dst, src, wt, None, ALU.mult)
                        else:
                            last = dve.scalar_tensor_tensor(out=core.y[:, b, t, :] if e == E - 1 else dst, in0=src, scalar=wt,
                                                            in1=dst, op0=ALU.mult, op1=ALU.add)
                    last.then_inc(down_used, 1)
                    dve.drain()

                for e in range(E):
                    for c in range(CH):
                        dve.wait_ge(silu_ready, (b * E + e) * CH + c + 1)
                        dve.tensor_tensor(hid[:, e % 2, c], act_g[:, c], ps[:, 2 + c, :], ALU.mult).then_inc(hid_ready, 1)
                    if e:
                        weigh(e - 1)
                weigh(E - 1)


def causal_attention(core, w):
    nc = core.nc
    HEADS, HD = 16, 8
    VW = HD + 1
    STEPS = 10
    QUADS = HEADS // 4
    SEGS = [[(0, 3, 0)], [(0, 2, 0), (0, 0, 384)], [(1, 3, 0)], [(1, 2, 0), (1, 0, 384)], [(0, 1, 0), (1, 1, 256)]]
    DIAG = [(384, 1, 0), (256, 2, P), (384, 1, 0), (256, 2, P), (P, 2, 256)]
    with ExitStack() as ctx:
        def sb(n, shape, dt=F32):
            return ctx.enter_context(nc.sbuf_tensor(f"ca_{n}", shape, dt))

        def sem(n):
            return core.sem(f"ca_{n}")

        xs = sb("xs", [P, TOK])
        wT = sb("wT", [P, 4, P])
        qT = sb("qT", [P, TOK])
        kT = sb("kT", [P, TOK])
        vals = sb("vals", [P, TILES, HEADS, VW])
        qz = sb("qz", [P, 4, TOK])
        top = sb("top", [P, 2, 2])
        pr = sb("pr", [P, 2, TOK])
        prT = sb("prT", [P, 2, TOK])
        rden = sb("rden", [P, 2, 2])
        att = sb("att", [P, TILES, QUADS, 4 * HD])
        attT = sb("attT", [P, TOK])
        w_turned = sem("w_turned")
        wT_ready = sem("wT_ready")
        ones_set = sem("ones_set")
        xs_ready = sem("xs_ready")
        qkv_ready = sem("qkv_ready")
        qT_ready = sem("qT_ready")
        kv_ready = sem("kv_ready")
        qz_ready = sem("qz_ready")
        scores_ready = sem("scores_ready")
        maxed = sem("maxed")
        exp_ready = sem("exp_ready")
        turned = sem("turned")
        prT_ready = sem("prT_ready")
        out_ready = sem("out_ready")
        out_used = sem("out_used")
        attT_turned = sem("attT_turned")
        attT_ready = sem("attT_ready")
        proj_ready = sem("proj_ready")
        y_ready = sem("y_ready")
        ps = core.ps
        block = ctx.enter_context(nc.Block())

        @block.gpsimd
        def _(pool):
            pool.memset(vals[:], 1.0).then_inc(ones_set, 1)
            pool.sem_inc(qkv_ready, 1)
            pool.sem_inc(scores_ready, STEPS)
            with pool.Fori(0, SEQS) as b:
                pool.wait_ge(qkv_ready, b + 1)
                pool.tensor_copy(xs[:], core.xnT[:, b, :]).then_inc(xs_ready, 1)
                with pool.Fori(0, QUADS) as q:
                    pool.wait_ge(qT_ready, b + 1)
                    for u in range(4):
                        if u % 2 == 0:
                            pool.wait_ge(scores_ready, (b * QUADS + q) * STEPS + 5 * (u // 2 + 1))
                        pool.tensor_tensor(qz[:, u], qT[:], core.t.head8[:, q * 4 + u, :].broadcast_to([P, TOK]), ALU.mult).then_inc(qz_ready, 1)

        @block.tensor
        def _(pe):
            pe.wait_ge(w.loaded, 16 * w.n)
            for n in range(4):
                last = pe.transpose(ps[:, 0, n * P:(n + 1) * P], w.w_qkv[:, n, :] if n < 3 else w.w_out[:], core.ident[:])
            last.then_inc(w_turned, 1)
            pe.wait_ge(wT_ready, 1)
            with pe.Fori(0, SEQS) as b:
                pe.wait_ge(y_ready, b + 1)
                for n in range(2):
                    pe.matmul(ps[:, n, :], wT[:, n, :], core.xnT[:, b, :], start=True, stop=True)
                pe.wait_ge(xs_ready, b + 1)
                for t in range(TILES):
                    last = pe.matmul(ps[:, 2, t * P:(t + 1) * P], xs[:, t * P:(t + 1) * P], wT[:, 2, :], start=True, stop=True)
                last.then_inc(qkv_ready, 1)
                with pe.Fori(0, QUADS) as q:
                    pe.wait_ge(kv_ready, b + 1)
                    base = (b * QUADS + q) * STEPS
                    heads = (b * QUADS + q) * 4

                    def score(i):
                        pair, c = i // 5, i % 2
                        pe.wait_ge(qz_ready, heads + 2 * pair + (1 if i % 5 < 2 else 2))
                        pe.wait_ge(exp_ready, base + i + 1)
                        for h, t, col in SEGS[i % 5]:
                            last = pe.matmul(ps[:, c, col:col + (t + 1) * P], qz[:, 2 * pair + h, t * P:(t + 1) * P],
                                             kT[:, 0:(t + 1) * P], start=True, stop=True)
                        last.then_inc(scores_ready, 1)

                    def turn(i):
                        pe.wait_ge(exp_ready, base + i + 3)
                        pe.wait_ge(prT_ready, base + i + 1)
                        for k in range(TILES):
                            last = pe.transpose(ps[:, 2 + i % 2, k * P:(k + 1) * P], pr[:, i % 2, k * P:(k + 1) * P], core.ident[:])
                        last.then_inc(turned, 1)

                    def values(i):
                        pe.wait_ge(prT_ready, base + i + 3)
                        pe.wait_ge(out_used, base + i + 1)
                        for s, (h, t, col) in enumerate(SEGS[i % 5]):
                            for k in range(t + 1):
                                last = pe.matmul(ps[:, 4 + i % 2, s * VW:(s + 1) * VW], prT[:, i % 2, col + k * P:col + (k + 1) * P],
                                                 vals[:, k, q * 4 + 2 * (i // 5) + h, :], start=(k == 0), stop=(k == t))
                        last.then_inc(out_ready, 1)

                    score(0)
                    for i in range(STEPS):
                        if i + 1 < STEPS:
                            score(i + 1)
                        turn(i)
                        if i:
                            values(i - 1)
                    values(STEPS - 1)
                pe.wait_ge(out_used, (b + 1) * QUADS * STEPS + 2)
                for t in range(TILES):
                    last = pe.transpose(ps[:, 6, t * P:(t + 1) * P], att[:, t].rearrange("p q c -> p (q c)"), core.ident[:])
                last.then_inc(attT_turned, 1)
                pe.wait_ge(attT_ready, b + 1)
                for t in range(TILES):
                    last = pe.matmul(ps[:, 7, t * P:(t + 1) * P], attT[:, t * P:(t + 1) * P], wT[:, 3, :], start=True, stop=True)
                last.then_inc(proj_ready, 1)

        @block.scalar
        def _(act):
            act.wait_ge(w_turned, 1)
            act.copy(wT[:], ps[:, 0, :].rearrange("p (n c) -> p n c", n=4)).then_inc(wT_ready, 1)
            act.wait_ge(ones_set, 1)
            act.sem_inc(exp_ready, 2)
            act.sem_inc(prT_ready, 2)
            with act.Fori(0, SEQS) as b:
                act.wait_ge(qkv_ready, b + 2)
                act.activation(qT[:], ps[:, 0, :], ACT.Copy, scale=float(HD) ** -0.5).then_inc(qT_ready, 1)
                act.copy(kT[:], ps[:, 1, :])
                act.copy(vals[:, :, :, 0:HD].rearrange("p t h d -> p (t h) d"),
                         ps[:, 2, :].rearrange("p (t h d) -> p (t h) d", t=TILES, d=HD)).then_inc(kv_ready, 1)
                with act.Fori(0, QUADS) as q:
                    base = (b * QUADS + q) * STEPS
                    for i in range(STEPS):
                        c = i % 2
                        segs = SEGS[i % 5]
                        act.wait_ge(maxed, base + i + 1)
                        for s, (h, t, col) in enumerate(segs):
                            last = act.activation(pr[:, c, col:col + (t + 1) * P], ps[:, c, col:col + (t + 1) * P], ACT.Exp,
                                                  bias=top[:, c, s:s + 1])
                        last.then_inc(exp_ready, 1)
                        act.wait_ge(turned, base + i + 1)
                        act.copy(prT[:, c], ps[:, 2 + c, :]).then_inc(prT_ready, 1)
                act.wait_ge(attT_turned, b + 1)
                act.copy(attT[:], ps[:, 6, :]).then_inc(attT_ready, 1)
                act.wait_ge(proj_ready, b + 1)
                act.copy(core.y[:, b], ps[:, 7, :].rearrange("p (t d) -> p t d", t=TILES)).then_inc(y_ready, 1)

        @block.vector
        def _(dve):
            dve.sem_inc(y_ready, 1)
            dve.sem_inc(out_used, 2)
            with dve.Fori(0, SEQS) as b:
                with dve.Fori(0, QUADS) as q:
                    base = (b * QUADS + q) * STEPS

                    def weigh(i):
                        c = i % 2
                        segs = SEGS[i % 5]
                        o = ps[:, 4 + c, 0:len(segs) * VW].rearrange("p (s c) -> p s c", c=VW)
                        dve.wait_ge(out_ready, base + i + 1)
                        dve.reciprocal(rden[:, c, 0:len(segs)], o[:, :, HD])
                        dve.drain()
                        for s, (h, t, _) in enumerate(segs):
                            j = 2 * (i // 5) + h
                            last = dve.tensor_scalar(att[:, t, q, j * HD:(j + 1) * HD], o[:, s, 0:HD], rden[:, c, s:s + 1], None, ALU.mult)
                        last.then_inc(out_used, 1)

                    for i in range(STEPS):
                        c = i % 2
                        d0, nd, step = DIAG[i % 5]
                        dve.wait_ge(scores_ready, base + i + 1 + STEPS)
                        if nd == 1:
                            blk, msk = ps[:, c, d0:d0 + P], core.t.lower_neg[:]
                        else:
                            blk = pair_of_blocks(ps, c, d0, step)
                            msk = core.t.lower_neg[:].unsqueeze(1).broadcast_to([P, 2, P])
                        dve.tensor_tensor(blk, blk, msk, ALU.add)
                        dve.drain()
                        for s, (h, t, col) in enumerate(SEGS[i % 5]):
                            last = dve.tensor_reduce(top[:, c, s:s + 1], ps[:, c, col:col + (t + 1) * P], AX_X, ALU.max, negate=True)
                        last.then_inc(maxed, 1)
                        if i:
                            weigh(i - 1)
                    weigh(STEPS - 1)


def local_transformer(core, w):
    nc = core.nc
    LAYERS, HEADS, HD, WIN = 6, 16, 64, 32
    PAIRS, INNER, KEYS = HEADS // 2, HEADS * HD, 2 * WIN
    HID, CH = 341, 3
    QK_SCALE = 8.0
    NORM_SCALE = 2.0 ** 18
    NORM_FLOOR = 1e-24
    with ExitStack() as ctx:
        def sb(n, shape, dt=F32):
            return ctx.enter_context(nc.sbuf_tensor(f"lt_{n}", shape, dt))

        def sem(n):
            return core.sem(f"lt_{n}")

        zs = sb("zs", [P, TILES, D])
        zb = sb("zb", [P, TILES, D])
        xsT = sb("xsT", [P, WIN + TOK])
        rope = sb("rope", [P, 4, TILES, HD])
        rot = sb("rot", [P, 2, INNER])
        sq = rot
        ss = sb("ss", [P, 2, HEADS])
        logs = sb("logs", [P, 2, HEADS])
        rr = sb("rr", [P, 2, HEADS])
        qa = core.xnT[:].rearrange("p b t -> p (b t)").rearrange("p (c n) -> p c n", c=2)
        qb = sb("qb", [P, 2, INNER])
        qT = sb("qT", [P, PAIRS, P])
        kT = sb("kT", [P, PAIRS, WIN + TOK])
        pr = sb("pr", [P, HEADS, KEYS])
        top = sb("top", [P, 3, HEADS])
        prT = sb("prT", [P, PAIRS, P])
        vals = sb("vals", [P, 4, PAIRS, HD])
        att = sb("att", [P, HEADS, HD])
        attT = sb("attT", [P, PAIRS, P])
        st = sb("st", [P, TILES, 6])
        mv = sb("mv", [P, TILES, 2])
        sd = sb("sd", [P, 3, TILES])
        nrm = sb("nrm", [P, TILES, D])
        fT = sb("fT", [P, TOK])
        gl = sb("gl", [P, 2, TOK])
        hid = sb("hid", [P, CH, TOK])
        cols = sb("cols", [P, 8, LAYERS, 1])
        names = """cols_turned cols_ready zeroed zs_ready z_turned xs_low xs_high q_psum k_psum v_psum s_psum prT_turned
                   o_psum q_turned k_turned att_turned y_psum sq_ready rr_ready exp_ready v_ready prT_ready qT_ready
                   kT_ready attT_ready ss_ready qa_ready shifted att_ready z_ready rot_ready f_turned f_low f_high back_turned
                   var_ready rstd_ready nrm_ready fn_turned fT_ready gu_psum gelu_ready hid_ready down_psum seq_done
                   layer_done""".split()
        S = namedtuple("Semaphores", names)(*[sem(n) for n in names])
        ps = core.ps
        flat = "p a b -> p (a b)"
        heads = "p (h c) -> p h c"
        by_parity = "p (a o) c -> p o a c"
        block = ctx.enter_context(nc.Block())

        def each_layer(eng, body):
            with eng.Fori(0, LAYERS // 2) as lp:
                for s in range(2):
                    body(lp * 2 + s, s, lp)

        @block.sync
        def _(sync):
            with sync.Fori(0, LAYERS // 2 - 1) as lp:
                for s in range(2):
                    sync.wait_ge(S.layer_done, lp * 2 + s + 1)
                    for dst, src in w.layer_loads(s, lp * 2 + 2 + s):
                        sync.dma_start(dst, src).then_inc(w.layer_loaded[s], 16)

        @block.gpsimd
        def _(pool):
            def layer(l, s, lp):
                with pool.Fori(0, SEQS) as b:
                    q = l * SEQS + b
                    pool.wait_ge(S.seq_done, q + 1)
                    pool.tensor_copy(zs[:], core.y[:, b]).then_inc(S.zs_ready, 1)
                    for t in range(TILES):
                        n = q * TILES + t
                        for c in range(2):
                            pool.wait_ge(S.qa_ready, n * 2 + c + 1)
                            pool.tensor_tensor(qb[:, c], qa[:, c], qb[:, c], ALU.add)
                            pool.drain()
                            pool.wait_ge(S.rr_ready, n * 2 + c + 1)
                            pool.tensor_tensor(rot[:, c].rearrange(heads, c=HD), qb[:, c].rearrange(heads, c=HD),
                                               rr[:, c].unsqueeze(2).broadcast_to([P, HEADS, HD]), ALU.mult).then_inc(S.rot_ready, 1)

            pool.memset(xsT[:, 0:WIN + 1], 0.0)
            pool.memset(kT[:, :, 0:WIN], 0.0).then_inc(S.zeroed, 1)
            pool.sem_inc(S.seq_done, 1)
            each_layer(pool, layer)

        @block.tensor
        def _(pe):
            pe.wait_ge(w.loaded, 16 * w.n)
            for c in range(8):
                src = w.rows[0:LAYERS, c, :]
                last = pe.transpose(ps[:, 0, c * LAYERS:(c + 1) * LAYERS], src, core.ident[0:LAYERS, 0:LAYERS])
            last.then_inc(S.cols_turned, 1)
            pe.wait_ge(S.cols_ready, 1)
            pe.wait_ge(S.zeroed, 1)

            def layer(l, s, lp):
                W = w.bufs[s]

                def project(n, t, banks):
                    for c in banks:
                        last = pe.matmul(ps[:, c, :], xsT[:, WIN + t * P:WIN + (t + 1) * P],
                                         W.qkv[:, c * BANK:(c + 1) * BANK], start=True, stop=True)
                        if c % 2:
                            last.then_inc((S.q_psum, S.k_psum)[c // 2], 1)

                def turn_qk(n):
                    for c, done in enumerate((S.q_turned, S.k_turned)):
                        pe.wait_ge(S.rot_ready, n * 2 + c + 1)
                        for p in range(PAIRS):
                            last = pe.transpose(ps[:, 2 * c + p // 4, (p % 4) * P:(p % 4 + 1) * P], rot[:, c, p * P:(p + 1) * P], core.ident[:])
                        last.then_inc(done, 1)

                def qk_transposed(n):
                    pe.wait_ge(S.qT_ready, n + 1)
                    pe.wait_ge(S.kT_ready, n + 1)

                def window_values(n, t, v, before_last=None):
                    if t and v == 0:
                        pe.wait_ge(S.z_ready, n)
                    if v >= 2:
                        pe.wait_ge(S.v_ready, n * 4 + v - 1)
                    k0 = t * P + v * WIN
                    for odd in range(2):
                        if odd and before_last:
                            before_last(n)
                        last = pe.matmul(ps[64 * odd:64 * odd + 64, 6 + v % 2, :], xsT[:, k0:k0 + KEYS],
                                         W.qkv[:, 2 * INNER:].rearrange("p (a o c) -> p a o c", o=2, c=HD)[:, :, odd, :],
                                         start=True, stop=True)
                    last.then_inc(S.v_psum, 1)

                def scores(n, t):
                    for h in range(HEADS):
                        r = slice(64 * (h % 2), 64 * (h % 2) + 64)
                        for v in range(4):
                            k0 = t * P + v * WIN
                            last = pe.matmul(ps[32 * v:32 * v + 32, 4 + h % 2, (h // 2) * KEYS:(h // 2 + 1) * KEYS],
                                             qT[r, h // 2, v * WIN:(v + 1) * WIN], kT[r, h // 2, k0:k0 + KEYS],
                                             start=True, stop=True)
                    last.then_inc(S.s_psum, 1)

                def weigh_values(n):
                    for h in range(HEADS):
                        r = slice(64 * (h % 2), 64 * (h % 2) + 64)
                        for v in range(4):
                            last = pe.matmul(ps[32 * v:32 * v + 32, 6 + h % 2, (h // 2) * HD:(h // 2 + 1) * HD],
                                             prT[r, h // 2, v * WIN:(v + 1) * WIN], vals[r, v, h // 2, :], start=True, stop=True)
                    last.then_inc(S.o_psum, 1)

                def project_out(n):
                    pe.wait_ge(S.attT_ready, n + 1)
                    for p in range(PAIRS):
                        last = pe.matmul(ps[:, 6, 0:D], attT[:, p], W.wo[:, p, :], start=(p == 0), stop=(p == PAIRS - 1))
                    last.then_inc(S.y_psum, 1)

                def ready_to_weigh(n):
                    pe.wait_ge(S.prT_ready, n + 1)
                    pe.wait_ge(S.v_ready, n * 4 + 4)

                with pe.Fori(0, SEQS) as b:
                    q = l * SEQS + b
                    pe.wait_ge(w.layer_loaded[s], (lp + 1) * 16 * w.n_layer)
                    pe.wait_ge(S.seq_done, q + 1)
                    pe.wait_ge(S.zs_ready, q + 1)
                    for t in range(TILES):
                        last = pe.transpose(ps[:, 4, t * P:(t + 1) * P], zs[:, t], core.ident[:])
                    last.then_inc(S.z_turned, 1)
                    pe.wait_ge(S.xs_low, q + 1)
                    pe.wait_ge(S.xs_high, q + 1)
                    n = q * TILES
                    project(n, 0, range(4))
                    for v in range(3):
                        window_values(n, 0, v)
                    turn_qk(n)
                    window_values(n, 0, 3, before_last=qk_transposed)
                    for t in range(TILES):
                        n = q * TILES + t
                        scores(n, t)
                        if t:
                            project_out(n - 1)
                        if t + 1 < TILES:
                            project(n + 1, t + 1, range(3))
                        if t:
                            for v in range(4):
                                window_values(n, t, v)
                        pe.wait_ge(S.exp_ready, n + 1)
                        for p in range(PAIRS):
                            last = pe.transpose(ps[:, 4 + p // 4, (p % 4) * P:(p % 4 + 1) * P],
                                                pr[:, 2 * p:2 * p + 2, :].rearrange("p h k -> p (h k)"), core.ident[:])
                        last.then_inc(S.prT_turned, 1)
                        if t + 1 < TILES:
                            ready_to_weigh(n)
                            project(n + 1, t + 1, [3])
                        else:
                            pe.transpose(ps[:, 0, 0:P], zs[:, 0], core.ident[:])
                            ready_to_weigh(n)
                            pe.transpose(ps[:, 0, P:2 * P], zs[:, 1], core.ident[:])
                        weigh_values(n)
                        if t + 1 < TILES:
                            turn_qk(n + 1)
                        pe.wait_ge(S.att_ready, n + 1)
                        for p in range(PAIRS):
                            if p == PAIRS - 1 and t + 1 < TILES:
                                qk_transposed(n + 1)
                            last = pe.transpose(ps[:, 6 + p // 4, (p % 4) * P:(p % 4 + 1) * P],
                                                att[:, 2 * p:2 * p + 2, :].rearrange("p h k -> p (h k)"), core.ident[:])
                        last.then_inc(S.att_turned, 1)
                    project_out(q * TILES + TILES - 1)
                    pe.wait_ge(S.z_ready, (q + 1) * TILES)
                    for t in range(2, TILES):
                        last = pe.transpose(ps[:, 0, t * P:(t + 1) * P], zs[:, t], core.ident[:])
                    last.then_inc(S.f_turned, 1)
                    pe.wait_ge(S.f_low, q + 1)
                    pe.wait_ge(S.f_high, q + 1)
                    for t in range(TILES):
                        last = pe.transpose(ps[:, 1, t * P:(t + 1) * P], xsT[:, WIN + t * P:WIN + (t + 1) * P], core.ident[:])
                    last.then_inc(S.back_turned, 1)
                    pe.wait_ge(S.nrm_ready, q + 1)
                    for t in range(TILES):
                        last = pe.transpose(ps[:, 2, t * P:(t + 1) * P], nrm[:, t], core.ident[:])
                    last.then_inc(S.fn_turned, 1)
                    pe.wait_ge(S.fT_ready, q + 1)
                    for c in range(CH):
                        if c == 2:
                            pe.wait_ge(S.hid_ready, q * CH + 1)
                        for g in range(2):
                            last = pe.matmul(ps[:, 3 + 2 * g + c % 2, :], W.w1[:, 1 - g, c * P:(c + 1) * P], fT[:], start=True, stop=True)
                        last.then_inc(S.gu_psum, 1)
                    pe.wait_ge(S.hid_ready, (q + 1) * CH)
                    for t in range(TILES):
                        for c in range(CH):
                            last = pe.matmul(ps[:, 7, t * P:(t + 1) * P], hid[:, c, t * P:(t + 1) * P], W.w2[:, c, :],
                                             start=(c == 0), stop=(c == CH - 1))
                    last.then_inc(S.down_psum, 1)

            each_layer(pe, layer)

        @block.scalar
        def _(act):
            act.wait_ge(S.cols_turned, 1)
            act.copy(cols[:].rearrange("p c l a -> p (c l a)"), ps[:, 0, 0:8 * LAYERS]).then_inc(S.cols_ready, 1)

            def layer(l, s, lp):
                def squares(n, c):
                    act.wait_ge((S.q_psum, S.k_psum)[c], n + 1)
                    act.activation(sq[:, c], ps[:, 2 * c:2 * c + 2, :].rearrange(flat), ACT.Square).then_inc(S.sq_ready, 1)

                def inverse_norms(n, c):
                    act.wait_ge(S.ss_ready, n * 2 + c + 1)
                    inverse_sqrt(act, rr[:, c], ss[:, c], logs[:, c], scale=NORM_SCALE).then_inc(S.rr_ready, 1)

                def window_values(n):
                    for v in range(4):
                        act.wait_ge(S.v_psum, n * 4 + v + 1)
                        act.copy(vals[:, v], ps[:, 6 + v % 2, :].rearrange("p (a c) -> p a c", c=HD)).then_inc(S.v_ready, 1)

                def evacuate_qk(n, t):
                    act.wait_ge(S.q_turned, n + 1)
                    act.copy(qT[:], ps[:, 0:2, :].rearrange("p a (b c) -> p (a b) c", c=P)).then_inc(S.qT_ready, 1)
                    act.wait_ge(S.k_turned, n + 1)
                    act.copy(kT[:, :, WIN + t * P:WIN + (t + 1) * P],
                             ps[:, 2:4, :].rearrange("p a (b c) -> p (a b) c", c=P)).then_inc(S.kT_ready, 1)

                with act.Fori(0, SEQS) as b:
                    q = l * SEQS + b
                    act.wait_ge(S.z_turned, q + 1)
                    act.copy(xsT[0:64, WIN:], ps[0:64, 4, :]).then_inc(S.xs_low, 1)
                    for c in range(2):
                        squares(q * TILES, c)
                    for c in range(2):
                        inverse_norms(q * TILES, c)
                    for v in range(3):
                        act.wait_ge(S.v_psum, q * TILES * 4 + v + 1)
                        act.copy(vals[:, v], ps[:, 6 + v % 2, :].rearrange("p (a c) -> p a c", c=HD)).then_inc(S.v_ready, 1)
                    evacuate_qk(q * TILES, 0)
                    act.wait_ge(S.v_psum, q * TILES * 4 + 4)
                    act.copy(vals[:, 3], ps[:, 7, :].rearrange("p (a c) -> p a c", c=HD)).then_inc(S.v_ready, 1)
                    for t in range(TILES):
                        n = q * TILES + t
                        if t + 1 < TILES:
                            squares(n + 1, 0)
                        act.wait_ge(S.shifted, n + 1)
                        act.activation(pr[:], pr[:], ACT.Exp, scale=QK_SCALE).then_inc(S.exp_ready, 1)
                        if t:
                            window_values(n)
                        if t + 1 < TILES:
                            inverse_norms(n + 1, 0)
                        act.wait_ge(S.prT_turned, n + 1)
                        act.copy(prT[:], ps[:, 4:6, :].rearrange("p a (b c) -> p (a b) c", c=P)).then_inc(S.prT_ready, 1)
                        if t + 1 < TILES:
                            squares(n + 1, 1)
                            inverse_norms(n + 1, 1)
                            evacuate_qk(n + 1, t + 1)
                        act.wait_ge(S.att_turned, n + 1)
                        act.copy(attT[:], ps[:, 6:8, :].rearrange("p a (b c) -> p (a b) c", c=P)).then_inc(S.attT_ready, 1)
                    act.wait_ge(S.f_turned, q + 1)
                    act.copy(xsT[0:64, WIN:], ps[0:64, 0, :]).then_inc(S.f_low, 1)
                    act.wait_ge(S.var_ready, q + 1)
                    inverse_sqrt(act, sd[:, 2], sd[:, 0], sd[:, 1]).then_inc(S.rstd_ready, 1)
                    act.wait_ge(S.fn_turned, q + 1)
                    act.activation(fT[:], ps[:, 2, :], ACT.Identity, bias=cols[:, 7, l, :], scale=cols[:, 6, l, :]).then_inc(S.fT_ready, 1)
                    for c in range(CH):
                        act.wait_ge(S.gu_psum, q * CH + c + 1)
                        if c == 2:
                            act.wait_ge(S.hid_ready, q * CH + 1)
                        act.activation(gl[:, c % 2], ps[:, 3 + c % 2, :], ACT.Gelu, bias=cols[:, 3 + c, l, :]).then_inc(S.gelu_ready, 1)

            each_layer(act, layer)

        @block.vector
        def _(dve):
            dve.wait_ge(S.zeroed, 1)
            dve.wait_ge(S.cols_ready, 1)

            def layer(l, s, lp):
                dve.wait_ge(w.layer_loaded[s], (lp + 1) * 16 * w.n_layer)
                for c in range(2):
                    gain = w.bufs[s].gains[:, c, :]
                    dve.tensor_tensor(rope[:, 2 * c], core.t.rope64[:, 2 * c], gain.unsqueeze(1).broadcast_to([P, TILES, HD]), ALU.mult)
                    for half in range(2):
                        a, z = slice(32 * half, 32 * half + 32), slice(32 - 32 * half, 64 - 32 * half)
                        dve.tensor_tensor(rope[:, 2 * c + 1, :, a], core.t.rope64[:, 2 * c + 1, :, a],
                                          gain[:, z].unsqueeze(1).broadcast_to([P, TILES, 32]), ALU.mult)
                dve.drain()

                def rotate(n, t, c):
                    dve.wait_ge(S.sq_ready, n * 2 + c + 1)
                    dve.tensor_reduce(ss[:, c], sq[:, c].rearrange(heads, c=HD), AX_X, ALU.add)
                    dve.drain()
                    dve.tensor_scalar(ss[:, c], ss[:, c], NORM_FLOOR, None, ALU.max).then_inc(S.ss_ready, 1)
                    src = ps[:, 2 * c:2 * c + 2, :].rearrange("p a (h c) -> p (a h) c", c=HD)
                    dve.tensor_tensor(qa[:, c].rearrange(heads, c=HD), src,
                                      rope[:, 2 * c, t].unsqueeze(1).broadcast_to([P, HEADS, HD]), ALU.mult)
                    for half in range(2):
                        a, z = slice(32 * half, 32 * half + 32), slice(32 - 32 * half, 64 - 32 * half)
                        last = dve.tensor_tensor(qb[:, c].rearrange(heads, c=HD)[:, :, a], src[:, :, z],
                                                 rope[:, 2 * c + 1, t, a].unsqueeze(1).broadcast_to([P, HEADS, 32]), ALU.mult)
                    last.then_inc(S.qa_ready, 1)

                with dve.Fori(0, SEQS) as b:
                    q = l * SEQS + b

                    def add_output(t):
                        dve.wait_ge(S.y_psum, q * TILES + t + 1)
                        dve.tensor_tensor(zs[:, t], ps[:, 6, 0:D], zs[:, t], ALU.add).then_inc(S.z_ready, 1)

                    dve.wait_ge(S.z_turned, q + 1)
                    dve.tensor_copy(xsT[64:128, WIN + 1:], ps[64:128, 4, 0:TOK - 1]).then_inc(S.xs_high, 1)
                    rotate(q * TILES, 0, 0)
                    rotate(q * TILES, 0, 1)
                    for t in range(TILES):
                        n = q * TILES + t
                        dve.wait_ge(S.s_psum, n + 1)
                        for odd in range(2):
                            dve.tensor_tensor(pr[:].rearrange(by_parity, o=2)[:, odd], ps[:, 4 + odd, :].rearrange(heads, c=KEYS),
                                              core.t.window[:, min(t, 1), :].unsqueeze(1).broadcast_to([P, PAIRS, KEYS]), ALU.add)
                        dve.drain()
                        dve.tensor_reduce(top[:, 0], pr[:], AX_X, ALU.max)
                        dve.drain()
                        dve.tensor_tensor(pr[:], pr[:], top[:, 0].unsqueeze(2).broadcast_to([P, HEADS, KEYS]),
                                          ALU.subtract).then_inc(S.shifted, 1)
                        if t:
                            add_output(t - 1)
                        if t + 1 < TILES:
                            rotate(n + 1, t + 1, 0)
                        dve.wait_ge(S.exp_ready, n + 1)
                        dve.tensor_reduce(top[:, 1], pr[:], AX_X, ALU.add)
                        dve.drain()
                        dve.reciprocal(top[:, 2], top[:, 1])
                        if t + 1 < TILES:
                            rotate(n + 1, t + 1, 1)
                        else:
                            dve.drain()
                        dve.wait_ge(S.o_psum, n + 1)
                        for odd in range(2):
                            last = dve.tensor_tensor(att[:].rearrange(by_parity, o=2)[:, odd], ps[:, 6 + odd, :].rearrange(heads, c=HD),
                                                     top[:, 2].rearrange("p (a o) -> p o a", o=2)[:, odd].unsqueeze(2)
                                                     .broadcast_to([P, PAIRS, HD]), ALU.mult)
                        last.then_inc(S.att_ready, 1)
                    add_output(TILES - 1)
                    dve.wait_ge(S.f_turned, q + 1)
                    dve.tensor_copy(xsT[64:128, WIN + 1:], ps[64:128, 0, 0:TOK - 1]).then_inc(S.f_high, 1)
                    dve.tensor_tensor(zb[:], zs[:], w.bufs[s].b2[:].unsqueeze(1).broadcast_to([P, TILES, D]), ALU.add)
                    dve.wait_ge(S.back_turned, q + 1)
                    for t in range(TILES):
                        dve.bn_stats(st[:, t], ps[:, 1, t * P:(t + 1) * P])
                    dve.drain()
                    for t in range(TILES):
                        dve.bn_aggr(mv[:, t], st[:, t])
                    dve.drain()
                    dve.tensor_scalar(sd[:, 0], mv[:, :, 1], LN_EPS, None, ALU.add).then_inc(S.var_ready, 1)
                    dve.wait_ge(S.rstd_ready, q + 1)
                    for t in range(TILES):
                        last = dve.tensor_scalar(nrm[:, t], ps[:, 1, t * P:(t + 1) * P], mv[:, t, 0:1], sd[:, 2, t:t + 1],
                                                 ALU.subtract, ALU.mult)
                    last.then_inc(S.nrm_ready, 1)
                    for c in range(CH):
                        dve.wait_ge(S.gelu_ready, q * CH + c + 1)
                        dve.scalar_tensor_tensor(out=hid[:, c], in0=ps[:, 5 + c % 2, :], scalar=cols[:, c, l, :], in1=gl[:, c % 2],
                                                 op0=ALU.add, op1=ALU.mult).then_inc(S.hid_ready, 1)
                    dve.wait_ge(S.down_psum, q + 1)
                    dve.tensor_tensor(core.y[:, b], ps[:, 7, :].rearrange("p (t d) -> p t d", t=TILES), zb[:], ALU.add).then_inc(S.seq_done, 1)
                dve.drain()
                dve.sem_inc(S.layer_done, 1)

            each_layer(dve, layer)


def weights_diff_attention(w, ins, sb):
    w.Wq, w.Wk, w.Wv, w.Wproj = (sb(n, [P, P]) for n in ("Wq", "Wk", "Wv", "Wproj"))
    w.lam = sb("lam", [P, 4, 4])
    parts = [(dst[:], ins[f"L0_attn_{n}"]) for n, dst in (("Wq", w.Wq), ("Wk", w.Wk), ("Wv", w.Wv), ("Wproj", w.Wproj))]
    for n, v in enumerate(("lambda_q1", "lambda_k1", "lambda_q2", "lambda_k2")):
        parts.append((w.lam[:, n, :], ins[f"L0_attn_{v}"].rearrange("(a n) -> a n", a=1).broadcast_to([P, 4])))
    return parts


def weights_gated_ffn(w, ins, sb):
    w.gate, w.up, w.down = (sb(n, [P, 3, P], I32) for n in ("gate", "up", "down"))
    return [(w.gate[:], ins["L0_ffn_w_gate"].rearrange("(c p) d -> p c d", p=P)),
            (w.up[:], ins["L0_ffn_w_up"].rearrange("(c p) d -> p c d", p=P)),
            (w.down[:], ins["L0_ffn_w_down"].rearrange("p (c h) -> p c h", h=P))]


def weights_band_attention(w, ins, sb):
    w.WQ, w.WK, w.WV = (sb(n, [P, P]) for n in ("WQ", "WK", "WV"))
    return [(w.WQ[:], ins["L1_attn_WQ"]), (w.WK[:], ins["L1_attn_WK"]), (w.WV[:], ins["L1_attn_WV"])]


def weights_shared_expert_ffn(w, ins, sb):
    w.W_shared, w.W_expert, w.bias = (sb(n, [P, P]) for n in ("W_shared", "W_expert", "bias"))
    w.W_gate = sb("W_gate", [P, 7])
    return [(w.W_shared[:], ins["L1_ffn_W_shared"]), (w.W_expert[:], ins["L1_ffn_W_expert"]),
            (w.W_gate[:], ins["L1_ffn_W_gate"]),
            (w.bias[:], ins["L1_ffn_bias"].rearrange("(a n) -> a n", a=1).broadcast_to([P, P]))]


def weights_linear_attention(w, ins, sb):
    w.w_qkv, w.w_gate, w.w_out = sb("w_qkv", [P, 3072]), sb("w_gate", [P, 1024]), sb("w_out", [P, 8, P])
    return [(w.w_qkv[:], ins["L2_attn_w_qkv"]), (w.w_gate[:], ins["L2_attn_w_gate"]),
            (w.w_out[:], ins["L2_attn_w_out"].rearrange("(c p) d -> p c d", p=P))]


def weights_expert_ffn(w, ins, sb):
    w.router, w.gating, w.up = sb("router", [P, 8]), sb("gating", [P, 8, 256]), sb("up", [P, 8, 256])
    w.down = sb("down", [P, 8, 2, P])
    return [(w.router[:], ins["L2_ffn_router_kernel_DE"]),
            (w.gating[:], ins["L2_ffn_kernel_gating_EDF"].rearrange("e d f -> d e f")),
            (w.up[:], ins["L2_ffn_kernel_up_EDF"].rearrange("e d f -> d e f")),
            (w.down[:].rearrange("p e c d -> p (e c) d"), ins["L2_ffn_kernel_down_EFD"].rearrange("e (c p) d -> p (e c) d", p=P))]


def weights_causal_attention(w, ins, sb):
    w.w_qkv, w.w_out = sb("w_qkv", [P, 3, P]), sb("w_out", [P, P])
    return [(w.w_qkv[:], ins["L3_attn_w_qkv"].rearrange("(c p) d -> p c d", p=P)), (w.w_out[:], ins["L3_attn_w_out"])]


def weights_local_transformer(w, ins, sb):
    HID, INNER = 341, 1024
    w.bufs = []
    for s in range(2):
        b = Shared()
        b.qkv, b.wo = sb(f"qkv{s}", [P, 3 * INNER]), sb(f"wo{s}", [P, 8, P])
        b.w1, b.w2 = sb(f"w1_{s}", [P, 2, 3 * P]), sb(f"w2_{s}", [P, 3, P])
        b.b2, b.gains = sb(f"b2_{s}", [P, D]), sb(f"gains{s}", [P, 2, 64])
        w.bufs.append(b)
    w.rows = sb("rows", [6, 8, P])
    get = {n: ins[f"L3_ffn_{n}"] for n in ("Wqkv", "Wo", "W1", "W2", "b1", "b2", "ln_g", "ln_b", "q_scale", "k_scale")}
    w.padded = [b.w1 for b in w.bufs] + [b.w2 for b in w.bufs] + [w.rows]

    def layer_loads(s, l):
        b = w.bufs[s]
        return [(b.qkv[:], get["Wqkv"][l]),
                (b.wo[:], get["Wo"][l].rearrange("(c p) d -> p c d", p=P)),
                (b.w1[:, :, 0:HID], get["W1"][l].rearrange("d (a h) -> d a h", a=2)),
                (b.w2[:, 0:2, :], get["W2"][l][0:2 * P].rearrange("(c p) d -> p c d", p=P)),
                (b.w2[0:HID - 2 * P, 2, :], get["W2"][l][2 * P:HID]),
                (b.b2[:], get["b2"][l].rearrange("(a n) -> a n", a=1).broadcast_to([P, D])),
                (b.gains[:, 0], get["q_scale"][l].rearrange("(a n) -> a n", a=1).broadcast_to([P, 64])),
                (b.gains[:, 1], get["k_scale"][l].rearrange("(a n) -> a n", a=1).broadcast_to([P, 64]))]

    w.layer_loads = layer_loads
    w.n_layer = len(layer_loads(0, 0))
    w.first_layers = [layer_loads(s, s) for s in range(2)]
    rows = w.rows[:].rearrange("l c p -> l (c p)")
    return [(rows[:, 0:HID], get["b1"][:, 0:HID]), (rows[:, 3 * P:3 * P + HID], get["b1"][:, HID:]),
            (w.rows[:, 6, :], get["ln_g"]), (w.rows[:, 7, :], get["ln_b"])]


SUBLAYERS = [diff_attention, gated_ffn, band_attention, shared_expert_ffn, linear_attention, expert_ffn, causal_attention, local_transformer]
WEIGHTS = [weights_diff_attention, weights_gated_ffn, weights_band_attention, weights_shared_expert_ffn, weights_linear_attention, weights_expert_ffn, weights_causal_attention, weights_local_transformer]
UNUSED = ("L1_ffn_cond", "L1_ffn_mask")
PHASES = (0, 1, 2, 3, 4, 5, 6, 7)


def tables():
    f = np.float32
    pos = np.arange(TOK)
    out = {"ident": np.eye(P, dtype=f)}
    inv = (1.0 / np.power(f(10000.0), np.arange(0, 8, 2, dtype=f) / f(8))).astype(f)
    ang = (pos.astype(f)[:, None] * inv[None, :]).astype(f)
    c, s = np.cos(ang), np.sin(ang)
    rope = np.stack([np.concatenate([c, c], 1), np.concatenate([s, -s], 1)])
    out["rope8"] = rope.reshape(2, TILES, P, 8).transpose(2, 0, 1, 3)
    out["head8"] = np.repeat(np.eye(16, dtype=f), 8, axis=0)[:, :, None]
    out["upper"] = np.triu(np.ones((P, P), f))
    i, j = pos[:, None], pos[None, :]
    width = 64
    band = ((i - j <= width // 2) & (j - i <= (width - 1) // 2)) / np.sqrt(f(D))
    out["band"] = band.reshape(TILES, P, TOK).transpose(1, 0, 2)
    out["count8"] = np.broadcast_to(np.arange(8, dtype=f), (P, TILES, 8))
    out["lower_neg"] = np.triu(np.full((P, P), -1e30, f), 1)
    half = np.arange(0, 64, 2, dtype=f)
    inv = (f(1.0) / np.power(f(10000.0), half / f(64))).astype(f)
    ang = (pos.astype(f)[:, None] * inv[None, :]).astype(f)
    power = (pos.astype(f) - TOK // 2) / f(16)
    scale = np.power(((half + f(0.4 * 64)) / f(1.4 * 64))[None, :], power[:, None]).astype(f)
    c, s = np.cos(ang), np.sin(ang)
    rows = [np.concatenate([g * c, g * c], 1) if not odd else np.concatenate([-g * s, g * s], 1)
            for g in (scale, f(1) / scale) for odd in (0, 1)]
    out["rope64"] = (np.stack(rows) * f(512)).reshape(4, TILES, P, 64).transpose(2, 0, 1, 3)
    i, j = (np.arange(P) % 32)[:, None], np.arange(64)[None, :]
    seen = (j >= i) & (j <= i + 32)
    first = seen & ((j >= 32) | (np.arange(P) >= 32)[:, None])
    out["window"] = np.where(np.stack([first, seen], 1), f(0), f(-1e30))
    return {k: np.ascontiguousarray(v.astype(f)) for k, v in out.items()}


def build(nc, ins, tabs, out, phases=tuple(range(8))):
    with ExitStack() as ctx:
        def sb(n, shape, dt=F32):
            return ctx.enter_context(nc.sbuf_tensor(n, shape, dt))

        def sem(n):
            return ctx.enter_context(nc.semaphore(n))

        core = Shared()
        core.nc = nc
        core.x = sb("x", [P, SEQS, TILES, D])
        core.y = sb("y", [P, SEQS, TILES, D])
        core.xnT = sb("xnT", [P, SEQS, TOK])
        core.bn = sb("bn", [P, ALL_TILES, 6])
        core.small = sb("small", [P, 8, ALL_TILES])
        core.ps = ctx.enter_context(nc.psum_tensor("ps", [P, 8, BANK], F32))
        used = []

        def sublayer_sem(n):
            used.append(nc.alloc_semaphore(name=n))
            return used[-1]

        core.sem = sublayer_sem
        core.norm = Shared()
        core.norm.turns = core.norm.calls = core.norm.adds = 0
        core.norm.var_ready, core.norm.rstd_ready, core.norm.xn_ready = sem("norm_var_ready"), sem("norm_rstd_ready"), sem("norm_xn_ready")
        core.norm.x_ready, core.norm.turned, core.norm.stored = sem("norm_x_ready"), sem("norm_turned"), sem("norm_stored")
        core.x_loaded = sem("x_loaded")
        core.tables_loaded = sem("tables_loaded")
        core.n_tables = len(tabs)
        tiles = []
        loads = []
        for n, a in tabs.items():
            dst = sb(f"t_{n}", list(a.shape))
            loads.append((dst[:], a, core.tables_loaded))
            tiles.append(dst)
        core.t = namedtuple("Tables", list(tabs))(*tiles)
        core.ident = core.t.ident
        weights = {}
        scopes = {}
        for group in ((6, 7), (4, 5), (0, 1, 2, 3)):
            scopes[group] = ctx.enter_context(ExitStack())
            for k in group:
                if k not in phases:
                    continue
                w = Shared()
                w.loaded = sem(f"weights{k}_loaded")
                if k == 7:
                    w.layer_loaded = [sem(f"layer_loaded{s}") for s in range(2)]
                w.parts = WEIGHTS[k](w, ins, lambda n, shape, dt=F32: scopes[group].enter_context(
                    nc.sbuf_tensor(f"w{k}_{n}", shape, dt)))
                w.n = len(w.parts)
                weights[k] = w
        padded = weights[7].padded if 7 in weights else []
        zeros_set = sem("zeros_set")

        with nc.Block() as block:
            @block.gpsimd
            def _(pool):
                for n, buf in enumerate(padded):
                    pool.memset(buf[:], 0.0).then_inc(zeros_set, 1)

            @block.sync
            def _(sync):
                sync.dma_start(core.x[:].rearrange("p b t d -> p (b t) d"),
                               ins["L0_attn_x"].rearrange("b (t p) d -> p (b t) d", p=P)).then_inc(core.x_loaded, 16)
                for dst, src, loaded in loads:
                    sync.dma_start(dst, src).then_inc(loaded, 16)
                for k in phases:
                    w = weights[k]
                    if k == 7:
                        sync.wait_ge(zeros_set, len(padded))
                        for s in range(2):
                            for dst, src in w.first_layers[s]:
                                sync.dma_start(dst, src).then_inc(w.layer_loaded[s], 16)
                    for dst, src in w.parts:
                        sync.dma_start(dst, src).then_inc(w.loaded, 16)

        for n, k in enumerate(phases):
            residual_and_norm(core, first=(n == 0))
            SUBLAYERS[k](core, weights[k])
            nc.clear_and_free_semaphores(used)
            used.clear()
            nc.all_engine_barrier()
            for group, scope in scopes.items():
                if k == max((p for p in phases if p in group), default=None):
                    scope.close()
        residual_and_norm(core, final=out)


def kernel(**inputs):
    import concourse.bacc as bacc
    from concourse.bass_utils import run_bass_kernel_spmd

    nc = bacc.Bacc("TRN2", target_bir_lowering=False, num_devices=1)
    arrays, ins, tabs = {}, {}, {}
    for name, a in inputs.items():
        if name in UNUSED:
            continue
        a = np.ascontiguousarray(a)
        arrays[f"in_{name}"] = a
        ins[name] = nc.dram_tensor(f"in_{name}", a.shape, mybir.dt.from_np(a.dtype), kind="ExternalInput").ap()
    for name, a in tables().items():
        arrays[f"table_{name}"] = a
        tabs[name] = nc.dram_tensor(f"table_{name}", a.shape, F32, kind="ExternalInput").ap()
    out = nc.dram_tensor("out_x", (SEQS, TOK, D), F32, kind="ExternalOutput").ap()
    build(nc, ins, tabs, out, PHASES)
    r = run_bass_kernel_spmd(nc, [arrays], core_ids=[0])
    return r.results[0]["out_x"]
```

```python
from collections import namedtuple
from contextlib import ExitStack

import numpy as np

import concourse.bass as bass
from concourse import mybir

F32 = mybir.dt.float32
I32 = mybir.dt.int32
U32 = mybir.dt.uint32
ALU = mybir.AluOpType
ACT = mybir.ActivationFunctionType
AX_X = mybir.AxisListType.X

P = 128
D = 128
SEQS = 4
TOK = 512
TILES = TOK // P
ALL_TILES = SEQS * TILES
BANK = 512
LN_EPS = 1e-5
LN_EXP = "natural_log_exp_and_others"
GELU = "gelu_and_others"


class Shared:
    pass


def normalise_rows(core, dve, src, dst, sems, turn):
    st, sm = core.bn, core.small
    with dve.Fori(0, SEQS) as g:
        for u in range(4):
            dve.bn_stats(st[:, g * 4 + u, :], src[:, g, u, :])
    dve.drain()
    dve.tensor_tensor(sm[:, 0], st[:, :, 1], st[:, :, 4], ALU.add)
    dve.tensor_tensor(sm[:, 1], st[:, :, 1], st[:, :, 4], ALU.subtract)
    dve.tensor_tensor(sm[:, 2], st[:, :, 2], st[:, :, 5], ALU.add)
    dve.drain()
    dve.tensor_scalar(sm[:, 3], sm[:, 0], 0.5, None, ALU.mult)
    dve.tensor_tensor(sm[:, 4], sm[:, 1], sm[:, 1], ALU.mult)
    dve.tensor_scalar(sm[:, 5], sm[:, 2], 1.0 / D, LN_EPS, ALU.mult, ALU.add)
    dve.drain()
    dve.scalar_tensor_tensor(out=sm[:, 6], in0=sm[:, 4], scalar=0.25, in1=sm[:, 5],
                             op0=ALU.mult, op1=ALU.add).then_inc(sems.var_ready, 1)
    dve.wait_ge(sems.rstd_ready, turn + 1)
    for g in range(SEQS):
        for t in range(TILES):
            n = TILES * g + t
            last = dve.tensor_scalar(dst[:, g, t, :], src[:, g, t, :], sm[:, 3, n:n + 1], sm[:, 7, n:n + 1],
                                     ALU.subtract, ALU.mult)
        if turn == sems.last_turn:
            last.then_inc(sems.xn_ready, 1)


def residual_and_norm(core, first=False, final=None):
    nc = core.nc
    turns = (0 if first else 1) + (1 if final is None else 0)
    with ExitStack() as ctx:
        sems = core.norm
        t0, c0 = sems.turns, sems.calls
        sems.turns += turns
        sems.calls += 1 if final is None else 0
        sems.last_turn = t0 + turns - 1 if final is None else -1
        x_ready, turned, stored = sems.x_ready, sems.turned, sems.stored
        x0 = sems.adds * SEQS
        sems.adds += 0 if first else 1
        block = ctx.enter_context(nc.Block())

        @block.sync
        def _(sync):
            if final is not None:
                for b in range(SEQS):
                    sync.wait_ge(x_ready, x0 + b + 1)
                    sync.dma_start(final[b].rearrange("(t p) d -> p t d", p=P),
                                   core.x[:, b]).then_inc(stored, 16)
                sync.wait_ge(stored, 16 * SEQS)

        @block.vector
        def _(dve):
            turn = t0
            if first:
                dve.wait_ge(core.x_loaded, 16)
                dve.wait_ge(core.tables_loaded, 16 * core.n_tables)
            else:
                normalise_rows(core, dve, core.y, core.y, sems, turn)
                turn += 1
                dve.drain()
                for b in range(SEQS):
                    dve.tensor_tensor(core.x[:, b], core.x[:, b], core.y[:, b], ALU.add).then_inc(x_ready, 1)
                dve.drain()
            if final is None:
                normalise_rows(core, dve, core.x, core.y, sems, turn)

        @block.tensor
        def _(pe):
            if final is None:
                if first:
                    pe.wait_ge(core.tables_loaded, 16 * core.n_tables)
                for b in range(SEQS):
                    pe.wait_ge(sems.xn_ready, c0 * SEQS + b + 1)
                    for t in range(TILES):
                        last = pe.transpose(core.ps[:, b, t * P:(t + 1) * P], core.y[:, b, t, :], core.ident[:])
                    last.then_inc(turned, 1)

        @block.scalar
        def _(act):
            act.preload_act_table_set(LN_EXP)
            for turn in range(t0, t0 + turns):
                act.wait_ge(sems.var_ready, turn + 1)
                inverse_sqrt(act, core.small[:, 7], core.small[:, 6], core.small[:, 7]).then_inc(sems.rstd_ready, 1)
            if final is None:
                for b in range(SEQS):
                    act.wait_ge(turned, c0 * SEQS + b + 1)
                    act.copy(core.xnT[:, b, :], core.ps[:, b, :])


def inverse_sqrt(act, dst, src, logs, scale=1.0):
    act.activation(logs, src, ACT.Ln, scale=scale)
    act.drain()
    return act.activation(dst, logs, ACT.Exp, scale=-0.5)


def pair_of_blocks(buf, c, off, step):
    v = buf[:, c, off:off + P].unsqueeze(1)
    return bass.AP(v.tensor, v.offset, [list(v.ap[0]), [step, 2], [1, P]])


def diff_attention(core, w):
    nc = core.nc
    HEADS, HD = 16, 8
    PAIRS, VD = HEADS // 2, 2 * HD
    VW = VD + 1
    SPAN = TILES * (TILES + 1) // 2 * P
    OFF = [0, 512, 1024, 896]
    LAMBDA_INIT = 0.8 - 0.6 * float(np.exp(-0.3 * 1))
    RMS_EPS = float(np.finfo(np.float32).eps)
    with ExitStack() as ctx:
        def sb(n, shape, dt=F32):
            return ctx.enter_context(nc.sbuf_tensor(f"da_{n}", shape, dt))

        def sem(n):
            return core.sem(f"da_{n}")

        wT = sb("wT", [P, 4, P])
        qk = sb("qk", [P, TILES, 2 * P])
        rot = sb("rot", [P, TILES, 2 * P])
        swp = sb("swp", [P, TILES, 2 * P])
        ss = sb("ss", [P, TILES, 2 * HEADS])
        rr = sb("rr", [P, TILES, 2 * HEADS])
        vals = sb("vals", [P, TILES, PAIRS, VW])
        qT = sb("qT", [P, TOK])
        kT = sb("kT", [P, TOK])
        qz = sb("qz", [P, 2, TOK])
        probs = sb("probs", [P, 2, SPAN])
        rden = sb("rden", [P, 2, TILES])
        part = sb("part", [P, 2, TILES, VD])
        att = sb("att", [P, TILES, PAIRS, VD])
        attT = sb("attT", [P, TOK])
        lam = sb("lam", [P, 8])
        lamv = sb("lamv", [P, 2, HD // 2])
        xs = sb("xs", [P, TOK])
        xs_ready = sem("xs_ready")
        w_turned = sem("w_turned")
        wT_ready = sem("wT_ready")
        lam_sums = sem("lam_sums")
        lam_exps = sem("lam_exps")
        ones_set = sem("ones_set")
        qkv_ready = sem("qkv_ready")
        sq_ready = sem("sq_ready")
        v_ready = sem("v_ready")
        ms_ready = sem("ms_ready")
        rms_ready = sem("rms_ready")
        rot_ready = sem("rot_ready")
        qkT_turned = sem("qkT_turned")
        qT_ready = sem("qT_ready")
        kT_ready = sem("kT_ready")
        qz_ready = sem("qz_ready")
        scores_ready = sem("scores_ready")
        exp_ready = sem("exp_ready")
        masked = sem("masked")
        out_ready = sem("out_ready")
        out_used = sem("out_used")
        att_ready = sem("att_ready")
        attT_turned = sem("attT_turned")
        attT_ready = sem("attT_ready")
        proj_ready = sem("proj_ready")
        proj_used = sem("proj_used")
        ps = core.ps
        scores = [ps[:, 0:3, :].rearrange("p a b -> p (a b)"), ps[:, 3:6, :].rearrange("p a b -> p (a b)")]
        outs = [ps[:, 6, 0:TILES * VW].rearrange("p (t c) -> p t c", c=VW),
                ps[:, 7, 0:TILES * VW].rearrange("p (t c) -> p t c", c=VW)]
        block = ctx.enter_context(nc.Block())

        @block.tensor
        def _(pe):
            pe.wait_ge(w.loaded, 16 * w.n)
            for n, m in enumerate((w.Wq, w.Wk, w.Wv, w.Wproj)):
                last = pe.transpose(ps[:, 0, n * P:(n + 1) * P], m[:], core.ident[:])
            last.then_inc(w_turned, 1)
            pe.wait_ge(wT_ready, 1)
            with pe.Fori(0, SEQS) as b:
                pe.wait_ge(proj_used, b + 1)
                pe.wait_ge(xs_ready, b + 1)
                for t in range(TILES):
                    last = pe.matmul(ps[:, t, 0:3 * P], xs[:, t * P:(t + 1) * P],
                                     wT[:, 0:3, :], start=True, stop=True)
                last.then_inc(qkv_ready, 1)
                pe.wait_ge(rot_ready, b + 1)
                for c in range(2):
                    for t in range(TILES):
                        last = pe.transpose(ps[:, 4 + c, t * P:(t + 1) * P], rot[:, t, c * P:(c + 1) * P],
                                            core.ident[:])
                last.then_inc(qkT_turned, 1)
                pe.wait_ge(kT_ready, b + 1)
                pe.wait_ge(v_ready, b + 1)

                def score(n, c):
                    pe.wait_ge(qz_ready, n)
                    for j in range(TILES):
                        last = pe.matmul(scores[c][:, OFF[j]:OFF[j] + TOK - j * P], kT[:, j * P:(j + 1) * P],
                                         qz[:, c, j * P:TOK], start=True, stop=True)
                    last.then_inc(scores_ready, 1)

                def values(n, c, pair):
                    pe.wait_ge(masked, n)
                    pe.wait_ge(out_used, n)
                    for i in range(TILES):
                        for j in range(i + 1):
                            last = pe.matmul(outs[c][:, i, :], probs[:, c, OFF[j] + (i - j) * P:OFF[j] + (i - j + 1) * P],
                                             vals[:, j, pair, :], start=(j == 0), stop=(j == i))
                    last.then_inc(out_ready, 1)

                score(b * HEADS + 1, 0)
                with pe.Fori(0, PAIRS - 1) as k:
                    score(b * HEADS + k * 2 + 2, 1)
                    values(b * HEADS + k * 2 + 1, 0, k)
                    score(b * HEADS + k * 2 + 3, 0)
                    values(b * HEADS + k * 2 + 2, 1, k)
                score(b * HEADS + HEADS, 1)
                values(b * HEADS + HEADS - 1, 0, PAIRS - 1)
                values(b * HEADS + HEADS, 1, PAIRS - 1)
                pe.wait_ge(att_ready, b + 1)
                for t in range(TILES):
                    last = pe.transpose(ps[:, 0, t * P:(t + 1) * P], att[:, t].rearrange("p h d -> p (h d)"), core.ident[:])
                last.then_inc(attT_turned, 1)
                pe.wait_ge(attT_ready, b + 1)
                for t in range(TILES):
                    last = pe.matmul(ps[:, 1, t * P:(t + 1) * P], attT[:, t * P:(t + 1) * P], wT[:, 3, :],
                                     start=True, stop=True)
                last.then_inc(proj_ready, 1)

        @block.scalar
        def _(act):
            act.preload_act_table_set(LN_EXP)
            act.wait_ge(w_turned, 1)
            act.copy(wT[:], ps[:, 0, :].rearrange("p (n c) -> p n c", n=4)).then_inc(wT_ready, 1)
            act.wait_ge(lam_sums, 1)
            act.activation(lam[:, 2:4], lam[:, 0:2], ACT.Exp).then_inc(lam_exps, 1)
            act.wait_ge(ones_set, 1)
            act.sem_inc(out_ready, 2)
            with act.Fori(0, SEQS) as b:
                act.wait_ge(qkv_ready, b + 2)
                act.activation(swp[:], ps[:, 0:TILES, 0:2 * P], ACT.Square).then_inc(sq_ready, 1)
                for t in range(TILES):
                    last = act.copy(vals[:, t, :, 0:VD], ps[:, t, 2 * P:3 * P].rearrange("p (h d) -> p h d", d=VD))
                last.then_inc(v_ready, 1)
                act.wait_ge(ms_ready, b + 1)
                inverse_sqrt(act, rr[:], ss[:], rr[:]).then_inc(rms_ready, 1)
                act.wait_ge(qkT_turned, b + 1)
                act.copy(qT[:], ps[:, 4, :]).then_inc(qT_ready, 1)
                act.copy(kT[:], ps[:, 5, :]).then_inc(kT_ready, 1)
                with act.Fori(0, PAIRS) as k:
                    for c in range(2):
                        act.wait_ge(scores_ready, b * HEADS + k * 2 + c + 1)
                        act.wait_ge(out_ready, b * HEADS + k * 2 + c + 1)
                        act.activation(probs[:, c, :], scores[c][:, 0:SPAN], ACT.Exp,
                                       scale=float(HD) ** -0.5).then_inc(exp_ready, 1)
                act.wait_ge(attT_turned, b + 1)
                act.copy(attT[:], ps[:, 0, :]).then_inc(attT_ready, 1)
                act.wait_ge(proj_ready, b + 1)
                act.copy(core.y[:, b],
                         ps[:, 1, :].rearrange("p (t d) -> p t d", t=TILES)).then_inc(proj_used, 1)

        @block.gpsimd
        def _(pool):
            pool.sem_inc(qkv_ready, 1)
            with pool.Fori(0, SEQS) as b:
                pool.wait_ge(qkv_ready, b + 1)
                pool.tensor_copy(xs[:], core.xnT[:, b, :]).then_inc(xs_ready, 1)

        @block.vector
        def _(dve):
            dve.wait_ge(w.loaded, 16 * w.n)
            dve.tensor_tensor(lamv[:, 0], w.lam[:, 0], w.lam[:, 1], ALU.mult)
            dve.tensor_tensor(lamv[:, 1], w.lam[:, 2], w.lam[:, 3], ALU.mult)
            dve.drain()
            dve.tensor_reduce(lam[:, 0:2], lamv[:], AX_X, ALU.add).then_inc(lam_sums, 1)
            dve.memset(vals[:], 1.0).then_inc(ones_set, 1)
            dve.sem_inc(proj_used, 1)
            dve.wait_ge(lam_exps, 1)
            dve.tensor_tensor(lam[:, 4:5], lam[:, 3:4], lam[:, 2:3], ALU.subtract)
            dve.drain()
            dve.tensor_scalar(lam[:, 5:6], lam[:, 4:5], -LAMBDA_INIT, None, ALU.add)
            dve.sem_inc(out_used, 2)
            heads = "p t (h d) -> p t h d"
            with dve.Fori(0, SEQS) as b:
                dve.wait_ge(sq_ready, b + 1)
                dve.tensor_reduce(ss[:], swp[:].rearrange(heads, d=HD), AX_X, ALU.add)
                dve.drain()
                dve.tensor_scalar(ss[:], ss[:], 1.0 / HD, RMS_EPS, ALU.mult, ALU.add).then_inc(ms_ready, 1)
                dve.wait_ge(rms_ready, b + 1)
                dve.wait_ge(v_ready, b + 1)
                for t in range(TILES):
                    dve.tensor_tensor(qk[:, t].rearrange("p (h d) -> p h d", d=HD),
                                      ps[:, t, 0:2 * P].rearrange("p (h d) -> p h d", d=HD),
                                      rr[:, t].unsqueeze(2).broadcast_to([P, 2 * HEADS, HD]), ALU.mult)
                dve.drain()
                for t in range(TILES):
                    src = qk[:, t].rearrange("p (h d) -> p h d", d=HD)
                    dst = swp[:, t].rearrange("p (h d) -> p h d", d=HD)
                    for half in range(2):
                        a, z = slice(4 * half, 4 * half + 4), slice(4 - 4 * half, 8 - 4 * half)
                        dve.tensor_tensor(dst[:, :, a], src[:, :, z],
                                          core.t.rope8[:, 1, t, a].unsqueeze(1).broadcast_to([P, 2 * HEADS, 4]), ALU.mult)
                    dve.tensor_tensor(rot[:, t].rearrange("p (h d) -> p h d", d=HD), src,
                                      core.t.rope8[:, 0, t, :].unsqueeze(1).broadcast_to([P, 2 * HEADS, HD]), ALU.mult)
                dve.drain()
                dve.tensor_tensor(rot[:], rot[:], swp[:], ALU.add).then_inc(rot_ready, 1)

                def head_q(n, h, c, ring_free):
                    if ring_free is not None:
                        dve.wait_ge(scores_ready, ring_free)
                    dve.tensor_scalar(qz[:, c, :], qT[:], core.t.head8[:, h, :], None, ALU.mult).then_inc(qz_ready, 1)

                def causal(n, c):
                    dve.wait_ge(exp_ready, n)
                    for off, step in ((0, 512), (896, 128)):
                        blocks = pair_of_blocks(probs, c, off, step)
                        last = dve.tensor_tensor(blocks, blocks,
                                                 core.t.upper[:].unsqueeze(1).broadcast_to([P, 2, P]), ALU.mult)
                    last.then_inc(masked, 1)

                def weigh(n, c, k):
                    dve.wait_ge(out_ready, n + 2)
                    dve.reciprocal(rden[:, c, :], outs[c][:, :, VD])
                    dve.drain()
                    dve.tensor_tensor(part[:, c], outs[c][:, :, 0:VD],
                                      rden[:, c, :].unsqueeze(2).broadcast_to([P, TILES, VD]), ALU.mult).then_inc(out_used, 1)
                    if c == 0:
                        return
                    dve.drain()
                    return dve.scalar_tensor_tensor(out=att[:, :, k, :], in0=part[:, 1], scalar=lam[:, 5:6],
                                                    in1=part[:, 0], op0=ALU.mult, op1=ALU.add)

                def step(k, c, more=True, before=True):
                    n = b * HEADS + k * 2 + c + 1
                    causal(n, c)
                    if more:
                        head_q(n, k + 1 + PAIRS * c, c, n)
                    if before:
                        weigh(n - 1, 1 - c, k if c else k - 1)

                dve.wait_ge(qT_ready, b + 1)
                head_q(0, 0, 0, None)
                head_q(0, PAIRS, 1, None)
                step(0, 0, before=False)
                step(0, 1)
                with dve.Fori(1, PAIRS - 1) as k:
                    step(k, 0)
                    step(k, 1)
                step(PAIRS - 1, 0, more=False)
                step(PAIRS - 1, 1, more=False)
                weigh(b * HEADS + HEADS, 1, PAIRS - 1).then_inc(att_ready, 1)


def gated_ffn(core, w):
    nc = core.nc
    CHUNKS = 384 // P
    with ExitStack() as ctx:
        def sb(n, shape, dt=F32):
            return ctx.enter_context(nc.sbuf_tensor(f"gf_{n}", shape, dt))

        def sem(n):
            return core.sem(f"gf_{n}")

        wf = sb("wf", [P, 3, CHUNKS, P])
        wT = sb("wT", [P, 3, CHUNKS, P])
        act_g = sb("act_g", [P, 2, TOK])
        hid = sb("hid", [P, 2, CHUNKS, TOK])
        w_float = sem("w_float")
        w_turned = sem("w_turned")
        wT_ready = sem("wT_ready")
        gu_ready = sem("gu_ready")
        silu_ready = sem("silu_ready")
        hid_ready = sem("hid_ready")
        down_ready = sem("down_ready")
        y_ready = sem("y_ready")
        ps = core.ps
        block = ctx.enter_context(nc.Block())

        @block.vector
        def _(dve):
            dve.wait_ge(w.loaded, 16 * w.n)
            for n, m in enumerate((w.gate, w.up, w.down)):
                last = dve.tensor_scalar(wf[:, n], m[:], float(np.float32(1.0 / 127.0)), None, ALU.mult)
            last.then_inc(w_float, 1)
            dve.sem_inc(y_ready, 1)
            with dve.Fori(0, SEQS // 2) as b2:
                for s in range(2):
                    for c in range(CHUNKS):
                        n = (b2 * 2 + s) * CHUNKS + c
                        dve.wait_ge(silu_ready, n + 1)
                        dve.tensor_tensor(hid[:, s, c], act_g[:, (s * CHUNKS + c) % 2], ps[:, 4 + (s * CHUNKS + c) % 2, :],
                                          ALU.mult).then_inc(hid_ready, 1)
                    dve.wait_ge(down_ready, b2 * 2 + s + 1)
                    dve.tensor_copy(core.y[:, b2 * 2 + s], ps[:, 6 + s, :].rearrange("p (t d) -> p t d", d=D)).then_inc(y_ready, 1)

        @block.tensor
        def _(pe):
            pe.wait_ge(w_float, 1)
            for n in range(3):
                for c in range(CHUNKS):
                    last = pe.transpose(ps[:, n, c * P:(c + 1) * P], wf[:, n, c, :], core.ident[:])
            last.then_inc(w_turned, 1)
            pe.wait_ge(wT_ready, 1)

            def down(n, s):
                pe.wait_ge(y_ready, n + 1)
                pe.wait_ge(hid_ready, (n + 1) * CHUNKS + 2)
                for t in range(TILES):
                    for c in range(CHUNKS):
                        last = pe.matmul(ps[:, 6 + s, t * P:(t + 1) * P], hid[:, s, c, t * P:(t + 1) * P], wT[:, 2, c, :],
                                         start=(c == 0), stop=(c == CHUNKS - 1))
                last.then_inc(down_ready, 1)

            with pe.Fori(0, SEQS // 2) as b2:
                for s in range(2):
                    for c in range(CHUNKS):
                        n = (b2 * 2 + s) * CHUNKS + c
                        pe.wait_ge(hid_ready, n + 1)
                        for g in range(2):
                            last = pe.matmul(ps[:, 2 + 2 * g + (s * CHUNKS + c) % 2, :], wT[:, g, c, :],
                                             core.xnT[:, b2 * 2 + s, :], start=True, stop=True)
                        last.then_inc(gu_ready, 1)
                    down(b2 * 2 + s, s)

        @block.scalar
        def _(act):
            act.wait_ge(w_turned, 1)
            act.copy(wT[:], ps[:, 0:3, 0:3 * P].rearrange("p n (c k) -> p n c k", c=CHUNKS)).then_inc(wT_ready, 1)
            act.sem_inc(hid_ready, 2)
            with act.Fori(0, SEQS // 2) as b2:
                for s in range(2):
                    for c in range(CHUNKS):
                        n = (b2 * 2 + s) * CHUNKS + c
                        act.wait_ge(gu_ready, n + 1)
                        act.wait_ge(hid_ready, n + 1)
                        act.activation(act_g[:, (s * CHUNKS + c) % 2], ps[:, 2 + (s * CHUNKS + c) % 2, :],
                                       ACT.Silu).then_inc(silu_ready, 1)


def band_attention(core, w):
    nc = core.nc
    STEPS = SEQS * TILES
    with ExitStack() as ctx:
        def sb(n, shape, dt=F32):
            return ctx.enter_context(nc.sbuf_tensor(f"ba_{n}", shape, dt))

        def sem(n):
            return core.sem(f"ba_{n}")

        xs = sb("xs", [P, TOK])
        qT = sb("qT", [P, TOK])
        kT = sb("kT", [P, TOK])
        vals = sb("vals", [P, TILES, D])
        sc = sb("sc", [P, 2, TOK])
        pr = sb("pr", [P, 2, TOK])
        prT = sb("prT", [P, 2, TILES, P])
        top = sb("top", [P, 2, 4])
        xs_ready = sem("xs_ready")
        qk_ready = sem("qk_ready")
        v_ready = sem("v_ready")
        qT_ready = sem("qT_ready")
        kT_ready = sem("kT_ready")
        vals_ready = sem("vals_ready")
        scores_ready = sem("scores_ready")
        banded = sem("banded")
        exp_ready = sem("exp_ready")
        turned = sem("turned")
        prT_ready = sem("prT_ready")
        out_ready = sem("out_ready")
        y_ready = sem("y_ready")
        ps = core.ps
        block = ctx.enter_context(nc.Block())

        @block.gpsimd
        def _(pool):
            pool.sem_inc(v_ready, 1)
            with pool.Fori(0, SEQS) as b:
                pool.wait_ge(v_ready, b + 1)
                pool.tensor_copy(xs[:], core.xnT[:, b, :]).then_inc(xs_ready, 1)

        @block.tensor
        def _(pe):
            pe.wait_ge(w.loaded, 16 * w.n)
            with pe.Fori(0, SEQS) as b:
                pe.wait_ge(y_ready, b * TILES + 2)
                for n, m in enumerate((w.WQ, w.WK)):
                    last = pe.matmul(ps[:, n, :], m[:], core.xnT[:, b, :], start=True, stop=True)
                last.then_inc(qk_ready, 1)
                pe.wait_ge(xs_ready, b + 1)
                for t in range(TILES):
                    last = pe.matmul(ps[:, 2, t * P:(t + 1) * P], xs[:, t * P:(t + 1) * P], w.WV[:], start=True, stop=True)
                last.then_inc(v_ready, 1)
                pe.wait_ge(qT_ready, b + 1)
                pe.wait_ge(kT_ready, b + 1)

                def score(t):
                    last = pe.matmul(ps[:, t % 2, :], qT[:, t * P:(t + 1) * P], kT[:], start=True, stop=True)
                    last.then_inc(scores_ready, 1)

                score(0)
                for t in range(TILES):
                    n = b * TILES + t
                    if t + 1 < TILES:
                        pe.wait_ge(banded, n + 1)
                        score(t + 1)
                    pe.wait_ge(exp_ready, n + 1)
                    for k in range(TILES):
                        last = pe.transpose(ps[:, 3 + t % 2, k * P:(k + 1) * P], pr[:, t % 2, k * P:(k + 1) * P], core.ident[:])
                    last.then_inc(turned, 1)
                    if t == 0:
                        pe.wait_ge(vals_ready, b + 1)
                    pe.wait_ge(prT_ready, n + 1)
                    pe.wait_ge(y_ready, n + 1)
                    for k in range(TILES):
                        last = pe.matmul(ps[:, 5 + t % 2, 0:D], prT[:, t % 2, k], vals[:, k], start=(k == 0),
                                         stop=(k == TILES - 1))
                    last.then_inc(out_ready, 1)

        @block.scalar
        def _(act):
            with act.Fori(0, SEQS) as b:
                act.wait_ge(qk_ready, b + 1)
                act.copy(qT[:], ps[:, 0, :]).then_inc(qT_ready, 1)
                act.wait_ge(v_ready, b + 2)
                act.copy(vals[:], ps[:, 2, :].rearrange("p (t d) -> p t d", d=D)).then_inc(vals_ready, 1)
                for t in range(TILES):
                    n = b * TILES + t
                    c = t % 2
                    act.wait_ge(banded, n + 1)
                    act.activation(pr[:, c], sc[:, c], ACT.Exp, bias=top[:, c, 1:2],
                                   accum_out=top[:, c, 2:3]).then_inc(exp_ready, 1)
                    act.wait_ge(turned, n + 1)
                    act.copy(prT[:, c], ps[:, 3 + c, :].rearrange("p (k q) -> p k q", q=P)).then_inc(prT_ready, 1)

        @block.vector
        def _(dve):
            dve.sem_inc(y_ready, 2)
            with dve.Fori(0, SEQS) as b:
                dve.wait_ge(qk_ready, b + 1)
                dve.tensor_copy(kT[:], ps[:, 1, :]).then_inc(kT_ready, 1)

                def weigh(n, t):
                    c = t % 2
                    dve.wait_ge(exp_ready, n)
                    dve.reciprocal(top[:, c, 3:4], top[:, c, 2:3])
                    dve.drain()
                    dve.wait_ge(out_ready, n)
                    dve.tensor_scalar(core.y[:, b, t, :], ps[:, 5 + c, 0:D], top[:, c, 3:4], None, ALU.mult).then_inc(y_ready, 1)

                for t in range(TILES):
                    n = b * TILES + t
                    c = t % 2
                    dve.wait_ge(scores_ready, n + 1)
                    dve.tensor_tensor(sc[:, c], ps[:, c, :], core.t.band[:, t, :], ALU.mult)
                    dve.drain()
                    dve.tensor_reduce(top[:, c, 1:2], sc[:, c], AX_X, ALU.max, negate=True).then_inc(banded, 1)
                    if t:
                        weigh(n, t - 1)
                weigh(b * TILES + TILES, TILES - 1)


def shared_expert_ffn(core, w):
    nc = core.nc
    E1 = 7
    with ExitStack() as ctx:
        def sb(n, shape, dt=F32):
            return ctx.enter_context(nc.sbuf_tensor(f"se_{n}", shape, dt))

        def sem(n):
            return core.sem(f"se_{n}")

        xs = sb("xs", [P, 2, TOK])
        wT = sb("wT", [P, 2 * P + E1])
        pr = sb("pr", [P, TILES, 8])
        m = sb("m", [P, 8, TILES])
        top = sb("top", [P, TILES, 8])
        base = sb("base", [P, 2, TILES, D])
        one = sb("one", [P, TILES, D])
        w_turned = sem("w_turned")
        wT_ready = sem("wT_ready")
        xs_ready = sem("xs_ready")
        mm_ready = sem("mm_ready")
        shifted = sem("shifted")
        exp_ready = sem("exp_ready")
        y_ready = sem("y_ready")
        ps = core.ps
        block = ctx.enter_context(nc.Block())

        @block.gpsimd
        def _(pool):
            pool.wait_ge(w.loaded, 16 * w.n)
            pool.tensor_copy(wT[:, 2 * P:], w.W_gate[:]).then_inc(wT_ready, 1)
            pool.sem_inc(mm_ready, 2)
            with pool.Fori(0, SEQS // 2) as b2:
                for s in range(2):
                    pool.wait_ge(mm_ready, b2 * 2 + s + 1)
                    pool.tensor_copy(xs[:, s], core.xnT[:, b2 * 2 + s, :]).then_inc(xs_ready, 1)

        @block.tensor
        def _(pe):
            pe.wait_ge(w.loaded, 16 * w.n)
            for n, mat in enumerate((w.W_shared, w.W_expert)):
                last = pe.transpose(ps[:, 0, n * P:(n + 1) * P], mat[:], core.ident[:])
            last.then_inc(w_turned, 1)
            pe.wait_ge(wT_ready, 2)
            with pe.Fori(0, SEQS // 2) as b2:
                for s in range(2):
                    pe.wait_ge(xs_ready, b2 * 2 + s + 1)
                    pe.wait_ge(y_ready, b2 * 2 + s + 1)
                    for t in range(TILES):
                        last = pe.matmul(ps[:, 4 * s + t, 0:2 * P + E1], xs[:, s, t * P:(t + 1) * P], wT[:],
                                         start=True, stop=True)
                    last.then_inc(mm_ready, 1)

        @block.scalar
        def _(act):
            act.wait_ge(w_turned, 1)
            act.copy(wT[:, 0:2 * P], ps[:, 0, 0:2 * P]).then_inc(wT_ready, 1)
            with act.Fori(0, SEQS) as b:
                act.wait_ge(shifted, b + 1)
                act.activation(pr[:, :, 0:E1], pr[:, :, 0:E1], ACT.Exp).then_inc(exp_ready, 1)

        @block.vector
        def _(dve):
            dve.wait_ge(w.loaded, 16 * w.n)
            dve.memset(pr[:], -1.0)
            dve.sem_inc(y_ready, 2)
            dve.drain()
            with dve.Fori(0, SEQS // 2) as b2:
                for s in range(2):
                    n = b2 * 2 + s
                    logits = ps[:, 4 * s:4 * s + 4, 2 * P:2 * P + E1]
                    dve.wait_ge(mm_ready, n + 3)
                    dve.tensor_reduce(m[:, 0], logits, AX_X, ALU.max)
                    dve.drain()
                    dve.tensor_tensor(pr[:, :, 0:E1], logits, m[:, 0].unsqueeze(2).broadcast_to([P, TILES, E1]),
                                      ALU.subtract).then_inc(shifted, 1)
                    for t in range(TILES):
                        dve.tensor_tensor(base[:, s, t], ps[:, 4 * s + t, 0:P], w.bias[:], ALU.add)
                    dve.wait_ge(exp_ready, n + 1)
                    dve.tensor_reduce(m[:, 1], pr[:, :, 0:E1], AX_X, ALU.add)
                    dve.drain()
                    dve.reciprocal(m[:, 2], m[:, 1])
                    dve.drain()
                    dve.tensor_tensor(pr[:, :, 0:E1], pr[:, :, 0:E1], m[:, 2].unsqueeze(2).broadcast_to([P, TILES, E1]), ALU.mult)
                    dve.drain()
                    for t in range(TILES):
                        dve.max(top[:, t], pr[:, t])
                    dve.drain()
                    dve.tensor_tensor(m[:, 3], top[:, :, 0], top[:, :, 1], ALU.add)
                    dve.drain()
                    dve.reciprocal(m[:, 4], m[:, 3])
                    dve.drain()
                    for c in range(2):
                        dve.tensor_tensor(m[:, 5 + c], top[:, :, c], m[:, 4], ALU.mult)
                    dve.drain()
                    for t in range(TILES):
                        dve.scalar_tensor_tensor(out=one[:, t], in0=ps[:, 4 * s + t, P:2 * P], scalar=m[:, 5, t:t + 1],
                                                 in1=base[:, s, t], op0=ALU.mult, op1=ALU.add)
                    dve.drain()
                    for t in range(TILES):
                        last = dve.scalar_tensor_tensor(out=core.y[:, n, t, :], in0=ps[:, 4 * s + t, P:2 * P],
                                                        scalar=m[:, 6, t:t + 1], in1=one[:, t], op0=ALU.mult, op1=ALU.add)
                    last.then_inc(y_ready, 1)


def linear_attention(core, w):
    nc = core.nc
    HEADS, HD = 16, 64
    PAIRS = HEADS // 2
    INNER = HEADS * HD
    VW = HD + 1
    ROUNDS = [(0, 3), (3, 3), (6, 2)]
    with ExitStack() as ctx:
        def sb(n, shape, dt=F32):
            return ctx.enter_context(nc.sbuf_tensor(f"la_{n}", shape, dt))

        def sem(n):
            return core.sem(f"la_{n}")

        xs = sb("xs", [P, TOK])
        relu = sb("relu", [P, 2, BANK])
        expo = sb("expo", [P, 2, BANK])
        qk = sb("qk", [P, 2, 2, INNER])
        vals = sb("vals", [P, 2, HEADS, VW])
        gate = sb("gate", [P, 2, INNER])
        qT = sb("qT", [P, PAIRS, P])
        kTz = sb("kTz", [P, PAIRS, 2, P])
        inner = sb("inner", [P, PAIRS, 2, P])
        state = sb("state", [P, PAIRS, 2 * VW])
        rden = sb("rden", [P, HEADS])
        att = sb("att", [P, INNER])
        attT = sb("attT", [P, PAIRS, P])
        ready = sem("ready")
        xs_ready = sem("xs_ready")
        proj_ready = sem("proj_ready")
        exp_ready = sem("exp_ready")
        phi_ready = sem("phi_ready")
        vg_ready = sem("vg_ready")
        k_turned = sem("k_turned")
        q_turned = sem("q_turned")
        kz_low = sem("kz_low")
        kz_high = sem("kz_high")
        qT_ready = sem("qT_ready")
        inner_ready = sem("inner_ready")
        masked = sem("masked")
        out_ready = sem("out_ready")
        att_ready = sem("att_ready")
        outer_ready = sem("outer_ready")
        state_ready = sem("state_ready")
        att_turned = sem("att_turned")
        attT_ready = sem("attT_ready")
        y_psum = sem("y_psum")
        y_ready = sem("y_ready")
        ps = core.ps
        block = ctx.enter_context(nc.Block())
        rhs = [w.w_qkv[:, j * BANK:(j + 1) * BANK] for j in range(6)] + [w.w_gate[:, j * BANK:(j + 1) * BANK] for j in range(2)]

        @block.gpsimd
        def _(pool):
            pool.memset(kTz[:], 0.0)
            pool.memset(vals[:], 1.0)
            pool.memset(state[:], 0.0).then_inc(ready, 1)
            pool.sem_inc(y_psum, 2)
            with pool.Fori(0, SEQS) as b:
                pool.wait_ge(y_psum, b * TILES + 1)
                pool.tensor_copy(xs[:], core.xnT[:, b, :]).then_inc(xs_ready, 1)

        @block.tensor
        def _(pe):
            pe.wait_ge(w.loaded, 16 * w.n)
            pe.wait_ge(ready, 1)
            with pe.Fori(0, SEQS) as b:
                def project(t, js):
                    n = b * TILES + t
                    for j in js:
                        if j < 2:
                            pe.wait_ge(vg_ready, n * 4 + 3 + j)
                        elif j < 6:
                            pe.wait_ge(phi_ready, n * 4 + j - 1)
                        else:
                            pe.wait_ge(vg_ready, n * 4 + j - 1)
                        last = pe.matmul(ps[:, j % 2, :], xs[:, t * P:(t + 1) * P], rhs[j], start=True, stop=True)
                        last.then_inc(proj_ready, 1)

                def outer(t, r):
                    p0, np_ = ROUNDS[r]
                    pe.wait_ge(state_ready, (b * TILES + t) * 3 + r + 1)
                    for p in range(p0, p0 + np_):
                        last = pe.matmul(ps[:, 7, (p - p0) * 2 * VW:(p - p0 + 1) * 2 * VW],
                                         qk[:, t % 2, 1, p * P:(p + 1) * P],
                                         vals[:, t % 2, 2 * p:2 * p + 2, :].rearrange("p h c -> p (h c)"), start=True, stop=True)
                    last.then_inc(outer_ready, 1)

                pe.wait_ge(xs_ready, b + 1)
                project(0, range(8))
                for t in range(TILES):
                    n = b * TILES + t
                    s = t % 2
                    pe.wait_ge(phi_ready, n * 4 + 4)
                    pe.wait_ge(y_ready, n + 1)
                    pe.wait_ge(attT_ready, n + 1)
                    for p in range(PAIRS):
                        last = pe.transpose(ps[:, 2 + p // 4, (p % 4) * P:(p % 4 + 1) * P], qk[:, s, 1, p * P:(p + 1) * P], core.ident[:])
                    last.then_inc(k_turned, 1)
                    for p in range(PAIRS):
                        last = pe.transpose(ps[:, 4 + p // 4, (p % 4) * P:(p % 4 + 1) * P], qk[:, s, 0, p * P:(p + 1) * P], core.ident[:])
                    last.then_inc(q_turned, 1)
                    pe.wait_ge(kz_low, n + 1)
                    pe.wait_ge(kz_high, n + 1)
                    pe.wait_ge(qT_ready, n + 1)
                    for g in range(4):
                        if g >= 2:
                            pe.wait_ge(masked, n * 4 + g - 1)
                        for u in range(4):
                            p, h = 2 * g + u // 2, u % 2
                            last = pe.matmul(ps[:, 2 + g % 2, u * P:(u + 1) * P], kTz[:, p, h, :], qT[:, p, :], start=True, stop=True)
                        last.then_inc(inner_ready, 1)
                    pe.wait_ge(state_ready, n * 3 + 1)
                    pe.wait_ge(vg_ready, n * 4 + 6)
                    for r, (p0, np_) in enumerate(ROUNDS):
                        pe.wait_ge(masked, n * 4 + (p0 + np_ + 1) // 2)
                        for p in range(p0, p0 + np_):
                            o = (p - p0) * 2 * VW
                            pe.matmul(ps[:, 4 + r, o:o + 2 * VW], qT[:, p, :], state[:, p, :], start=True, stop=True)
                            for h in range(2):
                                last = pe.matmul(ps[:, 4 + r, o + h * VW:o + (h + 1) * VW], inner[:, p, h, :],
                                                 vals[:, s, 2 * p + h, :], start=False, stop=True, skip_group_check=True)
                        last.then_inc(out_ready, 1)
                    outer(t, 0)
                    if t + 1 < TILES:
                        project(t + 1, range(0, 4))
                    outer(t, 1)
                    if t + 1 < TILES:
                        project(t + 1, range(4, 8))
                    outer(t, 2)
                    pe.wait_ge(att_ready, n + 1)
                    for p in range(PAIRS):
                        last = pe.transpose(ps[:, 2 + p // 4, (p % 4) * P:(p % 4 + 1) * P], att[:, p * P:(p + 1) * P], core.ident[:])
                    last.then_inc(att_turned, 1)
                    pe.wait_ge(attT_ready, n + 2)
                    for p in range(PAIRS):
                        last = pe.matmul(ps[:, 6, 0:D], attT[:, p, :], w.w_out[:, p, :], start=(p == 0), stop=(p == PAIRS - 1))
                    last.then_inc(y_psum, 1)

        @block.scalar
        def _(act):
            act.wait_ge(ready, 1)
            act.sem_inc(vg_ready, 4)
            act.sem_inc(attT_ready, 1)
            with act.Fori(0, SEQS) as b:
                def features(t):
                    n = b * TILES + t
                    for j in range(8):
                        act.wait_ge(proj_ready, n * 8 + j + 1)
                        src = ps[:, j % 2, :]
                        if j < 4:
                            act.wait_ge(phi_ready, n * 4 + j - 1) if j >= 2 else None
                            act.activation(relu[:, j % 2], src, ACT.Relu, scale=-1.0)
                            act.drain()
                            act.activation(expo[:, j % 2], relu[:, j % 2], ACT.Exp, scale=-1.0).then_inc(exp_ready, 1)
                        elif j < 6:
                            act.copy(vals[:, t % 2, 8 * (j - 4):8 * (j - 3), 0:HD], src.rearrange("p (h d) -> p h d", d=HD)).then_inc(vg_ready, 1)
                        else:
                            act.activation(gate[:, t % 2, (j - 6) * BANK:(j - 5) * BANK], src, ACT.Tanh, scale=0.5).then_inc(vg_ready, 1)

                features(0)
                for t in range(TILES):
                    n = b * TILES + t
                    act.wait_ge(k_turned, n + 1)
                    act.copy(kTz[0:64, :, 0, :], ps[0:64, 2:4, :].rearrange("p a (b c) -> p (a b) c", c=P)).then_inc(kz_low, 1)
                    act.wait_ge(q_turned, n + 1)
                    act.copy(qT[:], ps[:, 4:6, :].rearrange("p a (b c) -> p (a b) c", c=P)).then_inc(qT_ready, 1)
                    if t + 1 < TILES:
                        features(t + 1)
                    act.wait_ge(att_turned, n + 1)
                    act.copy(attT[:], ps[:, 2:4, :].rearrange("p a (b c) -> p (a b) c", c=P)).then_inc(attT_ready, 1)

        @block.vector
        def _(dve):
            dve.wait_ge(ready, 1)
            dve.sem_inc(y_ready, 1)
            dve.sem_inc(state_ready, 1)
            with dve.Fori(0, SEQS) as b:
                def phi(t, j):
                    dve.wait_ge(exp_ready, (b * TILES + t) * 4 + j + 1)
                    dve.scalar_tensor_tensor(out=qk[:, t % 2, j // 2, (j % 2) * BANK:(j % 2 + 1) * BANK], in0=ps[:, j % 2, :],
                                             scalar=0.0, in1=expo[:, j % 2], op0=ALU.max, op1=ALU.add).then_inc(phi_ready, 1)

                def add_state(t, r):
                    p0, np_ = ROUNDS[r]
                    dve.wait_ge(outer_ready, (b * TILES + t) * 3 + r + 1)
                    src = ps[:, 7, 0:np_ * 2 * VW].rearrange("p (a c) -> p a c", c=2 * VW)
                    for h in range(2):
                        rows, cols = slice(64 * h, 64 * h + 64), slice(VW * h, VW * h + VW)
                        dst = state[rows, p0:p0 + np_, cols]
                        if t == TILES - 1:
                            last = dve.memset(dst, 0.0)
                        else:
                            last = dve.tensor_tensor(dst, dst, src[rows, :, cols], ALU.add)
                    last.then_inc(state_ready, 1)

                for j in range(4):
                    phi(0, j)
                for t in range(TILES):
                    n = b * TILES + t
                    dve.wait_ge(k_turned, n + 1)
                    dve.tensor_copy(kTz[64:128, :, 1, :], ps[64:128, 2:4, :].rearrange("p a (b c) -> p (a b) c", c=P)).then_inc(kz_high, 1)
                    for g in range(4):
                        dve.wait_ge(inner_ready, n * 4 + g + 1)
                        dve.tensor_tensor(inner[:, 2 * g:2 * g + 2].rearrange("p a h c -> p (a h) c"),
                                          ps[:, 2 + g % 2, :].rearrange("p (a c) -> p a c", c=P),
                                          core.t.upper[:].unsqueeze(1).broadcast_to([P, 4, P]), ALU.mult).then_inc(masked, 1)
                    dve.wait_ge(vg_ready, n * 4 + 8)
                    for r, (p0, np_) in enumerate(ROUNDS):
                        h0, nh = 2 * p0, 2 * np_
                        o = ps[:, 4 + r, 0:nh * VW].rearrange("p (h c) -> p h c", c=VW)
                        a = att[:, h0 * HD:(h0 + nh) * HD].rearrange("p (h c) -> p h c", c=HD)
                        dve.wait_ge(out_ready, n * 3 + r + 1)
                        dve.tensor_scalar(rden[:, h0:h0 + nh], o[:, :, HD], 2.0, 2e-6, ALU.mult, ALU.add)
                        dve.scalar_tensor_tensor(out=a, in0=gate[:, t % 2, h0 * HD:(h0 + nh) * HD].rearrange("p (h c) -> p h c", c=HD),
                                                 scalar=1.0, in1=o[:, :, 0:HD], op0=ALU.add, op1=ALU.mult)
                        dve.drain()
                        dve.reciprocal(rden[:, h0:h0 + nh], rden[:, h0:h0 + nh])
                        dve.drain()
                        last = dve.tensor_tensor(a, a, rden[:, h0:h0 + nh].unsqueeze(2).broadcast_to([P, nh, HD]), ALU.mult)
                    last.then_inc(att_ready, 1)
                    add_state(t, 0)
                    if t + 1 < TILES:
                        phi(t + 1, 0)
                        phi(t + 1, 1)
                    add_state(t, 1)
                    if t + 1 < TILES:
                        phi(t + 1, 2)
                        phi(t + 1, 3)
                    add_state(t, 2)
                    dve.wait_ge(y_psum, n + 3)
                    dve.tensor_copy(core.y[:, b, t, :], ps[:, 6, 0:D]).then_inc(y_ready, 1)


def expert_ffn(core, w):
    nc = core.nc
    E, CH = 8, 2
    STEPS = E * CH
    with ExitStack() as ctx:
        def sb(n, shape, dt=F32):
            return ctx.enter_context(nc.sbuf_tensor(f"ef_{n}", shape, dt))

        def sem(n):
            return core.sem(f"ef_{n}")

        xs = sb("xs", [P, TOK])
        pr = sb("pr", [P, TILES, E])
        top = sb("top", [P, TILES, 8])
        idx = sb("idx", [P, TILES, 8], U32)
        idf = sb("idf", [P, TILES, 8])
        m = sb("m", [P, 8, TILES])
        hot = sb("hot", [P, 2, TILES, E])
        full = sb("full", [P, TILES, E])
        act_g = sb("act_g", [P, 2, TOK])
        hid = sb("hid", [P, 2, CH, TOK])
        acc = sb("acc", [P, TILES, D])
        xs_ready = sem("xs_ready")
        routed = sem("routed")
        shifted = sem("shifted")
        exp_ready = sem("exp_ready")
        picked = sem("picked")
        exp2_ready = sem("exp2_ready")
        gu_ready = sem("gu_ready")
        silu_ready = sem("silu_ready")
        hid_ready = sem("hid_ready")
        down_ready = sem("down_ready")
        down_used = sem("down_used")
        ps = core.ps
        block = ctx.enter_context(nc.Block())

        @block.gpsimd
        def _(pool):
            pool.sem_inc(routed, 1)
            with pool.Fori(0, SEQS) as b:
                pool.wait_ge(routed, b + 1)
                pool.tensor_copy(xs[:], core.xnT[:, b, :]).then_inc(xs_ready, 1)

        @block.tensor
        def _(pe):
            pe.wait_ge(w.loaded, 16 * w.n)
            with pe.Fori(0, SEQS) as b:
                pe.wait_ge(xs_ready, b + 1)
                pe.wait_ge(down_used, b * E + 2)
                for t in range(TILES):
                    last = pe.matmul(ps[:, 6, t * E:(t + 1) * E], xs[:, t * P:(t + 1) * P], w.router[:], start=True, stop=True)
                last.then_inc(routed, 1)

                def down(e):
                    n = b * E + e
                    pe.wait_ge(down_used, n + 1)
                    pe.wait_ge(hid_ready, n * CH + CH + 2)
                    for t in range(TILES):
                        for c in range(CH):
                            last = pe.matmul(ps[:, 4 + e % 2, t * P:(t + 1) * P], hid[:, e % 2, c, t * P:(t + 1) * P],
                                             w.down[:, e, c, :], start=(c == 0), stop=(c == CH - 1))
                    last.then_inc(down_ready, 1)

                for e in range(E):
                    for c in range(CH):
                        pe.wait_ge(hid_ready, (b * E + e) * CH + c + 1)
                        for g, m_ in enumerate((w.gating, w.up)):
                            last = pe.matmul(ps[:, 2 * g + c, :], m_[:, e, c * P:(c + 1) * P], core.xnT[:, b, :], start=True, stop=True)
                        last.then_inc(gu_ready, 1)
                    if e:
                        down(e - 1)
                down(E - 1)

        @block.scalar
        def _(act):
            act.sem_inc(hid_ready, 2)
            with act.Fori(0, SEQS) as b:
                act.wait_ge(shifted, b + 1)
                act.activation(pr[:], pr[:], ACT.Exp).then_inc(exp_ready, 1)
                act.wait_ge(picked, b + 1)
                act.activation(m[:, 4], m[:, 3], ACT.Exp).then_inc(exp2_ready, 1)
                for e in range(E):
                    for c in range(CH):
                        n = (b * E + e) * CH + c
                        act.wait_ge(gu_ready, n + 1)
                        act.wait_ge(hid_ready, n + 1)
                        act.activation(act_g[:, c], ps[:, c, :], ACT.Silu).then_inc(silu_ready, 1)

        @block.vector
        def _(dve):
            dve.sem_inc(down_used, 2)
            with dve.Fori(0, SEQS) as b:
                dve.wait_ge(routed, b + 2)
                logits = ps[:, 6, 0:TILES * E].rearrange("p (t e) -> p t e", e=E)
                dve.tensor_reduce(m[:, 0], logits, AX_X, ALU.max)
                dve.drain()
                dve.tensor_tensor(pr[:], logits, m[:, 0].unsqueeze(2).broadcast_to([P, TILES, E]), ALU.subtract).then_inc(shifted, 1)
                dve.wait_ge(exp_ready, b + 1)
                dve.tensor_reduce(m[:, 1], pr[:], AX_X, ALU.add)
                dve.drain()
                dve.reciprocal(m[:, 2], m[:, 1])
                dve.drain()
                dve.tensor_tensor(pr[:], pr[:], m[:, 2].unsqueeze(2).broadcast_to([P, TILES, E]), ALU.mult)
                dve.drain()
                for t in range(TILES):
                    dve.max(top[:, t], pr[:, t])
                dve.drain()
                for t in range(TILES):
                    dve.max_index(idx[:, t], top[:, t], pr[:, t])
                dve.tensor_tensor(m[:, 3], top[:, :, 1], top[:, :, 0], ALU.subtract).then_inc(picked, 1)
                dve.drain()
                dve.tensor_copy(idf[:], idx[:])
                dve.drain()
                for k in range(2):
                    dve.tensor_tensor(hot[:, k], core.t.count8[:], idf[:, :, k:k + 1].broadcast_to([P, TILES, E]), ALU.is_equal)
                dve.wait_ge(exp2_ready, b + 1)
                dve.tensor_scalar(m[:, 5], m[:, 4], 1.0, None, ALU.add)
                dve.drain()
                dve.reciprocal(m[:, 6], m[:, 5])
                dve.drain()
                dve.tensor_tensor(m[:, 7], m[:, 6], m[:, 4], ALU.mult)
                dve.drain()
                for k in range(2):
                    dve.tensor_tensor(hot[:, k], hot[:, k], m[:, 6 + k].unsqueeze(2).broadcast_to([P, TILES, E]), ALU.mult)
                dve.drain()
                dve.tensor_tensor(full[:], hot[:, 0], hot[:, 1], ALU.add)
                dve.drain()

                def weigh(e):
                    n = b * E + e
                    dve.wait_ge(down_ready, n + 1)
                    for t in range(TILES):
                        src, dst, wt = ps[:, 4 + e % 2, t * P:(t + 1) * P], acc[:, t], full[:, t, e:e + 1]
                        if e == 0:
                            last = dve.tensor_scalar(dst, src, wt, None, ALU.mult)
                        else:
                            last = dve.scalar_tensor_tensor(out=core.y[:, b, t, :] if e == E - 1 else dst, in0=src, scalar=wt,
                                                            in1=dst, op0=ALU.mult, op1=ALU.add)
                    last.then_inc(down_used, 1)
                    dve.drain()

                for e in range(E):
                    for c in range(CH):
                        dve.wait_ge(silu_ready, (b * E + e) * CH + c + 1)
                        dve.tensor_tensor(hid[:, e % 2, c], act_g[:, c], ps[:, 2 + c, :], ALU.mult).then_inc(hid_ready, 1)
                    if e:
                        weigh(e - 1)
                weigh(E - 1)


def causal_attention(core, w):
    nc = core.nc
    HEADS, HD = 16, 8
    VW = HD + 1
    PAIRS = HEADS // 2
    STEPS = 5 * PAIRS
    RING, AHEAD = 4, 2
    SEGS = [[(0, 3, 0)], [(0, 2, 0), (0, 0, 384)], [(1, 3, 0)], [(1, 2, 0), (1, 0, 384)], [(0, 1, 0), (1, 1, 256)]]
    DIAG = [(384, 1, 0), (256, 2, P), (384, 1, 0), (256, 2, P), (P, 2, 256)]
    with ExitStack() as ctx:
        def sb(n, shape, dt=F32):
            return ctx.enter_context(nc.sbuf_tensor(f"ca_{n}", shape, dt))

        def sem(n):
            return core.sem(f"ca_{n}")

        xs = sb("xs", [P, TOK])
        wT = sb("wT", [P, 4, P])
        qT = sb("qT", [P, TOK])
        kT = sb("kT", [P, TOK])
        vals = sb("vals", [P, TILES, HEADS, VW])
        qz = sb("qz", [P, 4, TOK])
        top = sb("top", [P, RING, 2])
        pr = sb("pr", [P, RING, TOK])
        prT = sb("prT", [P, 2, TOK])
        rden = sb("rden", [P, 2, 2])
        att = sb("att", [P, TILES, HEADS * HD])
        attT = sb("attT", [P, TOK])
        w_turned = sem("w_turned")
        wT_ready = sem("wT_ready")
        ones_set = sem("ones_set")
        xs_ready = sem("xs_ready")
        qkv_ready = sem("qkv_ready")
        qT_ready = sem("qT_ready")
        kv_ready = sem("kv_ready")
        qz_ready = sem("qz_ready")
        scores_ready = sem("scores_ready")
        maxed = sem("maxed")
        exp_ready = sem("exp_ready")
        turned = sem("turned")
        prT_ready = sem("prT_ready")
        out_ready = sem("out_ready")
        out_used = sem("out_used")
        attT_turned = sem("attT_turned")
        attT_ready = sem("attT_ready")
        proj_ready = sem("proj_ready")
        y_ready = sem("y_ready")
        ps = core.ps
        block = ctx.enter_context(nc.Block())

        @block.gpsimd
        def _(pool):
            pool.memset(vals[:], 1.0).then_inc(ones_set, 1)
            pool.sem_inc(qkv_ready, 1)
            with pool.Fori(0, SEQS) as b:
                pool.wait_ge(qkv_ready, b + 1)
                pool.tensor_copy(xs[:], core.xnT[:, b, :]).then_inc(xs_ready, 1)
                pool.wait_ge(qT_ready, b + 1)
                for h in range(HEADS):
                    if h % 2 == 0 and h >= 4:
                        pool.wait_ge(scores_ready, b * STEPS + 5 * (h // 2 - 1))
                    pool.tensor_tensor(qz[:, h % 4], qT[:], core.t.head8[:, h, :].broadcast_to([P, TOK]), ALU.mult).then_inc(qz_ready, 1)

        @block.tensor
        def _(pe):
            pe.wait_ge(w.loaded, 16 * w.n)
            for n in range(4):
                last = pe.transpose(ps[:, 0, n * P:(n + 1) * P], w.w_qkv[:, n, :] if n < 3 else w.w_out[:], core.ident[:])
            last.then_inc(w_turned, 1)
            pe.wait_ge(wT_ready, 1)
            with pe.Fori(0, SEQS) as b:
                pe.wait_ge(y_ready, b + 1)
                for n in range(2):
                    pe.matmul(ps[:, n, :], wT[:, n, :], core.xnT[:, b, :], start=True, stop=True)
                pe.wait_ge(xs_ready, b + 1)
                for t in range(TILES):
                    last = pe.matmul(ps[:, 2, t * P:(t + 1) * P], xs[:, t * P:(t + 1) * P], wT[:, 2, :], start=True, stop=True)
                last.then_inc(qkv_ready, 1)
                pe.wait_ge(kv_ready, b + 1)
                base = b * STEPS

                def score(i):
                    pair, c = i // 5, i % RING
                    pe.wait_ge(qz_ready, b * HEADS + 2 * pair + (1 if i % 5 < 2 else 2))
                    pe.wait_ge(exp_ready, base + i + 1)
                    for h, t, col in SEGS[i % 5]:
                        last = pe.matmul(ps[:, c, col:col + (t + 1) * P], qz[:, 2 * (pair % 2) + h, t * P:(t + 1) * P],
                                         kT[:, 0:(t + 1) * P], start=True, stop=True)
                    last.then_inc(scores_ready, 1)

                def turn(i):
                    pe.wait_ge(exp_ready, base + i + 1 + RING)
                    pe.wait_ge(prT_ready, base + i + 1)
                    for k in range(TILES):
                        last = pe.transpose(ps[:, 4 + i % 2, k * P:(k + 1) * P], pr[:, i % RING, k * P:(k + 1) * P], core.ident[:])
                    last.then_inc(turned, 1)

                def values(i):
                    pe.wait_ge(prT_ready, base + i + 3)
                    pe.wait_ge(out_used, base + i + 1)
                    for s, (h, t, col) in enumerate(SEGS[i % 5]):
                        for k in range(t + 1):
                            last = pe.matmul(ps[:, 6 + i % 2, s * VW:(s + 1) * VW], prT[:, i % 2, col + k * P:col + (k + 1) * P],
                                             vals[:, k, 2 * (i // 5) + h, :], start=(k == 0), stop=(k == t))
                    last.then_inc(out_ready, 1)

                for i in range(AHEAD):
                    score(i)
                for i in range(STEPS):
                    if i + AHEAD < STEPS:
                        score(i + AHEAD)
                    turn(i)
                    if i:
                        values(i - 1)
                values(STEPS - 1)
                pe.wait_ge(out_used, (b + 1) * STEPS + 2)
                for t in range(TILES):
                    last = pe.transpose(ps[:, 4, t * P:(t + 1) * P], att[:, t], core.ident[:])
                last.then_inc(attT_turned, 1)
                pe.wait_ge(attT_ready, b + 1)
                for t in range(TILES):
                    last = pe.matmul(ps[:, 5, t * P:(t + 1) * P], attT[:, t * P:(t + 1) * P], wT[:, 3, :], start=True, stop=True)
                last.then_inc(proj_ready, 1)

        @block.scalar
        def _(act):
            act.wait_ge(w_turned, 1)
            act.copy(wT[:], ps[:, 0, :].rearrange("p (n c) -> p n c", n=4)).then_inc(wT_ready, 1)
            act.wait_ge(ones_set, 1)
            act.sem_inc(exp_ready, RING)
            act.sem_inc(prT_ready, 2)
            with act.Fori(0, SEQS) as b:
                base = b * STEPS

                def exponentials(i):
                    c = i % RING
                    act.wait_ge(maxed, base + i + 1)
                    for s, (h, t, col) in enumerate(SEGS[i % 5]):
                        last = act.activation(pr[:, c, col:col + (t + 1) * P], ps[:, c, col:col + (t + 1) * P], ACT.Exp,
                                              bias=top[:, c, s:s + 1])
                    last.then_inc(exp_ready, 1)

                act.wait_ge(qkv_ready, b + 2)
                act.activation(qT[:], ps[:, 0, :], ACT.Copy, scale=float(HD) ** -0.5).then_inc(qT_ready, 1)
                act.copy(kT[:], ps[:, 1, :])
                act.copy(vals[:, :, :, 0:HD].rearrange("p t h d -> p (t h) d"),
                         ps[:, 2, :].rearrange("p (t h d) -> p (t h) d", t=TILES, d=HD)).then_inc(kv_ready, 1)
                for i in range(AHEAD):
                    exponentials(i)
                for i in range(STEPS):
                    act.wait_ge(turned, base + i + 1)
                    act.copy(prT[:, i % 2], ps[:, 4 + i % 2, :]).then_inc(prT_ready, 1)
                    if i + AHEAD < STEPS:
                        exponentials(i + AHEAD)
                act.wait_ge(attT_turned, b + 1)
                act.copy(attT[:], ps[:, 4, :]).then_inc(attT_ready, 1)
                act.wait_ge(proj_ready, b + 1)
                act.copy(core.y[:, b], ps[:, 5, :].rearrange("p (t d) -> p t d", t=TILES)).then_inc(y_ready, 1)

        @block.vector
        def _(dve):
            dve.sem_inc(y_ready, 1)
            dve.sem_inc(out_used, 2)
            with dve.Fori(0, SEQS) as b:
                base = b * STEPS

                def maxima(i):
                    c = i % RING
                    d0, nd, step = DIAG[i % 5]
                    dve.wait_ge(scores_ready, base + i + 1)
                    if nd == 1:
                        blk, msk = ps[:, c, d0:d0 + P], core.t.lower_neg[:]
                    else:
                        blk = pair_of_blocks(ps, c, d0, step)
                        msk = core.t.lower_neg[:].unsqueeze(1).broadcast_to([P, 2, P])
                    dve.tensor_tensor(blk, blk, msk, ALU.add)
                    dve.drain()
                    for s, (h, t, col) in enumerate(SEGS[i % 5]):
                        last = dve.tensor_reduce(top[:, c, s:s + 1], ps[:, c, col:col + (t + 1) * P], AX_X, ALU.max, negate=True)
                    last.then_inc(maxed, 1)

                def weigh(i):
                    c = i % 2
                    segs = SEGS[i % 5]
                    o = ps[:, 6 + c, 0:len(segs) * VW].rearrange("p (s c) -> p s c", c=VW)
                    dve.wait_ge(out_ready, base + i + 1)
                    dve.reciprocal(rden[:, c, 0:len(segs)], o[:, :, HD])
                    dve.drain()
                    for s, (h, t, _) in enumerate(segs):
                        j = 2 * (i // 5) + h
                        last = dve.tensor_scalar(att[:, t, j * HD:(j + 1) * HD], o[:, s, 0:HD], rden[:, c, s:s + 1], None, ALU.mult)
                    last.then_inc(out_used, 1)

                for i in range(STEPS):
                    maxima(i)
                    if i > AHEAD:
                        weigh(i - AHEAD - 1)
                for i in range(STEPS - AHEAD - 1, STEPS):
                    weigh(i)


def local_transformer(core, w):
    nc = core.nc
    LAYERS, HEADS, HD, WIN = 6, 16, 64, 32
    PAIRS, INNER, KEYS = HEADS // 2, HEADS * HD, 2 * WIN
    HID, CH = 341, 3
    QK_SCALE = 8.0
    NORM_SCALE = 2.0 ** 18
    NORM_FLOOR = 1e-24
    with ExitStack() as ctx:
        def sb(n, shape, dt=F32):
            return ctx.enter_context(nc.sbuf_tensor(f"lt_{n}", shape, dt))

        def sem(n):
            return core.sem(f"lt_{n}")

        zs = sb("zs", [P, TILES, D])
        zn = sb("zn", [P, TILES, D])
        zb = sb("zb", [P, TILES, D])
        xsT = sb("xsT", [P, WIN + TOK])
        xn = sb("xn", [P, P])
        xf = sb("xf", [P, TOK])
        rope = sb("rope", [P, 4, TILES, HD])
        rot = sb("rot", [P, 2, INNER])
        sq = rot
        ss = sb("ss", [P, 2, HEADS])
        logs = sb("logs", [P, 2, HEADS])
        rr = sb("rr", [P, 2, HEADS])
        qa = core.xnT[:].rearrange("p b t -> p (b t)").rearrange("p (c n) -> p c n", c=2)
        qb = sb("qb", [P, 2, INNER])
        qT = sb("qT", [P, PAIRS, P])
        kT = sb("kT", [P, PAIRS, WIN + TOK])
        pr = sb("pr", [P, HEADS, KEYS])
        top = sb("top", [P, 3, HEADS])
        prT = sb("prT", [P, PAIRS, P])
        vals = sb("vals", [P, 4, PAIRS, HD])
        att = sb("att", [P, HEADS, HD])
        attT = sb("attT", [P, PAIRS, P])
        st = sb("st", [P, TILES, 6])
        mv = sb("mv", [P, TILES, 2])
        sd = sb("sd", [P, 3, TILES])
        nrm = sb("nrm", [P, TILES, D])
        fT = sb("fT", [P, TOK])
        gl = sb("gl", [P, 2, TOK])
        hid = sb("hid", [P, CH, TOK])
        cols = sb("cols", [P, 8, LAYERS, 1])
        names = """cols_turned cols_ready zeroed zs_ready zn_ready first_turned xn_low xn_high z_turned xs_low xs_high q_psum k_psum v_psum s_psum prT_turned
                   o_psum q_turned k_turned att_turned y_psum sq_ready rr_ready exp_ready v_ready prT_ready qT_ready
                   kT_ready attT_ready ss_ready qa_ready shifted att_ready z_ready rot_ready f_turned f_low f_high back_turned
                   var_ready rstd_ready nrm_ready fn_turned fT_ready gu_psum gelu_ready hid_ready down_psum seq_done
                   zb_ready""".split()
        S = namedtuple("Semaphores", names)(*[sem(n) for n in names])
        ps = core.ps
        flat = "p a b -> p (a b)"
        heads = "p (h c) -> p h c"
        by_parity = "p (a o) c -> p o a c"
        block = ctx.enter_context(nc.Block())

        Place = namedtuple("Place", "q layer seq buf pair")

        def each_sequence(eng, tiles, hand_over):
            def layer(pair, s, following):
                def place(b, l=pair * 2 + s):
                    return Place(l * SEQS + b, l, b, s, pair)

                with eng.Fori(0, SEQS - 1) as b:
                    tiles(place(b), place(b + 1))
                    hand_over(place(b), place(b + 1))
                tiles(place(SEQS - 1), following)
                hand_over(place(SEQS - 1), following)

            def first_of(pair, s):
                return Place((pair * 2 + s) * SEQS, pair * 2 + s, 0, s, pair)

            with eng.Fori(0, LAYERS // 2 - 1) as pair:
                layer(pair, 0, first_of(pair, 1))
                layer(pair, 1, first_of(pair + 1, 0))
            layer(LAYERS // 2 - 1, 0, first_of(LAYERS // 2 - 1, 1))
            layer(LAYERS // 2 - 1, 1, None)

        FIRST = Place(0, 0, 0, 0, 0)

        def weights_here(eng, at):
            eng.wait_ge(w.layer_loaded[at.buf], (at.pair + 1) * 16 * w.n_layer)

        @block.sync
        def _(sync):
            with sync.Fori(0, LAYERS // 2 - 1) as lp:
                for s in range(2):
                    sync.wait_ge(S.seq_done, (lp * 2 + s + 1) * SEQS + 1)
                    for dst, src in w.layer_loads(s, lp * 2 + 2 + s):
                        sync.dma_start(dst, src).then_inc(w.layer_loaded[s], 16)

        @block.gpsimd
        def _(pool):
            def rotate(n):
                for c in range(2):
                    pool.wait_ge(S.qa_ready, n * 2 + c + 1)
                    pool.tensor_tensor(qb[:, c], qa[:, c], qb[:, c], ALU.add)
                    pool.drain()
                    pool.wait_ge(S.rr_ready, n * 2 + c + 1)
                    pool.tensor_tensor(rot[:, c].rearrange(heads, c=HD), qb[:, c].rearrange(heads, c=HD),
                                       rr[:, c].unsqueeze(2).broadcast_to([P, HEADS, HD]), ALU.mult).then_inc(S.rot_ready, 1)

            def tiles(at, nxt):
                for t in range(1, TILES):
                    if t < TILES - 1 or nxt:
                        rotate(at.q * TILES + t + 1)
                    if t == 1 and nxt:
                        pool.drain()
                        pool.tensor_copy(zn[:], core.y[:, nxt.seq]).then_inc(S.zn_ready, 1)

            def hand_over(at, nxt):
                pool.wait_ge(S.f_turned, at.q + 1)
                pool.tensor_tensor(zb[:], zs[:], w.bufs[at.buf].b2[:].unsqueeze(1).broadcast_to([P, TILES, D]),
                                   ALU.add).then_inc(S.zb_ready, 1)
                if nxt:
                    pool.drain()
                    pool.tensor_copy(zs[:], zn[:]).then_inc(S.zs_ready, 1)
                    rotate(nxt.q * TILES + 1)

            pool.sem_inc(S.seq_done, 1)
            pool.memset(xsT[:, 0:WIN + 1], 0.0)
            pool.memset(xn[:, 0:1], 0.0)
            pool.memset(xf[:, 0:1], 0.0)
            pool.memset(kT[:, :, 0:WIN], 0.0).then_inc(S.zeroed, 1)
            pool.tensor_copy(zn[:], core.y[:, 0]).then_inc(S.zn_ready, 1)
            pool.tensor_copy(zs[:], core.y[:, 0]).then_inc(S.zs_ready, 1)
            rotate(0)
            rotate(1)
            each_sequence(pool, tiles, hand_over)

        @block.tensor
        def _(pe):
            def project(at, x, c):
                for a in (2 * c, 2 * c + 1):
                    last = pe.matmul(ps[:, a, :], x,
                                     w.bufs[at.buf].qkv[:, a * BANK:(a + 1) * BANK], start=True, stop=True)
                last.then_inc((S.q_psum, S.k_psum)[c], 1)

            def tile(t):
                return xsT[:, WIN + t * P:WIN + (t + 1) * P]

            def turn(n, c, before_last=None):
                pe.wait_ge(S.rot_ready, n * 2 + c + 1)
                for p in range(PAIRS):
                    if before_last and p == PAIRS - 1:
                        before_last(n - 1)
                    last = pe.transpose(ps[:, 2 * c + p // 4, (p % 4) * P:(p % 4 + 1) * P], rot[:, c, p * P:(p + 1) * P], core.ident[:])
                last.then_inc((S.q_turned, S.k_turned)[c], 1)

            def window_values(at, t, windows):
                n = at.q * TILES + t
                for v in windows:
                    if t == 0 and v == 0:
                        pe.wait_ge(S.seq_done, at.q + 1)
                    if t and v == 1:
                        pe.wait_ge(S.z_ready, n)
                    if v >= 2:
                        pe.wait_ge(S.v_ready, n * 4 + v - 1)
                    k0 = t * P + v * WIN
                    for odd in range(2):
                        last = pe.matmul(ps[64 * odd:64 * odd + 64, 7 - v % 2, :], xsT[:, k0:k0 + KEYS],
                                         w.bufs[at.buf].qkv[:, 2 * INNER:].rearrange("p (a o c) -> p a o c", o=2, c=HD)[:, :, odd, :],
                                         start=True, stop=True)
                    last.then_inc(S.v_psum, 1)

            def scores(n, t):
                for h in range(HEADS):
                    r = slice(64 * (h % 2), 64 * (h % 2) + 64)
                    for v in range(4):
                        k0 = t * P + v * WIN
                        last = pe.matmul(ps[32 * v:32 * v + 32, 4 + h % 2, (h // 2) * KEYS:(h // 2 + 1) * KEYS],
                                         qT[r, h // 2, v * WIN:(v + 1) * WIN], kT[r, h // 2, k0:k0 + KEYS],
                                         start=True, stop=True)
                last.then_inc(S.s_psum, 1)

            def weigh_values(n):
                for h in range(HEADS):
                    r = slice(64 * (h % 2), 64 * (h % 2) + 64)
                    for v in range(4):
                        last = pe.matmul(ps[32 * v:32 * v + 32, 6 + h % 2, (h // 2) * HD:(h // 2 + 1) * HD],
                                         prT[r, h // 2, v * WIN:(v + 1) * WIN], vals[r, v, h // 2, :], start=True, stop=True)
                last.then_inc(S.o_psum, 1)

            def turn_output(n):
                pe.wait_ge(S.att_ready, n + 1)
                for p in range(PAIRS):
                    last = pe.transpose(ps[:, 6 + p // 4, (p % 4) * P:(p % 4 + 1) * P],
                                        att[:, 2 * p:2 * p + 2, :].rearrange("p h k -> p (h k)"), core.ident[:])
                last.then_inc(S.att_turned, 1)

            def project_out(at, n):
                pe.wait_ge(S.attT_ready, n + 1)
                for p in range(PAIRS):
                    last = pe.matmul(ps[:, 6, 0:D], attT[:, p], w.bufs[at.buf].wo[:, p, :], start=(p == 0), stop=(p == PAIRS - 1))
                last.then_inc(S.y_psum, 1)

            def ready_to_weigh(n):
                pe.wait_ge(S.prT_ready, n + 1)
                pe.wait_ge(S.v_ready, n * 4 + 4)

            def turn_next(nxt):
                pe.wait_ge(S.zn_ready, nxt.q + 1)
                for t in range(TILES):
                    last = pe.transpose(ps[:, 7, t * P:(t + 1) * P], zn[:, t], core.ident[:])
                last.then_inc(S.z_turned, 1)

            def project_second(nxt):
                n = nxt.q * TILES
                pe.wait_ge(S.xs_low, nxt.q + 1)
                pe.wait_ge(S.xs_high, nxt.q + 1)
                pe.wait_ge(S.qT_ready, n + 1)
                project(nxt, tile(1), 0)
                pe.wait_ge(S.kT_ready, n + 1)
                project(nxt, tile(1), 1)

            def tiles(at, nxt):
                for t in range(TILES):
                    n = at.q * TILES + t
                    more = t + 1 < TILES or nxt is not None
                    crossing = t + 1 == TILES and nxt is not None
                    if t:
                        pe.wait_ge(S.qT_ready, n + 1)
                        if crossing:
                            pe.transpose(ps[:, 0, 0:P], zn[:, 0], core.ident[:]).then_inc(S.first_turned, 1)
                        elif more:
                            project(at, tile(t + 1), 0)
                        turn_output(n - 1)
                        if crossing:
                            if nxt.buf != at.buf:
                                weights_here(pe, nxt)
                            pe.wait_ge(S.xn_low, nxt.q)
                            pe.wait_ge(S.xn_high, nxt.q)
                            project(nxt, xn[:], 0)
                        pe.wait_ge(S.kT_ready, n + 1)
                        if crossing:
                            project(nxt, xn[:], 1)
                        elif more:
                            project(at, tile(t + 1), 1)
                        else:
                            project_out(at, n - 1)
                    scores(n, t)
                    if t and more:
                        project_out(at, n - 1)
                    window_values(at, t, range(4))
                    pe.wait_ge(S.exp_ready, n + 1)
                    for p in range(PAIRS):
                        last = pe.transpose(ps[:, 4 + p // 4, (p % 4) * P:(p % 4 + 1) * P],
                                            pr[:, 2 * p:2 * p + 2, :].rearrange("p h k -> p (h k)"), core.ident[:])
                    last.then_inc(S.prT_turned, 1)
                    if more:
                        turn(n + 1, 0, before_last=ready_to_weigh)
                    else:
                        ready_to_weigh(n)
                        pe.transpose(ps[:, 0, 0:P], zs[:, 0], core.ident[:])
                    weigh_values(n)
                    if more:
                        turn(n + 1, 1)
                for t in range(TILES - 1):
                    pe.transpose(ps[:, 4, t * P:(t + 1) * P], zs[:, t], core.ident[:])
                turn_output(at.q * TILES + TILES - 1)
                project_out(at, at.q * TILES + TILES - 1)

            def hand_over(at, nxt):
                q, W = at.q, w.bufs[at.buf]
                if nxt:
                    turn_next(nxt)
                pe.wait_ge(S.z_ready, (q + 1) * TILES)
                pe.transpose(ps[:, 4, 3 * P:4 * P], zs[:, 3], core.ident[:]).then_inc(S.f_turned, 1)
                pe.wait_ge(S.f_low, q + 1)
                pe.wait_ge(S.f_high, q + 1)
                for t in range(TILES):
                    last = pe.transpose(ps[:, 5, t * P:(t + 1) * P], xf[:, t * P:(t + 1) * P], core.ident[:])
                last.then_inc(S.back_turned, 1)
                if nxt:
                    project_second(nxt)
                pe.wait_ge(S.nrm_ready, q + 1)
                for t in range(TILES):
                    last = pe.transpose(ps[:, 4, t * P:(t + 1) * P], nrm[:, t], core.ident[:])
                last.then_inc(S.fn_turned, 1)
                pe.wait_ge(S.fT_ready, q + 1)
                for c in range(CH):
                    if c == 2:
                        pe.wait_ge(S.hid_ready, q * CH + 1)
                    for g in range(2):
                        last = pe.matmul(ps[:, 4 + 2 * g + c % 2, :], W.w1[:, 1 - g, c * P:(c + 1) * P], fT[:], start=True, stop=True)
                    last.then_inc(S.gu_psum, 1)
                pe.wait_ge(S.hid_ready, (q + 1) * CH)
                for t in range(TILES):
                    for c in range(CH):
                        last = pe.matmul(ps[:, 7, t * P:(t + 1) * P], hid[:, c, t * P:(t + 1) * P], W.w2[:, c, :],
                                         start=(c == 0), stop=(c == CH - 1))
                last.then_inc(S.down_psum, 1)

            pe.wait_ge(w.loaded, 16 * w.n)
            for c in range(8):
                src = w.rows[0:LAYERS, c, :]
                last = pe.transpose(ps[:, 0, c * LAYERS:(c + 1) * LAYERS], src, core.ident[0:LAYERS, 0:LAYERS])
            last.then_inc(S.cols_turned, 1)
            pe.wait_ge(S.cols_ready, 1)
            pe.wait_ge(S.zeroed, 1)
            weights_here(pe, FIRST)
            turn_next(FIRST)
            pe.wait_ge(S.xs_low, 1)
            pe.wait_ge(S.xs_high, 1)
            for c in range(2):
                project(FIRST, tile(0), c)
            for c in range(2):
                turn(0, c)
            project_second(FIRST)
            each_sequence(pe, tiles, hand_over)

        @block.scalar
        def _(act):
            def squares(n, c):
                act.wait_ge((S.q_psum, S.k_psum)[c], n + 1)
                act.activation(sq[:, c], ps[:, 2 * c:2 * c + 2, :].rearrange(flat), ACT.Square).then_inc(S.sq_ready, 1)

            def inverse_norms(n, c):
                act.wait_ge(S.ss_ready, n * 2 + c + 1)
                inverse_sqrt(act, rr[:, c], ss[:, c], logs[:, c], scale=NORM_SCALE).then_inc(S.rr_ready, 1)

            def window_values(n, windows):
                for v in windows:
                    act.wait_ge(S.v_psum, n * 4 + v + 1)
                    act.copy(vals[:, v], ps[:, 7 - v % 2, :].rearrange("p (a c) -> p a c", c=HD)).then_inc(S.v_ready, 1)

            def take_q(n):
                act.wait_ge(S.q_turned, n + 1)
                act.copy(qT[:], ps[:, 0:2, :].rearrange("p a (b c) -> p (a b) c", c=P)).then_inc(S.qT_ready, 1)

            def take_k(n, t):
                act.wait_ge(S.k_turned, n + 1)
                act.copy(kT[:, :, WIN + t * P:WIN + (t + 1) * P],
                         ps[:, 2:4, :].rearrange("p a (b c) -> p (a b) c", c=P)).then_inc(S.kT_ready, 1)

            def take_output(n):
                act.wait_ge(S.att_turned, n + 1)
                act.copy(attT[:], ps[:, 6:8, :].rearrange("p a (b c) -> p (a b) c", c=P)).then_inc(S.attT_ready, 1)

            def take_next(nxt):
                act.wait_ge(S.z_turned, nxt.q + 1)
                act.copy(xsT[0:64, WIN:], ps[0:64, 7, :]).then_inc(S.xs_low, 1)

            def tiles(at, nxt):
                for t in range(TILES):
                    n = at.q * TILES + t
                    more = t + 1 < TILES or nxt is not None
                    if t + 1 == TILES and nxt:
                        act.wait_ge(S.first_turned, nxt.q)
                        act.copy(xn[0:64, :], ps[0:64, 0, 0:P]).then_inc(S.xn_low, 1)
                    if t:
                        if more:
                            squares(n + 1, 0)
                        take_output(n - 1)
                        if more:
                            squares(n + 1, 1)
                            inverse_norms(n + 1, 0)
                            inverse_norms(n + 1, 1)
                    window_values(n, (0, 1))
                    act.wait_ge(S.shifted, n + 1)
                    act.activation(pr[:], pr[:], ACT.Exp, scale=QK_SCALE).then_inc(S.exp_ready, 1)
                    window_values(n, (2, 3))
                    act.wait_ge(S.prT_turned, n + 1)
                    act.copy(prT[:], ps[:, 4:6, :].rearrange("p a (b c) -> p (a b) c", c=P)).then_inc(S.prT_ready, 1)
                    if more:
                        take_q(n + 1)
                        take_k(n + 1, (t + 1) % TILES)
                take_output(at.q * TILES + TILES - 1)

            def hand_over(at, nxt):
                q = at.q
                if nxt:
                    take_next(nxt)
                act.wait_ge(S.f_turned, q + 1)
                act.copy(xf[0:64, :], ps[0:64, 4, :]).then_inc(S.f_low, 1)
                act.wait_ge(S.var_ready, q + 1)
                inverse_sqrt(act, sd[:, 2], sd[:, 0], sd[:, 1]).then_inc(S.rstd_ready, 1)
                if nxt:
                    squares(nxt.q * TILES + 1, 0)
                act.wait_ge(S.fn_turned, q + 1)
                act.activation(fT[:], ps[:, 4, :], ACT.Identity, bias=cols[:, 7, at.layer, :], scale=cols[:, 6, at.layer, :]).then_inc(S.fT_ready, 1)
                if nxt:
                    inverse_norms(nxt.q * TILES + 1, 0)
                act.preload_act_table_set(GELU)
                for c in range(CH):
                    if c == 1 and nxt:
                        squares(nxt.q * TILES + 1, 1)
                    act.wait_ge(S.gu_psum, q * CH + c + 1)
                    if c == 2:
                        act.wait_ge(S.hid_ready, q * CH + 1)
                    act.activation(gl[:, c % 2], ps[:, 4 + c % 2, :], ACT.Gelu, bias=cols[:, 3 + c, at.layer, :]).then_inc(S.gelu_ready, 1)
                if nxt:
                    act.preload_act_table_set(LN_EXP)
                    inverse_norms(nxt.q * TILES + 1, 1)

            act.preload_act_table_set(LN_EXP)
            act.wait_ge(S.cols_turned, 1)
            act.copy(cols[:].rearrange("p c l a -> p (c l a)"), ps[:, 0, 0:8 * LAYERS]).then_inc(S.cols_ready, 1)
            take_next(FIRST)
            for c in range(2):
                squares(0, c)
                inverse_norms(0, c)
            take_q(0)
            take_k(0, 0)
            for c in range(2):
                squares(1, c)
                inverse_norms(1, c)
            each_sequence(act, tiles, hand_over)

        @block.vector
        def _(dve):
            def new_tables(at):
                weights_here(dve, at)
                for c in range(2):
                    gain = w.bufs[at.buf].gains[:, c, :]
                    dve.tensor_tensor(rope[:, 2 * c], core.t.rope64[:, 2 * c], gain.unsqueeze(1).broadcast_to([P, TILES, HD]), ALU.mult)
                    for half in range(2):
                        a, z = slice(32 * half, 32 * half + 32), slice(32 - 32 * half, 64 - 32 * half)
                        dve.tensor_tensor(rope[:, 2 * c + 1, :, a], core.t.rope64[:, 2 * c + 1, :, a],
                                          gain[:, z].unsqueeze(1).broadcast_to([P, TILES, 32]), ALU.mult)
                dve.drain()

            def sum_squares(n, c):
                dve.wait_ge(S.sq_ready, n * 2 + c + 1)
                dve.tensor_reduce(ss[:, c], sq[:, c].rearrange(heads, c=HD), AX_X, ALU.add)
                dve.drain()
                dve.tensor_scalar(ss[:, c], ss[:, c], NORM_FLOOR, None, ALU.max).then_inc(S.ss_ready, 1)

            def rotate(t, c):
                src = ps[:, 2 * c:2 * c + 2, :].rearrange("p a (h c) -> p (a h) c", c=HD)
                dve.tensor_tensor(qa[:, c].rearrange(heads, c=HD), src,
                                  rope[:, 2 * c, t].unsqueeze(1).broadcast_to([P, HEADS, HD]), ALU.mult)
                for half in range(2):
                    a, z = slice(32 * half, 32 * half + 32), slice(32 - 32 * half, 64 - 32 * half)
                    last = dve.tensor_tensor(qb[:, c].rearrange(heads, c=HD)[:, :, a], src[:, :, z],
                                             rope[:, 2 * c + 1, t, a].unsqueeze(1).broadcast_to([P, HEADS, 32]), ALU.mult)
                last.then_inc(S.qa_ready, 1)

            def take_next(nxt):
                dve.wait_ge(S.z_turned, nxt.q + 1)
                dve.tensor_copy(xsT[64:128, WIN + 1:], ps[64:128, 7, 0:TOK - 1]).then_inc(S.xs_high, 1)

            def add_output(n, t):
                dve.wait_ge(S.y_psum, n + 1)
                dve.tensor_tensor(zs[:, t], ps[:, 6, 0:D], zs[:, t], ALU.add).then_inc(S.z_ready, 1)

            def tiles(at, nxt):
                for t in range(TILES):
                    n = at.q * TILES + t
                    more = t > 0 and (t + 1 < TILES or nxt is not None)
                    if t + 1 == TILES and nxt:
                        dve.wait_ge(S.first_turned, nxt.q)
                        dve.tensor_copy(xn[64:128, 1:], ps[64:128, 0, 0:P - 1]).then_inc(S.xn_high, 1)
                        if nxt.buf != at.buf:
                            new_tables(nxt)
                    if more:
                        sum_squares(n + 1, 0)
                        rotate((t + 1) % TILES, 0)
                        sum_squares(n + 1, 1)
                    dve.wait_ge(S.s_psum, n + 1)
                    for odd in range(2):
                        dve.tensor_tensor(pr[:].rearrange(by_parity, o=2)[:, odd], ps[:, 4 + odd, :].rearrange(heads, c=KEYS),
                                          core.t.window[:, min(t, 1), :].unsqueeze(1).broadcast_to([P, PAIRS, KEYS]), ALU.add)
                    dve.drain()
                    dve.tensor_reduce(top[:, 0], pr[:], AX_X, ALU.max)
                    if t == 1:
                        dve.wait_ge(S.zs_ready, at.q + 1)
                    if t:
                        add_output(n - 1, t - 1)
                    dve.drain()
                    dve.tensor_tensor(pr[:], pr[:], top[:, 0].unsqueeze(2).broadcast_to([P, HEADS, KEYS]),
                                      ALU.subtract).then_inc(S.shifted, 1)
                    if more:
                        rotate((t + 1) % TILES, 1)
                    dve.wait_ge(S.exp_ready, n + 1)
                    dve.tensor_reduce(top[:, 1], pr[:], AX_X, ALU.add)
                    dve.drain()
                    dve.reciprocal(top[:, 2], top[:, 1])
                    dve.drain()
                    dve.wait_ge(S.o_psum, n + 1)
                    for odd in range(2):
                        last = dve.tensor_tensor(att[:].rearrange(by_parity, o=2)[:, odd], ps[:, 6 + odd, :].rearrange(heads, c=HD),
                                                 top[:, 2].rearrange("p (a o) -> p o a", o=2)[:, odd].unsqueeze(2)
                                                 .broadcast_to([P, PAIRS, HD]), ALU.mult)
                    last.then_inc(S.att_ready, 1)
                add_output(at.q * TILES + TILES - 1, TILES - 1)

            def hand_over(at, nxt):
                q = at.q
                dve.wait_ge(S.f_turned, q + 1)
                dve.tensor_copy(xf[64:128, 1:], ps[64:128, 4, 0:TOK - 1]).then_inc(S.f_high, 1)
                if nxt:
                    take_next(nxt)
                dve.wait_ge(S.back_turned, q + 1)
                for t in range(TILES):
                    dve.bn_stats(st[:, t], ps[:, 5, t * P:(t + 1) * P])
                dve.drain()
                for t in range(TILES):
                    dve.bn_aggr(mv[:, t], st[:, t])
                dve.drain()
                dve.tensor_scalar(sd[:, 0], mv[:, :, 1], LN_EPS, None, ALU.add).then_inc(S.var_ready, 1)
                dve.wait_ge(S.rstd_ready, q + 1)
                for t in range(TILES):
                    last = dve.tensor_scalar(nrm[:, t], ps[:, 5, t * P:(t + 1) * P], mv[:, t, 0:1], sd[:, 2, t:t + 1],
                                             ALU.subtract, ALU.mult)
                last.then_inc(S.nrm_ready, 1)
                if nxt:
                    sum_squares(nxt.q * TILES + 1, 0)
                    rotate(1, 0)
                for c in range(CH):
                    if c == 1 and nxt:
                        sum_squares(nxt.q * TILES + 1, 1)
                    dve.wait_ge(S.gelu_ready, q * CH + c + 1)
                    dve.scalar_tensor_tensor(out=hid[:, c], in0=ps[:, 6 + c % 2, :], scalar=cols[:, c, at.layer, :], in1=gl[:, c % 2],
                                             op0=ALU.add, op1=ALU.mult).then_inc(S.hid_ready, 1)
                if nxt:
                    rotate(1, 1)
                dve.wait_ge(S.down_psum, q + 1)
                dve.wait_ge(S.zb_ready, q + 1)
                dve.tensor_tensor(core.y[:, at.seq], ps[:, 7, :].rearrange("p (t d) -> p t d", t=TILES), zb[:], ALU.add).then_inc(S.seq_done, 1)

            dve.wait_ge(S.zeroed, 1)
            dve.wait_ge(S.cols_ready, 1)
            new_tables(FIRST)
            take_next(FIRST)
            for t in range(2):
                for c in range(2):
                    sum_squares(t, c)
                    rotate(t, c)
            each_sequence(dve, tiles, hand_over)


def weights_diff_attention(w, ins, sb):
    w.Wq, w.Wk, w.Wv, w.Wproj = (sb(n, [P, P]) for n in ("Wq", "Wk", "Wv", "Wproj"))
    w.lam = sb("lam", [P, 4, 4])
    parts = [(dst[:], ins[f"L0_attn_{n}"]) for n, dst in (("Wq", w.Wq), ("Wk", w.Wk), ("Wv", w.Wv), ("Wproj", w.Wproj))]
    for n, v in enumerate(("lambda_q1", "lambda_k1", "lambda_q2", "lambda_k2")):
        parts.append((w.lam[:, n, :], ins[f"L0_attn_{v}"].rearrange("(a n) -> a n", a=1).broadcast_to([P, 4])))
    return parts


def weights_gated_ffn(w, ins, sb):
    w.gate, w.up, w.down = (sb(n, [P, 3, P], I32) for n in ("gate", "up", "down"))
    return [(w.gate[:], ins["L0_ffn_w_gate"].rearrange("(c p) d -> p c d", p=P)),
            (w.up[:], ins["L0_ffn_w_up"].rearrange("(c p) d -> p c d", p=P)),
            (w.down[:], ins["L0_ffn_w_down"].rearrange("p (c h) -> p c h", h=P))]


def weights_band_attention(w, ins, sb):
    w.WQ, w.WK, w.WV = (sb(n, [P, P]) for n in ("WQ", "WK", "WV"))
    return [(w.WQ[:], ins["L1_attn_WQ"]), (w.WK[:], ins["L1_attn_WK"]), (w.WV[:], ins["L1_attn_WV"])]


def weights_shared_expert_ffn(w, ins, sb):
    w.W_shared, w.W_expert, w.bias = (sb(n, [P, P]) for n in ("W_shared", "W_expert", "bias"))
    w.W_gate = sb("W_gate", [P, 7])
    return [(w.W_shared[:], ins["L1_ffn_W_shared"]), (w.W_expert[:], ins["L1_ffn_W_expert"]),
            (w.W_gate[:], ins["L1_ffn_W_gate"]),
            (w.bias[:], ins["L1_ffn_bias"].rearrange("(a n) -> a n", a=1).broadcast_to([P, P]))]


def weights_linear_attention(w, ins, sb):
    w.w_qkv, w.w_gate, w.w_out = sb("w_qkv", [P, 3072]), sb("w_gate", [P, 1024]), sb("w_out", [P, 8, P])
    return [(w.w_qkv[:], ins["L2_attn_w_qkv"]), (w.w_gate[:], ins["L2_attn_w_gate"]),
            (w.w_out[:], ins["L2_attn_w_out"].rearrange("(c p) d -> p c d", p=P))]


def weights_expert_ffn(w, ins, sb):
    w.router, w.gating, w.up = sb("router", [P, 8]), sb("gating", [P, 8, 256]), sb("up", [P, 8, 256])
    w.down = sb("down", [P, 8, 2, P])
    return [(w.router[:], ins["L2_ffn_router_kernel_DE"]),
            (w.gating[:], ins["L2_ffn_kernel_gating_EDF"].rearrange("e d f -> d e f")),
            (w.up[:], ins["L2_ffn_kernel_up_EDF"].rearrange("e d f -> d e f")),
            (w.down[:].rearrange("p e c d -> p (e c) d"), ins["L2_ffn_kernel_down_EFD"].rearrange("e (c p) d -> p (e c) d", p=P))]


def weights_causal_attention(w, ins, sb):
    w.w_qkv, w.w_out = sb("w_qkv", [P, 3, P]), sb("w_out", [P, P])
    return [(w.w_qkv[:], ins["L3_attn_w_qkv"].rearrange("(c p) d -> p c d", p=P)), (w.w_out[:], ins["L3_attn_w_out"])]


def weights_local_transformer(w, ins, sb):
    HID, INNER = 341, 1024
    w.bufs = []
    for s in range(2):
        b = Shared()
        b.qkv, b.wo = sb(f"qkv{s}", [P, 3 * INNER]), sb(f"wo{s}", [P, 8, P])
        b.w1, b.w2 = sb(f"w1_{s}", [P, 2, 3 * P]), sb(f"w2_{s}", [P, 3, P])
        b.b2, b.gains = sb(f"b2_{s}", [P, D]), sb(f"gains{s}", [P, 2, 64])
        w.bufs.append(b)
    w.rows = sb("rows", [6, 8, P])
    get = {n: ins[f"L3_ffn_{n}"] for n in ("Wqkv", "Wo", "W1", "W2", "b1", "b2", "ln_g", "ln_b", "q_scale", "k_scale")}
    w.padded = [b.w1 for b in w.bufs] + [b.w2 for b in w.bufs] + [w.rows]

    def layer_loads(s, l):
        b = w.bufs[s]
        return [(b.qkv[:], get["Wqkv"][l]),
                (b.wo[:], get["Wo"][l].rearrange("(c p) d -> p c d", p=P)),
                (b.w1[:, :, 0:HID], get["W1"][l].rearrange("d (a h) -> d a h", a=2)),
                (b.w2[:, 0:2, :], get["W2"][l][0:2 * P].rearrange("(c p) d -> p c d", p=P)),
                (b.w2[0:HID - 2 * P, 2, :], get["W2"][l][2 * P:HID]),
                (b.b2[:], get["b2"][l].rearrange("(a n) -> a n", a=1).broadcast_to([P, D])),
                (b.gains[:, 0], get["q_scale"][l].rearrange("(a n) -> a n", a=1).broadcast_to([P, 64])),
                (b.gains[:, 1], get["k_scale"][l].rearrange("(a n) -> a n", a=1).broadcast_to([P, 64]))]

    w.layer_loads = layer_loads
    w.n_layer = len(layer_loads(0, 0))
    w.first_layers = [layer_loads(s, s) for s in range(2)]
    rows = w.rows[:].rearrange("l c p -> l (c p)")
    return [(rows[:, 0:HID], get["b1"][:, 0:HID]), (rows[:, 3 * P:3 * P + HID], get["b1"][:, HID:]),
            (w.rows[:, 6, :], get["ln_g"]), (w.rows[:, 7, :], get["ln_b"])]


SUBLAYERS = [diff_attention, gated_ffn, band_attention, shared_expert_ffn, linear_attention, expert_ffn, causal_attention, local_transformer]
WEIGHTS = [weights_diff_attention, weights_gated_ffn, weights_band_attention, weights_shared_expert_ffn, weights_linear_attention, weights_expert_ffn, weights_causal_attention, weights_local_transformer]
UNUSED = ("L1_ffn_cond", "L1_ffn_mask")
PHASES = (0, 1, 2, 3, 4, 5, 6, 7)


def tables():
    f = np.float32
    pos = np.arange(TOK)
    out = {"ident": np.eye(P, dtype=f)}
    inv = (1.0 / np.power(f(10000.0), np.arange(0, 8, 2, dtype=f) / f(8))).astype(f)
    ang = (pos.astype(f)[:, None] * inv[None, :]).astype(f)
    c, s = np.cos(ang), np.sin(ang)
    rope = np.stack([np.concatenate([c, c], 1), np.concatenate([s, -s], 1)])
    out["rope8"] = rope.reshape(2, TILES, P, 8).transpose(2, 0, 1, 3)
    out["head8"] = np.repeat(np.eye(16, dtype=f), 8, axis=0)[:, :, None]
    out["upper"] = np.triu(np.ones((P, P), f))
    i, j = pos[:, None], pos[None, :]
    width = 64
    band = ((i - j <= width // 2) & (j - i <= (width - 1) // 2)) / np.sqrt(f(D))
    out["band"] = band.reshape(TILES, P, TOK).transpose(1, 0, 2)
    out["count8"] = np.broadcast_to(np.arange(8, dtype=f), (P, TILES, 8))
    out["lower_neg"] = np.triu(np.full((P, P), -1e30, f), 1)
    half = np.arange(0, 64, 2, dtype=f)
    inv = (f(1.0) / np.power(f(10000.0), half / f(64))).astype(f)
    ang = (pos.astype(f)[:, None] * inv[None, :]).astype(f)
    power = (pos.astype(f) - TOK // 2) / f(16)
    scale = np.power(((half + f(0.4 * 64)) / f(1.4 * 64))[None, :], power[:, None]).astype(f)
    c, s = np.cos(ang), np.sin(ang)
    rows = [np.concatenate([g * c, g * c], 1) if not odd else np.concatenate([-g * s, g * s], 1)
            for g in (scale, f(1) / scale) for odd in (0, 1)]
    out["rope64"] = (np.stack(rows) * f(512)).reshape(4, TILES, P, 64).transpose(2, 0, 1, 3)
    i, j = (np.arange(P) % 32)[:, None], np.arange(64)[None, :]
    seen = (j >= i) & (j <= i + 32)
    first = seen & ((j >= 32) | (np.arange(P) >= 32)[:, None])
    out["window"] = np.where(np.stack([first, seen], 1), f(0), f(-1e30))
    return {k: np.ascontiguousarray(v.astype(f)) for k, v in out.items()}


def build(nc, ins, tabs, out, phases=tuple(range(8))):
    with ExitStack() as ctx:
        def sb(n, shape, dt=F32):
            return ctx.enter_context(nc.sbuf_tensor(n, shape, dt))

        def sem(n):
            return ctx.enter_context(nc.semaphore(n))

        core = Shared()
        core.nc = nc
        core.x = sb("x", [P, SEQS, TILES, D])
        core.y = sb("y", [P, SEQS, TILES, D])
        core.xnT = sb("xnT", [P, SEQS, TOK])
        core.bn = sb("bn", [P, ALL_TILES, 6])
        core.small = sb("small", [P, 8, ALL_TILES])
        core.ps = ctx.enter_context(nc.psum_tensor("ps", [P, 8, BANK], F32))
        used = []

        def sublayer_sem(n):
            used.append(nc.alloc_semaphore(name=n))
            return used[-1]

        core.sem = sublayer_sem
        core.norm = Shared()
        core.norm.turns = core.norm.calls = core.norm.adds = 0
        core.norm.var_ready, core.norm.rstd_ready, core.norm.xn_ready = sem("norm_var_ready"), sem("norm_rstd_ready"), sem("norm_xn_ready")
        core.norm.x_ready, core.norm.turned, core.norm.stored = sem("norm_x_ready"), sem("norm_turned"), sem("norm_stored")
        core.x_loaded = sem("x_loaded")
        core.tables_loaded = sem("tables_loaded")
        core.n_tables = len(tabs)
        tiles = []
        loads = []
        for n, a in tabs.items():
            dst = sb(f"t_{n}", list(a.shape))
            loads.append((dst[:], a, core.tables_loaded))
            tiles.append(dst)
        core.t = namedtuple("Tables", list(tabs))(*tiles)
        core.ident = core.t.ident
        weights = {}
        scopes = {}
        for group in ((6, 7), (4, 5), (0, 1, 2, 3)):
            scopes[group] = ctx.enter_context(ExitStack())
            for k in group:
                if k not in phases:
                    continue
                w = Shared()
                w.loaded = sem(f"weights{k}_loaded")
                if k == 7:
                    w.layer_loaded = [sem(f"layer_loaded{s}") for s in range(2)]
                w.parts = WEIGHTS[k](w, ins, lambda n, shape, dt=F32: scopes[group].enter_context(
                    nc.sbuf_tensor(f"w{k}_{n}", shape, dt)))
                w.n = len(w.parts)
                weights[k] = w
        padded = weights[7].padded if 7 in weights else []
        zeros_set = sem("zeros_set")

        with nc.Block() as block:
            @block.gpsimd
            def _(pool):
                for n, buf in enumerate(padded):
                    pool.memset(buf[:], 0.0).then_inc(zeros_set, 1)

            @block.sync
            def _(sync):
                sync.dma_start(core.x[:].rearrange("p b t d -> p (b t) d"),
                               ins["L0_attn_x"].rearrange("b (t p) d -> p (b t) d", p=P)).then_inc(core.x_loaded, 16)
                for dst, src, loaded in loads:
                    sync.dma_start(dst, src).then_inc(loaded, 16)
                for k in phases:
                    w = weights[k]
                    if k == 7:
                        sync.wait_ge(zeros_set, len(padded))
                        for s in range(2):
                            for dst, src in w.first_layers[s]:
                                sync.dma_start(dst, src).then_inc(w.layer_loaded[s], 16)
                    for dst, src in w.parts:
                        sync.dma_start(dst, src).then_inc(w.loaded, 16)

        for n, k in enumerate(phases):
            residual_and_norm(core, first=(n == 0))
            SUBLAYERS[k](core, weights[k])
            nc.clear_and_free_semaphores(used)
            used.clear()
            nc.all_engine_barrier()
            for group, scope in scopes.items():
                if k == max((p for p in phases if p in group), default=None):
                    scope.close()
        residual_and_norm(core, final=out)


def kernel(**inputs):
    import concourse.bacc as bacc
    from concourse.bass_utils import run_bass_kernel_spmd

    nc = bacc.Bacc("TRN2", target_bir_lowering=False, num_devices=1)
    arrays, ins, tabs = {}, {}, {}
    for name, a in inputs.items():
        if name in UNUSED:
            continue
        a = np.ascontiguousarray(a)
        arrays[f"in_{name}"] = a
        ins[name] = nc.dram_tensor(f"in_{name}", a.shape, mybir.dt.from_np(a.dtype), kind="ExternalInput").ap()
    for name, a in tables().items():
        arrays[f"table_{name}"] = a
        tabs[name] = nc.dram_tensor(f"table_{name}", a.shape, F32, kind="ExternalInput").ap()
    out = nc.dram_tensor("out_x", (SEQS, TOK, D), F32, kind="ExternalOutput").ap()
    build(nc, ins, tabs, out, PHASES)
    r = run_bass_kernel_spmd(nc, [arrays], core_ids=[0])
    return r.results[0]["out_x"]
```
